# Optimizing a Trainium2 kernel written in Bass

```python
import numpy as np
import jax
import jax.numpy as jnp

def _softmax(x, axis=-1):
    return jax.nn.softmax(x, axis=axis)

def _gelu(x):
    return jax.nn.gelu(x, approximate=True)

def _silu(x):
    return jax.nn.silu(x)

def _sigmoid(x):
    return jax.nn.sigmoid(x)

def _layernorm(x, axis=-1, eps=1e-05):
    m = jnp.mean(x, axis=axis, keepdims=True)
    v = jnp.var(x, axis=axis, keepdims=True)
    return (x - m) / jnp.sqrt(v + eps)

def _scatter_add(tgt, idx, src, axis=0):
    return tgt.at[idx].add(src)

def _segment_sum(src, seg, n):
    return jax.ops.segment_sum(src, seg, n)
kernel_name = 'mk_gps_d4_gnn_r8_b511d7'

def setup_inputs(seed: int=0):
    np.random.seed(seed)
    _w = jnp.asarray

    def _rec_inputs():
        import jax
        import jax.numpy as jnp
        _gk = jax.random.key(seed)
        x = -0.0005963 + 1.001 * jax.random.normal(jax.random.fold_in(_gk, 1), (512, 768), jnp.float32)
        _s = jax.random.randint(jax.random.fold_in(_gk, 2), (4096,), 0, 512, jnp.int32)
        _d = jax.random.randint(jax.random.fold_in(_gk, 3), (4096,), 0, 512, jnp.int32)
        _loop = jnp.arange(512, dtype=jnp.int32)
        src = jnp.concatenate([_s, _d, _loop])
        dst = jnp.concatenate([_d, _s, _loop])
        _o = jnp.argsort(dst, stable=True)
        src = src[_o]
        dst = dst[_o]
        edge_attr_256 = 0.000121155 + 1.00018 * jax.random.normal(jax.random.fold_in(_gk, 12), (8704, 256), jnp.float32)
        edge_type_3 = jax.random.randint(jax.random.fold_in(_gk, 14), (8704,), 0, 3, jnp.int32)
        edge_type_4 = jax.random.randint(jax.random.fold_in(_gk, 15), (8704,), 0, 4, jnp.int32)
        return (x, src, dst, edge_attr_256, edge_type_3, edge_type_4)
    x, src, dst, edge_attr_256, edge_type_3, edge_type_4 = _rec_inputs()

    def _L0_gnn_setup():
        import jax, jax.numpy as jnp
        import numpy as np
        N_NODES = 512
        N_EDGES = 16384
        D = 768
        DE = 256
        L = 3
        H = 8
        DH = D // H
        EPS = 1e-05

        def _layernorm(x, g, b):
            mu = jnp.mean(x, axis=-1, keepdims=True)
            var = jnp.var(x, axis=-1, keepdims=True)
            return (x - mu) * jax.lax.rsqrt(var + EPS) * g + b
        key = jax.random.key(seed)
        ks = jax.random.split(key, 20)
        s = 0.02
        inp = {'node_features': jax.random.normal(ks[0], (N_NODES, D), jnp.float32), 'edge_index': jax.random.randint(ks[1], (2, N_EDGES), 0, N_NODES, jnp.int64 if jax.config.x64_enabled else jnp.int32), 'edge_features': jax.random.normal(ks[2], (N_EDGES, DE), jnp.float32), 'Wn': jax.random.normal(ks[3], (D, D), jnp.float32) * s, 'bn': jnp.zeros((D,), jnp.float32), 'We': jax.random.normal(ks[4], (D, DE), jnp.float32) * s, 'be': jnp.zeros((D,), jnp.float32), 'W1': jax.random.normal(ks[5], (L, D, 2 * D), jnp.float32) * s, 'b1': jnp.zeros((L, D), jnp.float32), 'ln_g': jnp.ones((L, D), jnp.float32), 'ln_b': jnp.zeros((L, D), jnp.float32), 'W2': jax.random.normal(ks[6], (L, D, D), jnp.float32) * s, 'b2': jnp.zeros((L, D), jnp.float32), 'Wqkv': jax.random.normal(ks[7], (3 * D, D), jnp.float32) * s, 'bqkv': jnp.zeros((3 * D,), jnp.float32), 'Wo': jax.random.normal(ks[8], (D, D), jnp.float32) * s, 'bo': jnp.zeros((D,), jnp.float32)}
        return inp
    _L0_gnn_all = _L0_gnn_setup()
    _L0_gnn_in = {k: v for k, v in _L0_gnn_all.items() if k in ('Wn', 'bn', 'We', 'be', 'W1', 'b1', 'ln_g', 'ln_b', 'W2', 'b2', 'Wqkv', 'bqkv', 'Wo', 'bo')}
    del _L0_gnn_all

    def _L0_mix_setup():
        import jax, jax.numpy as jnp
        import numpy as np
        EMBED_DIM = 768
        NUM_HEADS = 8
        HEAD_DIM = EMBED_DIM // NUM_HEADS
        NUM_RF = 256
        B, N = (8, 512)
        key = jax.random.key(seed)
        ks = jax.random.split(key, 6)
        x = jax.random.normal(ks[0], (B, N, EMBED_DIM), dtype=jnp.float32)
        s_qkv = 1.0 / np.sqrt(EMBED_DIM)
        qkv_w = jax.random.uniform(ks[1], (3 * EMBED_DIM, EMBED_DIM), minval=-s_qkv, maxval=s_qkv)
        qkv_b = jax.random.uniform(ks[2], (3 * EMBED_DIM,), minval=-s_qkv, maxval=s_qkv)
        proj_w = jax.random.uniform(ks[3], (EMBED_DIM, EMBED_DIM), minval=-s_qkv, maxval=s_qkv)
        proj_b = jax.random.uniform(ks[4], (EMBED_DIM,), minval=-s_qkv, maxval=s_qkv)
        rf = jax.random.normal(ks[5], (NUM_RF, HEAD_DIM), dtype=jnp.float32)
        rf = rf / jnp.linalg.norm(rf, axis=1, keepdims=True)
        return {'x': x, 'qkv_w': qkv_w, 'qkv_b': qkv_b, 'proj_w': proj_w, 'proj_b': proj_b, 'rf': rf}
    _L0_mix_all = _L0_mix_setup()
    _L0_mix_in = {k: v for k, v in _L0_mix_all.items() if k in ('qkv_w', 'qkv_b', 'proj_w', 'proj_b', 'rf')}
    del _L0_mix_all

    def _L0_ffn_setup():
        import jax, jax.numpy as jnp
        import numpy as np
        B, S, D, F, E = (4, 256, 768, 384, 8)
        key = jax.random.key(seed)
        ks = jax.random.split(key, 5)
        return {'x': jax.random.normal(ks[0], (B, S, D), dtype=jnp.float32), 'Ws': jax.random.normal(ks[1], (D, E), dtype=jnp.float32) * 0.02, 'bs': jnp.zeros((E,), dtype=jnp.float32), 'W1': jax.random.normal(ks[2], (E, D, F), dtype=jnp.float32) * 0.02, 'b1': jnp.zeros((E, F), dtype=jnp.float32), 'W2': jax.random.normal(ks[3], (E, F, D), dtype=jnp.float32) * 0.02, 'b2': jnp.zeros((E, D), dtype=jnp.float32)}
    _L0_ffn_all = _L0_ffn_setup()
    _L0_ffn_in = {k: v for k, v in _L0_ffn_all.items() if k in ('Ws', 'bs', 'W1', 'b1', 'W2', 'b2')}
    del _L0_ffn_all

    def _L1_gnn_setup():
        import jax, jax.numpy as jnp
        import numpy as np
        NEG_SLOPE = 0.2
        EPS = 1e-16
        N_NODES = 4096
        N_EDGES = 20000
        DIM = 768
        HEADS1 = 4
        OUT1 = DIM // HEADS1
        HEADS2 = 1
        OUT2 = DIM
        N_REL = 3

        def rgat_conv(x, W, q, k, b, src, dst, etype, heads, out_ch, n_nodes):
            xr = jnp.einsum('nd,rdf->rnf', x, W)
            oi = xr[etype, dst]
            oj = xr[etype, src]
            qi = oi @ q
            kj = oj @ k
            alpha = jax.nn.leaky_relu(qi + kj, NEG_SLOPE)
            m = jax.ops.segment_max(alpha, dst, num_segments=n_nodes)
            e = jnp.exp(alpha - m[dst])
            z = jax.ops.segment_sum(e, dst, num_segments=n_nodes)
            a = e / (z[dst] + EPS)
            msg = (a[:, :, None] * oj.reshape(-1, heads, out_ch)).reshape(-1, heads * out_ch)
            out = jax.ops.segment_sum(msg, dst, num_segments=n_nodes)
            return out + b
        key = jax.random.key(seed)
        ks = jax.random.split(key, 12)
        s = 0.02
        return {'x': jax.random.normal(ks[0], (N_NODES, DIM), dtype=jnp.float32), 'edge_index': jax.random.randint(ks[1], (2, N_EDGES), 0, N_NODES, dtype=jnp.int64), 'edge_type': jax.random.randint(ks[2], (N_EDGES,), 0, N_REL, dtype=jnp.int64), 'W1': jax.random.normal(ks[3], (N_REL, DIM, HEADS1 * OUT1), dtype=jnp.float32) * s, 'q1': jax.random.normal(ks[4], (HEADS1 * OUT1, HEADS1), dtype=jnp.float32) * s, 'k1': jax.random.normal(ks[5], (HEADS1 * OUT1, HEADS1), dtype=jnp.float32) * s, 'b1': jnp.zeros((HEADS1 * OUT1,), dtype=jnp.float32), 'W2': jax.random.normal(ks[6], (N_REL, DIM, HEADS2 * OUT2), dtype=jnp.float32) * s, 'q2': jax.random.normal(ks[7], (HEADS2 * OUT2, HEADS2), dtype=jnp.float32) * s, 'k2': jax.random.normal(ks[8], (HEADS2 * OUT2, HEADS2), dtype=jnp.float32) * s, 'b2': jnp.zeros((HEADS2 * OUT2,), dtype=jnp.float32)}
    _L1_gnn_all = _L1_gnn_setup()
    _L1_gnn_in = {k: v for k, v in _L1_gnn_all.items() if k in ('W1', 'q1', 'k1', 'b1', 'W2', 'q2', 'k2', 'b2')}
    del _L1_gnn_all

    def _L1_mix_setup():
        import jax, jax.numpy as jnp
        import numpy as np
        import math
        B, N, C = (8, 512, 768)
        H = 12
        DH = C // H
        M = 256
        LN_EPS = 1e-05

        def _phi(t, random_features):
            norm_sq = 0.5 * jnp.sum(t * t, axis=-1, keepdims=True)
            proj = jnp.einsum('bhnd,md->bhnm', t, random_features)
            return jnp.exp(proj - norm_sq) * (1.0 / math.sqrt(M))
        key = jax.random.key(seed)
        ks = jax.random.split(key, 7)
        x = jax.random.normal(ks[0], (B, N, C), dtype=jnp.float32)
        W_qkv = jax.random.normal(ks[1], (C, 3 * C), dtype=jnp.float32) * (1.0 / math.sqrt(C))
        W_proj = jax.random.normal(ks[2], (C, C), dtype=jnp.float32) * (1.0 / math.sqrt(C))
        b_proj = jnp.zeros((C,), dtype=jnp.float32)
        gamma = jnp.ones((C,), dtype=jnp.float32)
        beta = jnp.zeros((C,), dtype=jnp.float32)
        random_features = jax.random.normal(ks[3], (M, DH), dtype=jnp.float32) / math.sqrt(DH)
        return {'x': x, 'W_qkv': W_qkv, 'W_proj': W_proj, 'b_proj': b_proj, 'gamma': gamma, 'beta': beta, 'random_features': random_features}
    _L1_mix_all = _L1_mix_setup()
    _L1_mix_in = {k: v for k, v in _L1_mix_all.items() if k in ('W_qkv', 'W_proj', 'b_proj', 'gamma', 'beta', 'random_features')}
    del _L1_mix_all

    def _L1_ffn_setup():
        import jax, jax.numpy as jnp
        import numpy as np
        B, S, D_IN, D_HID, D_OUT = (32, 512, 768, 384, 768)
        key = jax.random.key(seed)
        k1, k2, k3, k4 = jax.random.split(key, 4)
        init_k = float(np.sqrt(1.0 / D_IN))
        init_k2 = float(np.sqrt(1.0 / D_HID))
        x = jax.random.normal(k1, (B, S, D_IN), dtype=jnp.float32)
        in_weight = jax.random.uniform(k2, (D_HID, D_IN), dtype=jnp.float32, minval=-init_k, maxval=init_k)
        in_bias = jax.random.uniform(k3, (D_HID,), dtype=jnp.float32, minval=-init_k, maxval=init_k)
        out_weight = jax.random.uniform(k4, (D_HID, D_OUT), dtype=jnp.float32, minval=-init_k2, maxval=init_k2)
        return {'x': x, 'in_weight': in_weight, 'in_bias': in_bias, 'out_weight': out_weight}
    _L1_ffn_all = _L1_ffn_setup()
    _L1_ffn_in = {k: v for k, v in _L1_ffn_all.items() if k in ('in_weight', 'in_bias', 'out_weight')}
    del _L1_ffn_all

    def _L2_gnn_setup():
        import jax, jax.numpy as jnp
        import numpy as np
        N_NODES = 2500
        N_EDGES = 12500
        D = 768
        NUM_REL = 4

        def _rgcn_conv(x, weight, root, bias, src, dst, etype):
            n = x.shape[0]
            out = x @ root + bias
            for r in range(NUM_REL):
                sel = etype == r
                self_f = sel.astype(x.dtype)
                deg = jnp.zeros((n,), x.dtype).at[dst].add(self_f)
                norm = jnp.where(sel, 1.0 / jnp.maximum(deg[dst], 1.0), 0.0)
                h_r = x @ weight[r]
                msgs = h_r[src] * norm[:, None]
                out = out + jax.ops.segment_sum(msgs, dst, num_segments=n)
            return out
        key = jax.random.key(seed)
        ks = jax.random.split(key, 12)
        entity = jax.random.normal(ks[0], (N_NODES, D), dtype=jnp.float32)
        edge_index = jax.random.randint(ks[1], (2, N_EDGES), 0, N_NODES, dtype=jnp.int64)
        edge_type = jax.random.randint(ks[2], (N_EDGES,), 0, NUM_REL, dtype=jnp.int64)
        s = 0.02
        params = {}
        for i, layer in enumerate(['1', '2', '3']):
            params[f'W{layer}'] = jax.random.normal(ks[3 + 3 * i], (NUM_REL, D, D), dtype=jnp.float32) * s
            params[f'root{layer}'] = jax.random.normal(ks[4 + 3 * i], (D, D), dtype=jnp.float32) * s
            params[f'b{layer}'] = jnp.zeros((D,), dtype=jnp.float32)
        return {'entity': entity, 'edge_index': edge_index, 'edge_type': edge_type, **params}
    _L2_gnn_all = _L2_gnn_setup()
    _L2_gnn_in = {k: v for k, v in _L2_gnn_all.items() if k in ('W1', 'root1', 'b1', 'W2', 'root2', 'b2', 'W3', 'root3', 'b3')}
    del _L2_gnn_all

    def _L2_mix_setup():
        import jax, jax.numpy as jnp
        import numpy as np
        NUM_HEADS = 12

        def _reference_tuple_inner(x, w_qkv, w_proj, b_proj):
            B, S, E = x.shape
            H = NUM_HEADS
            D = E // H
            qkv = (x @ w_qkv).reshape(B, S, 3, H, D).transpose(2, 0, 3, 1, 4)
            q, k, v = (qkv[0], qkv[1], qkv[2])
            q = jax.nn.elu(q) + 1.0
            k = jax.nn.elu(k) + 1.0
            kv = jnp.einsum('bhsd,bhse->bhde', k, v)
            k_sum = jnp.sum(k, axis=-2)
            z = 1.0 / jnp.einsum('bhsd,bhd->bhs', q, k_sum)
            out = jnp.einsum('bhsd,bhde->bhse', q, kv) * z[..., None]
            out = out.transpose(0, 2, 1, 3).reshape(B, S, E)
            out = out @ w_proj + b_proj
            return (out, kv)
        key = jax.random.key(seed)
        k1, k2, k3 = jax.random.split(key, 3)
        B, S, E = (8, 512, 768)
        x = jax.random.normal(k1, (B, S, E), dtype=jnp.float32)
        w_qkv = jax.random.normal(k2, (E, 3 * E), dtype=jnp.float32) * 0.02
        w_proj = jax.random.normal(k3, (E, E), dtype=jnp.float32) * 0.02
        b_proj = jnp.zeros((E,), dtype=jnp.float32)
        return {'x': x, 'w_qkv': w_qkv, 'w_proj': w_proj, 'b_proj': b_proj}
    _L2_mix_all = _L2_mix_setup()
    _L2_mix_in = {k: v for k, v in _L2_mix_all.items() if k in ('w_qkv', 'w_proj', 'b_proj')}
    del _L2_mix_all

    def _L2_ffn_setup():
        import jax, jax.numpy as jnp
        import numpy as np
        B, S, D, F, E = (2, 1024, 768, 384, 8)
        key = jax.random.key(seed)
        k0, k1, k2, k3, k4, k5 = jax.random.split(key, 6)
        scale = 0.02
        return {'hidden_states': jax.random.normal(k0, (B, S, D), dtype=jnp.float32), 'Wg': jax.random.normal(k1, (D, E), dtype=jnp.float32) * scale, 'W1': jax.random.normal(k2, (E, D, F), dtype=jnp.float32) * scale, 'b1': jnp.zeros((E, F), dtype=jnp.float32), 'W2': jax.random.normal(k3, (E, F, D), dtype=jnp.float32) * scale, 'b2': jnp.zeros((E, D), dtype=jnp.float32)}
    _L2_ffn_all = _L2_ffn_setup()
    _L2_ffn_in = {k: v for k, v in _L2_ffn_all.items() if k in ('Wg', 'W1', 'b1', 'W2', 'b2')}
    del _L2_ffn_all

    def _L3_gnn_setup():
        import jax, jax.numpy as jnp
        import numpy as np
        N = 6250
        E = 31250
        H = 12
        D = 64
        NEG_SLOPE = 0.2
        key = jax.random.key(seed)
        k1, k2, k3, k4, k5, k6, k7 = jax.random.split(key, 7)
        h = jax.random.normal(k1, (N, H * D), dtype=jnp.float32)
        src = jnp.concatenate([jnp.arange(N, dtype=jnp.int32), jax.random.randint(k2, (E - N,), 0, N, dtype=jnp.int32)])
        dst = jnp.concatenate([jnp.arange(N, dtype=jnp.int32), jax.random.randint(k3, (E - N,), 0, N, dtype=jnp.int32)])
        xav = 1.414 / np.sqrt(D)
        W_fc = jax.random.normal(k4, (D, D), dtype=jnp.float32) * xav
        attn_l = jax.random.normal(k5, (H, D), dtype=jnp.float32) * 0.15
        attn_r = jax.random.normal(k6, (H, D), dtype=jnp.float32) * 0.15
        W_res = jax.random.normal(k7, (D, D), dtype=jnp.float32) * xav
        return {'h': h, 'W_fc': W_fc, 'attn_l': attn_l, 'attn_r': attn_r, 'W_res': W_res, 'src': src, 'dst': dst}
    _L3_gnn_all = _L3_gnn_setup()
    _L3_gnn_in = {k: v for k, v in _L3_gnn_all.items() if k in ('W_fc', 'attn_l', 'attn_r', 'W_res')}
    del _L3_gnn_all

    def _L3_mix_setup():
        import jax, jax.numpy as jnp
        import numpy as np
        NUM_HEADS = 12

        def _l2_norm(t):
            return t / jnp.linalg.norm(t, axis=-2, keepdims=True)

        def _reference_tuple_inner(x, w_qkv, w_proj, b_proj):
            B, N, C = x.shape
            H = NUM_HEADS
            D = C // H
            qkv = (x @ w_qkv).reshape(B, N, 3, H, D).transpose(2, 0, 3, 1, 4)
            q, k, v = (qkv[0], qkv[1], qkv[2])
            q = _l2_norm(q)
            kT = _l2_norm(k).transpose(0, 1, 3, 2)
            sum_k = kT.sum(axis=-1)
            D_inv = 1.0 / (N + jnp.einsum('bhnd,bhd->bhd', q, sum_k))
            attn_matrix = jnp.einsum('bhnd,bhdn->bhdn', q, kT) * D_inv[..., None]
            matrix = jnp.einsum('bhnd,bhdn->bdhn', v, kT)
            y = jnp.einsum('bdhn,bhdn->bhnd', matrix, attn_matrix)
            y = y.transpose(0, 2, 1, 3).reshape(B, N, C)
            out = y @ w_proj + b_proj
            return (out, attn_matrix)
        key = jax.random.key(seed)
        k1, k2, k3 = jax.random.split(key, 3)
        B, N, C = (64, 1024, 768)
        x = jax.random.normal(k1, (B, N, C), dtype=jnp.float32)
        w_qkv = jax.random.normal(k2, (C, 3 * C), dtype=jnp.float32) * 0.02
        w_proj = jax.random.normal(k3, (C, C), dtype=jnp.float32) * 0.02
        b_proj = jnp.zeros((C,), dtype=jnp.float32)
        return {'x': x, 'w_qkv': w_qkv, 'w_proj': w_proj, 'b_proj': b_proj}
    _L3_mix_all = _L3_mix_setup()
    _L3_mix_in = {k: v for k, v in _L3_mix_all.items() if k in ('w_qkv', 'w_proj', 'b_proj')}
    del _L3_mix_all

    def _L3_ffn_setup():
        import math
        import jax, jax.numpy as jnp
        import numpy as np
        B, L, D = (8, 512, 768)
        E = 16
        TOP_K = 2
        F_EXP = 4 * D
        F_SH = F_EXP * 2 // 4
        key = jax.random.key(seed)
        ks = jax.random.split(key, 8)
        s = lambda fan_in: 1.0 / math.sqrt(fan_in)
        return {'hidden_states': jax.random.normal(ks[0], (B, L, D), jnp.float32), 'gate_weight': jax.random.uniform(ks[1], (E, D), jnp.float32, -s(D), s(D)), 'Wg': jax.random.uniform(ks[2], (E, F_EXP, D), jnp.float32, -s(D), s(D)), 'Wu': jax.random.uniform(ks[3], (E, F_EXP, D), jnp.float32, -s(D), s(D)), 'Wd': jax.random.uniform(ks[4], (E, D, F_EXP), jnp.float32, -s(F_EXP), s(F_EXP)), 'Ws_g': jax.random.uniform(ks[5], (F_SH, D), jnp.float32, -s(D), s(D)), 'Ws_u': jax.random.uniform(ks[6], (F_SH, D), jnp.float32, -s(D), s(D)), 'Ws_d': jax.random.uniform(ks[7], (D, F_SH), jnp.float32, -s(F_SH), s(F_SH))}
    _L3_ffn_all = _L3_ffn_setup()
    _L3_ffn_in = {k: v for k, v in _L3_ffn_all.items() if k in ('gate_weight', 'Wg', 'Wu', 'Wd', 'Ws_g', 'Ws_u', 'Ws_d')}
    del _L3_ffn_all
    return {'x': x, 'src': src, 'dst': dst, 'edge_attr_256': edge_attr_256, 'edge_type_3': edge_type_3, 'edge_type_4': edge_type_4, 'L0_gnn_Wn': _L0_gnn_in['Wn'], 'L0_gnn_bn': _L0_gnn_in['bn'], 'L0_gnn_We': _L0_gnn_in['We'], 'L0_gnn_be': _L0_gnn_in['be'], 'L0_gnn_W1': _L0_gnn_in['W1'], 'L0_gnn_b1': _L0_gnn_in['b1'], 'L0_gnn_ln_g': _L0_gnn_in['ln_g'], 'L0_gnn_ln_b': _L0_gnn_in['ln_b'], 'L0_gnn_W2': _L0_gnn_in['W2'], 'L0_gnn_b2': _L0_gnn_in['b2'], 'L0_gnn_Wqkv': _L0_gnn_in['Wqkv'], 'L0_gnn_bqkv': _L0_gnn_in['bqkv'], 'L0_gnn_Wo': _L0_gnn_in['Wo'], 'L0_gnn_bo': _L0_gnn_in['bo'], 'L0_mix_qkv_w': _L0_mix_in['qkv_w'], 'L0_mix_qkv_b': _L0_mix_in['qkv_b'], 'L0_mix_proj_w': _L0_mix_in['proj_w'], 'L0_mix_proj_b': _L0_mix_in['proj_b'], 'L0_mix_rf': _L0_mix_in['rf'], 'L0_ffn_Ws': _L0_ffn_in['Ws'], 'L0_ffn_bs': _L0_ffn_in['bs'], 'L0_ffn_W1': _L0_ffn_in['W1'], 'L0_ffn_b1': _L0_ffn_in['b1'], 'L0_ffn_W2': _L0_ffn_in['W2'], 'L0_ffn_b2': _L0_ffn_in['b2'], 'L1_gnn_W1': _L1_gnn_in['W1'], 'L1_gnn_q1': _L1_gnn_in['q1'], 'L1_gnn_k1': _L1_gnn_in['k1'], 'L1_gnn_b1': _L1_gnn_in['b1'], 'L1_gnn_W2': _L1_gnn_in['W2'], 'L1_gnn_q2': _L1_gnn_in['q2'], 'L1_gnn_k2': _L1_gnn_in['k2'], 'L1_gnn_b2': _L1_gnn_in['b2'], 'L1_mix_W_qkv': _L1_mix_in['W_qkv'], 'L1_mix_W_proj': _L1_mix_in['W_proj'], 'L1_mix_b_proj': _L1_mix_in['b_proj'], 'L1_mix_gamma': _L1_mix_in['gamma'], 'L1_mix_beta': _L1_mix_in['beta'], 'L1_mix_random_features': _L1_mix_in['random_features'], 'L1_ffn_in_weight': _L1_ffn_in['in_weight'], 'L1_ffn_in_bias': _L1_ffn_in['in_bias'], 'L1_ffn_out_weight': _L1_ffn_in['out_weight'], 'L2_gnn_W1': _L2_gnn_in['W1'], 'L2_gnn_root1': _L2_gnn_in['root1'], 'L2_gnn_b1': _L2_gnn_in['b1'], 'L2_gnn_W2': _L2_gnn_in['W2'], 'L2_gnn_root2': _L2_gnn_in['root2'], 'L2_gnn_b2': _L2_gnn_in['b2'], 'L2_gnn_W3': _L2_gnn_in['W3'], 'L2_gnn_root3': _L2_gnn_in['root3'], 'L2_gnn_b3': _L2_gnn_in['b3'], 'L2_mix_w_qkv': _L2_mix_in['w_qkv'], 'L2_mix_w_proj': _L2_mix_in['w_proj'], 'L2_mix_b_proj': _L2_mix_in['b_proj'], 'L2_ffn_Wg': _L2_ffn_in['Wg'], 'L2_ffn_W1': _L2_ffn_in['W1'], 'L2_ffn_b1': _L2_ffn_in['b1'], 'L2_ffn_W2': _L2_ffn_in['W2'], 'L2_ffn_b2': _L2_ffn_in['b2'], 'L3_gnn_W_fc': _L3_gnn_in['W_fc'], 'L3_gnn_attn_l': _L3_gnn_in['attn_l'], 'L3_gnn_attn_r': _L3_gnn_in['attn_r'], 'L3_gnn_W_res': _L3_gnn_in['W_res'], 'L3_mix_w_qkv': _L3_mix_in['w_qkv'], 'L3_mix_w_proj': _L3_mix_in['w_proj'], 'L3_mix_b_proj': _L3_mix_in['b_proj'], 'L3_ffn_gate_weight': _L3_ffn_in['gate_weight'], 'L3_ffn_Wg': _L3_ffn_in['Wg'], 'L3_ffn_Wu': _L3_ffn_in['Wu'], 'L3_ffn_Wd': _L3_ffn_in['Wd'], 'L3_ffn_Ws_g': _L3_ffn_in['Ws_g'], 'L3_ffn_Ws_u': _L3_ffn_in['Ws_u'], 'L3_ffn_Ws_d': _L3_ffn_in['Ws_d']}

def reference(x, src, dst, edge_attr_256, edge_type_3, edge_type_4, L0_gnn_Wn, L0_gnn_bn, L0_gnn_We, L0_gnn_be, L0_gnn_W1, L0_gnn_b1, L0_gnn_ln_g, L0_gnn_ln_b, L0_gnn_W2, L0_gnn_b2, L0_gnn_Wqkv, L0_gnn_bqkv, L0_gnn_Wo, L0_gnn_bo, L0_mix_qkv_w, L0_mix_qkv_b, L0_mix_proj_w, L0_mix_proj_b, L0_mix_rf, L0_ffn_Ws, L0_ffn_bs, L0_ffn_W1, L0_ffn_b1, L0_ffn_W2, L0_ffn_b2, L1_gnn_W1, L1_gnn_q1, L1_gnn_k1, L1_gnn_b1, L1_gnn_W2, L1_gnn_q2, L1_gnn_k2, L1_gnn_b2, L1_mix_W_qkv, L1_mix_W_proj, L1_mix_b_proj, L1_mix_gamma, L1_mix_beta, L1_mix_random_features, L1_ffn_in_weight, L1_ffn_in_bias, L1_ffn_out_weight, L2_gnn_W1, L2_gnn_root1, L2_gnn_b1, L2_gnn_W2, L2_gnn_root2, L2_gnn_b2, L2_gnn_W3, L2_gnn_root3, L2_gnn_b3, L2_mix_w_qkv, L2_mix_w_proj, L2_mix_b_proj, L2_ffn_Wg, L2_ffn_W1, L2_ffn_b1, L2_ffn_W2, L2_ffn_b2, L3_gnn_W_fc, L3_gnn_attn_l, L3_gnn_attn_r, L3_gnn_W_res, L3_mix_w_qkv, L3_mix_w_proj, L3_mix_b_proj, L3_ffn_gate_weight, L3_ffn_Wg, L3_ffn_Wu, L3_ffn_Wd, L3_ffn_Ws_g, L3_ffn_Ws_u, L3_ffn_Ws_d):
    import jax
    import jax.numpy as jnp

    def _L0_gnn_ref(node_features, edge_index, edge_features, Wn, bn, We, be, W1, b1, ln_g, ln_b, W2, b2, Wqkv, bqkv, Wo, bo):
        import jax, jax.numpy as jnp
        import numpy as np
        N_NODES = 512
        N_EDGES = 16384
        D = 768
        DE = 256
        L = 3
        H = 8
        DH = D // H
        EPS = 1e-05

        def _layernorm(x, g, b):
            mu = jnp.mean(x, axis=-1, keepdims=True)
            var = jnp.var(x, axis=-1, keepdims=True)
            return (x - mu) * jax.lax.rsqrt(var + EPS) * g + b
        n = node_features.shape[0]
        nodes = node_features @ Wn.T + bn
        edge_proj = edge_features @ We.T + be
        src, dst = (edge_index[0], edge_index[1])
        for l in range(L):
            msgs = nodes[src] + nodes[dst] + edge_proj
            agg = jax.ops.segment_sum(msgs, dst, num_segments=n)
            combined = jnp.concatenate([nodes, agg], axis=-1)
            h = combined @ W1[l].T + b1[l]
            h = _layernorm(h, ln_g[l], ln_b[l])
            h = jax.nn.relu(h)
            h = h @ W2[l].T + b2[l]
            nodes = h + nodes
        qkv = nodes @ Wqkv.T + bqkv
        q, k, v = jnp.split(qkv, 3, axis=-1)
        q = q.reshape(n, H, DH) * DH ** (-0.5)
        k = k.reshape(n, H, DH)
        v = v.reshape(n, H, DH)
        scores = jnp.einsum('nhd,mhd->hnm', q, k)
        probs = jax.nn.softmax(scores, axis=-1)
        attn = jnp.einsum('hnm,mhd->nhd', probs, v).reshape(n, D)
        attended = attn @ Wo.T + bo
        return nodes + attended

    def _L0_mix_ref(x, qkv_w, qkv_b, proj_w, proj_b, rf):
        import jax, jax.numpy as jnp
        import numpy as np
        EMBED_DIM = 768
        NUM_HEADS = 8
        HEAD_DIM = EMBED_DIM // NUM_HEADS
        NUM_RF = 256
        B, N = (8, 512)
        Bn, Nn, C = x.shape
        H, D = (NUM_HEADS, HEAD_DIM)
        qkv = x @ qkv_w.T + qkv_b
        qkv = qkv.reshape(Bn, Nn, 3, H, D).transpose(2, 0, 3, 1, 4)
        q, k, v = (qkv[0], qkv[1], qkv[2])
        scale = D ** (-0.5)
        q = q * scale
        k = k * scale
        q_norm = jnp.sum(q * q, axis=-1, keepdims=True) * 0.5
        k_norm = jnp.sum(k * k, axis=-1, keepdims=True) * 0.5
        phi_q = jnp.exp(jnp.einsum('bhnd,md->bhnm', q, rf) - q_norm)
        phi_k = jnp.exp(jnp.einsum('bhnd,md->bhnm', k, rf) - k_norm)
        kv = jnp.einsum('bhnm,bhnd->bhmd', phi_k, v)
        numerator = jnp.einsum('bhnm,bhmd->bhnd', phi_q, kv)
        k_sum = jnp.sum(phi_k, axis=2)
        denominator = jnp.einsum('bhnm,bhm->bhn', phi_q, k_sum)[..., None]
        attn = numerator / jnp.maximum(denominator, 1e-06)
        out = attn.transpose(0, 2, 1, 3).reshape(Bn, Nn, C)
        return out @ proj_w.T + proj_b

    def _L0_ffn_ref(x, Ws, bs, W1, b1, W2, b2):
        import jax, jax.numpy as jnp
        import numpy as np
        B, S, D, F, E = (4, 256, 768, 384, 8)
        b, s, d = x.shape
        xt = x.reshape(-1, d)
        logits = xt @ Ws + bs
        probs = jax.nn.softmax(logits, axis=-1)
        routes = jnp.argmax(probs, axis=-1)
        prob_max = jnp.max(probs, axis=-1)
        h = jax.nn.gelu(jnp.einsum('td,edf->etf', xt, W1) + b1[:, None, :], approximate=False)
        y = jnp.einsum('etf,efd->etd', h, W2) + b2[:, None, :]
        out = jnp.take_along_axis(y, routes[None, :, None], axis=0)[0]
        out = out * prob_max[:, None]
        return out.reshape(b, s, d)

    def _L1_gnn_ref(x, edge_index, edge_type, W1, q1, k1, b1, W2, q2, k2, b2):
        import jax, jax.numpy as jnp
        import numpy as np
        NEG_SLOPE = 0.2
        EPS = 1e-16
        N_NODES = 4096
        N_EDGES = 20000
        DIM = 768
        HEADS1 = 4
        OUT1 = DIM // HEADS1
        HEADS2 = 1
        OUT2 = DIM
        N_REL = 3

        def rgat_conv(x, W, q, k, b, src, dst, etype, heads, out_ch, n_nodes):
            xr = jnp.einsum('nd,rdf->rnf', x, W)
            oi = xr[etype, dst]
            oj = xr[etype, src]
            qi = oi @ q
            kj = oj @ k
            alpha = jax.nn.leaky_relu(qi + kj, NEG_SLOPE)
            m = jax.ops.segment_max(alpha, dst, num_segments=n_nodes)
            e = jnp.exp(alpha - m[dst])
            z = jax.ops.segment_sum(e, dst, num_segments=n_nodes)
            a = e / (z[dst] + EPS)
            msg = (a[:, :, None] * oj.reshape(-1, heads, out_ch)).reshape(-1, heads * out_ch)
            out = jax.ops.segment_sum(msg, dst, num_segments=n_nodes)
            return out + b
        src, dst = (edge_index[0], edge_index[1])
        n = x.shape[0]
        h = rgat_conv(x, W1, q1, k1, b1, src, dst, edge_type, HEADS1, OUT1, n)
        h = jax.nn.elu(h)
        out = rgat_conv(h, W2, q2, k2, b2, src, dst, edge_type, HEADS2, OUT2, n)
        return out

    def _L1_mix_ref(x, W_qkv, W_proj, b_proj, gamma, beta, random_features):
        import jax, jax.numpy as jnp
        import numpy as np
        import math
        B, N, C = (8, 512, 768)
        H = 12
        DH = C // H
        M = 256
        LN_EPS = 1e-05

        def _phi(t, random_features):
            norm_sq = 0.5 * jnp.sum(t * t, axis=-1, keepdims=True)
            proj = jnp.einsum('bhnd,md->bhnm', t, random_features)
            return jnp.exp(proj - norm_sq) * (1.0 / math.sqrt(M))
        b, n, c = x.shape
        qkv = (x @ W_qkv).reshape(b, n, 3, H, DH)
        qkv = jnp.transpose(qkv, (2, 0, 3, 1, 4))
        q, k, v = (qkv[0], qkv[1], qkv[2])
        q_p = _phi(q, random_features)
        k_p = _phi(k, random_features)
        kv = jnp.einsum('bhnm,bhnd->bhmd', k_p, v)
        out = jnp.einsum('bhnm,bhmd->bhnd', q_p, kv)
        k_sum = jnp.sum(k_p, axis=2)
        normalizer = jnp.einsum('bhnm,bhm->bhn', q_p, k_sum)[..., None]
        out = out / (normalizer + 1e-06)
        x_attn = jnp.transpose(out, (0, 2, 1, 3)).reshape(b, n, c)
        x_attn = x_attn @ W_proj + b_proj
        y = x + x_attn
        mu = jnp.mean(y, axis=-1, keepdims=True)
        var = jnp.mean(jnp.square(y - mu), axis=-1, keepdims=True)
        return (y - mu) * jax.lax.rsqrt(var + LN_EPS) * gamma + beta

    def _L1_ffn_ref(x, in_weight, in_bias, out_weight):
        import jax, jax.numpy as jnp
        import numpy as np
        B, S, D_IN, D_HID, D_OUT = (32, 512, 768, 384, 768)
        lead = x.shape[:-1]
        xt = x.reshape(-1, in_weight.shape[1])
        h = jax.nn.gelu(jnp.einsum('td,hd->th', xt, in_weight) + in_bias, approximate=False)
        out = jnp.einsum('th,ho->to', h, out_weight)
        return out.reshape(*lead, out_weight.shape[1])

    def _L2_gnn_ref(entity, edge_index, edge_type, W1, root1, b1, W2, root2, b2, W3, root3, b3):
        import jax, jax.numpy as jnp
        import numpy as np
        N_NODES = 2500
        N_EDGES = 12500
        D = 768
        NUM_REL = 4

        def _rgcn_conv(x, weight, root, bias, src, dst, etype):
            n = x.shape[0]
            out = x @ root + bias
            for r in range(NUM_REL):
                sel = etype == r
                self_f = sel.astype(x.dtype)
                deg = jnp.zeros((n,), x.dtype).at[dst].add(self_f)
                norm = jnp.where(sel, 1.0 / jnp.maximum(deg[dst], 1.0), 0.0)
                h_r = x @ weight[r]
                msgs = h_r[src] * norm[:, None]
                out = out + jax.ops.segment_sum(msgs, dst, num_segments=n)
            return out
        src, dst = (edge_index[0], edge_index[1])
        x = jax.nn.relu(_rgcn_conv(entity, W1, root1, b1, src, dst, edge_type))
        x = jax.nn.relu(_rgcn_conv(x, W2, root2, b2, src, dst, edge_type))
        x = _rgcn_conv(x, W3, root3, b3, src, dst, edge_type)
        return x

    def _L2_mix_ref(x, w_qkv, w_proj, b_proj):
        import jax, jax.numpy as jnp
        import numpy as np
        NUM_HEADS = 12

        def _reference_tuple_inner(x, w_qkv, w_proj, b_proj):
            B, S, E = x.shape
            H = NUM_HEADS
            D = E // H
            qkv = (x @ w_qkv).reshape(B, S, 3, H, D).transpose(2, 0, 3, 1, 4)
            q, k, v = (qkv[0], qkv[1], qkv[2])
            q = jax.nn.elu(q) + 1.0
            k = jax.nn.elu(k) + 1.0
            kv = jnp.einsum('bhsd,bhse->bhde', k, v)
            k_sum = jnp.sum(k, axis=-2)
            z = 1.0 / jnp.einsum('bhsd,bhd->bhs', q, k_sum)
            out = jnp.einsum('bhsd,bhde->bhse', q, kv) * z[..., None]
            out = out.transpose(0, 2, 1, 3).reshape(B, S, E)
            out = out @ w_proj + b_proj
            return (out, kv)
        return _reference_tuple_inner(x, w_qkv, w_proj, b_proj)[0]

    def _L2_ffn_ref(hidden_states, Wg, W1, b1, W2, b2):
        import jax, jax.numpy as jnp
        import numpy as np
        B, S, D, F, E = (2, 1024, 768, 384, 8)
        b, s, d = hidden_states.shape
        e = W1.shape[0]
        x = hidden_states.reshape(-1, d)
        logits = x @ Wg
        probs = jax.nn.softmax(logits, axis=-1)
        gate = jnp.max(probs, axis=-1)
        expert_idx = jnp.argmax(probs, axis=-1)
        h = jax.nn.silu(jnp.einsum('td,edf->etf', x, W1) + b1[:, None, :])
        y = jnp.einsum('etf,efd->etd', h, W2) + b2[:, None, :]
        combine = jax.nn.one_hot(expert_idx, e, dtype=x.dtype) * gate[:, None]
        out = jnp.einsum('te,etd->td', combine, y)
        return out.reshape(b, s, d)

    def _L3_gnn_ref(h, W_fc, attn_l, attn_r, W_res, src, dst):
        import jax, jax.numpy as jnp
        import numpy as np
        N = 6250
        E = 31250
        H = 12
        D = 64
        NEG_SLOPE = 0.2
        n = h.shape[0]
        hh = h.reshape(n, H, D)
        ft = jnp.einsum('nhd,ed->nhe', hh, W_fc)
        a1 = jnp.einsum('nhd,hd->nh', ft, attn_l)
        a2 = jnp.einsum('nhd,hd->nh', ft, attn_r)
        e = jax.nn.leaky_relu(a1[src] + a2[dst], negative_slope=NEG_SLOPE)
        m = jax.ops.segment_max(e, dst, num_segments=n)
        ee = jnp.exp(e - m[dst])
        denom = jax.ops.segment_sum(ee, dst, num_segments=n)
        alpha = ee / denom[dst]
        agg = jax.ops.segment_sum(alpha[:, :, None] * ft[src], dst, num_segments=n)
        res = jnp.einsum('nhd,ed->nhe', hh, W_res)
        return jax.nn.relu((res + agg).reshape(n, H * D))

    def _L3_mix_ref(x, w_qkv, w_proj, b_proj):
        import jax, jax.numpy as jnp
        import numpy as np
        NUM_HEADS = 12

        def _l2_norm(t):
            return t / jnp.linalg.norm(t, axis=-2, keepdims=True)

        def _reference_tuple_inner(x, w_qkv, w_proj, b_proj):
            B, N, C = x.shape
            H = NUM_HEADS
            D = C // H
            qkv = (x @ w_qkv).reshape(B, N, 3, H, D).transpose(2, 0, 3, 1, 4)
            q, k, v = (qkv[0], qkv[1], qkv[2])
            q = _l2_norm(q)
            kT = _l2_norm(k).transpose(0, 1, 3, 2)
            sum_k = kT.sum(axis=-1)
            D_inv = 1.0 / (N + jnp.einsum('bhnd,bhd->bhd', q, sum_k))
            attn_matrix = jnp.einsum('bhnd,bhdn->bhdn', q, kT) * D_inv[..., None]
            matrix = jnp.einsum('bhnd,bhdn->bdhn', v, kT)
            y = jnp.einsum('bdhn,bhdn->bhnd', matrix, attn_matrix)
            y = y.transpose(0, 2, 1, 3).reshape(B, N, C)
            out = y @ w_proj + b_proj
            return (out, attn_matrix)
        return _reference_tuple_inner(x, w_qkv, w_proj, b_proj)[0]

    def _L3_ffn_ref(hidden_states, gate_weight, Wg, Wu, Wd, Ws_g, Ws_u, Ws_d):
        import math
        import jax, jax.numpy as jnp
        import numpy as np
        B, L, D = (8, 512, 768)
        E = 16
        TOP_K = 2
        F_EXP = 4 * D
        F_SH = F_EXP * 2 // 4
        b, l, d = hidden_states.shape
        n = b * l
        x = hidden_states.reshape(n, d)
        scores = jax.nn.sigmoid(x @ gate_weight.T)
        capacity = math.ceil(n / E * TOP_K)
        topk_score, topk_ids = jax.lax.top_k(scores.T, capacity)
        xg = x[topk_ids]
        gate = jax.nn.silu(jnp.einsum('ecd,efd->ecf', xg, Wg))
        up = jnp.einsum('ecd,efd->ecf', xg, Wu)
        out = jnp.einsum('ecf,edf->ecd', gate * up, Wd)
        out = out * topk_score[..., None]
        y = jnp.zeros((n, d), x.dtype).at[topk_ids.reshape(-1)].add(out.reshape(-1, d))
        y = y.reshape(b, l, d)
        shared = jax.nn.silu(hidden_states @ Ws_g.T) * (hidden_states @ Ws_u.T) @ Ws_d.T
        return y + shared
    edge_index = jnp.stack([src, dst])
    xn = _layernorm(x, axis=-1)
    x = x + _L0_gnn_ref(xn, edge_index, edge_attr_256, L0_gnn_Wn, L0_gnn_bn, L0_gnn_We, L0_gnn_be, L0_gnn_W1, L0_gnn_b1, L0_gnn_ln_g, L0_gnn_ln_b, L0_gnn_W2, L0_gnn_b2, L0_gnn_Wqkv, L0_gnn_bqkv, L0_gnn_Wo, L0_gnn_bo) + _L0_mix_ref(xn[None], L0_mix_qkv_w, L0_mix_qkv_b, L0_mix_proj_w, L0_mix_proj_b, L0_mix_rf)[0]
    x = x + _L0_ffn_ref(_layernorm(x, axis=-1)[None], L0_ffn_Ws, L0_ffn_bs, L0_ffn_W1, L0_ffn_b1, L0_ffn_W2, L0_ffn_b2)[0]
    xn = _layernorm(x, axis=-1)
    x = x + _L1_gnn_ref(xn, edge_index, edge_type_3, L1_gnn_W1, L1_gnn_q1, L1_gnn_k1, L1_gnn_b1, L1_gnn_W2, L1_gnn_q2, L1_gnn_k2, L1_gnn_b2) + _L1_mix_ref(xn[None], L1_mix_W_qkv, L1_mix_W_proj, L1_mix_b_proj, L1_mix_gamma, L1_mix_beta, L1_mix_random_features)[0]
    x = x + _L1_ffn_ref(_layernorm(x, axis=-1)[None], L1_ffn_in_weight, L1_ffn_in_bias, L1_ffn_out_weight)[0]
    xn = _layernorm(x, axis=-1)
    x = x + _L2_gnn_ref(xn, edge_index, edge_type_4, L2_gnn_W1, L2_gnn_root1, L2_gnn_b1, L2_gnn_W2, L2_gnn_root2, L2_gnn_b2, L2_gnn_W3, L2_gnn_root3, L2_gnn_b3) + _L2_mix_ref(xn[None], L2_mix_w_qkv, L2_mix_w_proj, L2_mix_b_proj)[0]
    x = x + _L2_ffn_ref(_layernorm(x, axis=-1)[None], L2_ffn_Wg, L2_ffn_W1, L2_ffn_b1, L2_ffn_W2, L2_ffn_b2)[0]
    xn = _layernorm(x, axis=-1)
    x = x + _L3_gnn_ref(xn, L3_gnn_W_fc, L3_gnn_attn_l, L3_gnn_attn_r, L3_gnn_W_res, src, dst) + _L3_mix_ref(xn[None], L3_mix_w_qkv, L3_mix_w_proj, L3_mix_b_proj)[0]
    x = x + _L3_ffn_ref(_layernorm(x, axis=-1)[None], L3_ffn_gate_weight, L3_ffn_Wg, L3_ffn_Wu, L3_ffn_Wd, L3_ffn_Ws_g, L3_ffn_Ws_u, L3_ffn_Ws_d)[0]
    return x

_drawn_inputs = setup_inputs


def setup_inputs(seed=0):
    import zlib

    import numpy as np

    out = dict(_drawn_inputs(seed))
    spreads = {'L0_gnn_bn': (0.0, 0.1),
     'L0_gnn_be': (0.0, 0.1),
     'L0_gnn_b1': (0.0, 0.795),
     'L0_gnn_ln_g': (1.0, 0.2),
     'L0_gnn_ln_b': (0.0, 0.1),
     'L0_gnn_b2': (0.0, 0.1),
     'L0_gnn_bqkv': (0.0, 0.1),
     'L0_gnn_bo': (0.0, 0.1),
     'L0_ffn_bs': (0.0, 0.668),
     'L0_ffn_b1': (0.0, 0.8),
     'L0_ffn_b2': (0.0, 0.443),
     'L1_gnn_b1': (0.0, 0.566),
     'L1_gnn_b2': (0.0, 0.1),
     'L1_mix_b_proj': (0.0, 0.1),
     'L1_mix_gamma': (1.0, 0.2),
     'L1_mix_beta': (0.0, 0.1),
     'L2_gnn_b1': (0.0, 0.337),
     'L2_gnn_b2': (0.0, 0.1),
     'L2_gnn_b3': (0.0, 0.1),
     'L2_mix_b_proj': (0.0, 0.1),
     'L2_ffn_b1': (0.0, 0.8),
     'L2_ffn_b2': (0.0, 0.767),
     'L3_mix_b_proj': (0.0, 0.293)}
    factors = {'L0_mix_qkv_w': 4.531,
     'L0_mix_qkv_b': 5.476,
     'L0_mix_proj_w': 3.856,
     'L0_mix_proj_b': 3.28,
     'L0_mix_rf': 8.0,
     'L1_gnn_W1': 2.961,
     'L1_gnn_q1': 8.0,
     'L1_gnn_k1': 8.0,
     'L1_gnn_q2': 8.0,
     'L1_gnn_k2': 8.0,
     'L1_mix_W_qkv': 8.0,
     'L1_mix_W_proj': 8.0,
     'L1_mix_random_features': 8.0,
     'L1_ffn_in_bias': 8.0,
     'L2_ffn_Wg': 3.931,
     'L2_ffn_W1': 4.901,
     'L2_ffn_W2': 4.731,
     'L3_mix_w_qkv': 64.0,
     'L3_mix_w_proj': 64.0}
    for name, (base, spread) in spreads.items():
        noise = np.random.default_rng([zlib.crc32(name.encode()), seed]).standard_normal(out[name].shape)
        drawn = base * np.exp(spread * noise) if base else spread * noise
        out[name] = jnp.asarray(drawn.astype(out[name].dtype))
    for name, factor in factors.items():
        out[name] = (out[name] * factor).astype(out[name].dtype)
    return out
```

```python
import numpy as np
import concourse.bass as bass
from concourse import mybir
from contextlib import ExitStack, contextmanager


N, D, P = 512, 768, 128
E, EC = 8704, 8704 // 128
KC, NT = D // P, N // P
H8, D8 = 8, 96
M_RF = 256
SLOT, RING = 1024, 6
NB = 4
ME, MF = 8, 384
NE, CAP, FX = 16, 64, 3072
NPAIR = NE // 2
FB, FC = FX // 512, FX // P
XSLOT, XRING = KC * 512, 6
SHARED = 1536
REL3, REL4 = 3, 4
BIG = 1e30
PACK, GROUPS = 4096, [(0, 24), (24, 48), (48, EC)]
PACKED = [(0, 1), (2, 3), (0, 1)]
SHIFT = 24 * P // 2
ROUND = 1.5 * 2 ** 23

COLS = [("L0_gnn_bn", D, P), ("L0_gnn_be", D, P), ("L0_gnn_b1", 3 * D, P), ("L0_gnn_ln_g", 3 * D, P),
        ("L0_gnn_ln_b", 3 * D, P), ("L0_gnn_b2", 3 * D, P), ("L0_gnn_bq", D, D8), ("L0_gnn_bk", D, D8),
        ("L0_gnn_bv", D, P), ("L0_gnn_bo", D, P), ("L0_mix_bq", D, D8), ("L0_mix_bk", D, D8),
        ("L0_mix_bv", D, P), ("L0_mix_proj_b", D, P), ("L0_ffn_b1", ME * MF, P), ("L1_gnn_b1", D, D8),
        ("L1_gnn_b2", D, P), ("L1_mix_b_proj", D, P), ("L1_mix_gamma", D, P), ("L1_mix_beta", D, P),
        ("L1_ffn_in_bias", MF, P), ("L2_gnn_b", 3 * D, P), ("L2_mix_b_proj", D, P),
        ("L2_ffn_b1", ME * MF, P), ("L3_mix_b_proj", D, P)]

SMALL = [("L0_Ws", (P, KC, ME)), ("L0_bs", (1, ME)), ("L2_Ws", (P, KC, ME)), ("L3_gate", (P, KC, NE)),
         ("rf0", (D8, M_RF)), ("rf1", (P, 2, M_RF)), ("q1", (P, KC, 4)), ("k1", (P, KC, 4)),
         ("q2", (P, KC, 1)), ("k2", (P, KC, 1)), ("fc", (P, P)), ("res", (P, P)),
         ("attn_l", (P, KC, 12)), ("attn_r", (P, KC, 12))]


def column_starts():
    at, out = 0, {}
    for name, n, width in COLS:
        out[name] = at
        at += n // width
    return out, at


class Tally:
    around = None

    def __init__(self, sem, known):
        self.sem, self.known, self.found = sem, dict(known), known
        self.n, self.loop, self.final = 0, None, bool(known)

    def tick(self, label=None):
        self.n += 1
        if label is not None:
            self.found[label] = (self.n, self.loop[0] if self.loop else None)
        return 1

    def now(self, ahead=0):
        if not self.loop:
            return self.n + ahead
        name, it = self.loop
        return it * self.known.get(("step", name), 1) + (self.n + ahead)

    def at(self, label, back=0):
        n, name = self.known[label] if self.final else (1, None)
        if name is None:
            return n
        step, times = self.known[("step", name)], self.known[("times", name)]
        if Tally.around and Tally.around[0] == name:
            return Tally.around[1] * step + (n - back * step)
        return n + (times - 1) * step


def program(nc, io, tables):
    f32, bf16, i32 = mybir.dt.float32, mybir.dt.bfloat16, mybir.dt.int32
    ALU, ACT, AX = mybir.AluOpType, mybir.ActivationFunctionType, mybir.AxisListType
    ctx = ExitStack()
    with ctx:
        def sb(name, shape, dt=f32):
            return ctx.enter_context(nc.sbuf_tensor(name, list(shape), dt))

        def sem(name):
            return ctx.enter_context(nc.semaphore(name))

        KB = 256
        CNT, A_, B_, C_, D_, XN_, T_, QK_, PQ_, XT_, WR_, E_, F_, END = (
            0, 32, 44, 56, 68, 80, 92, 108, 116, 124, 136, 160, 172, 184)
        mem = sb("mem", [P, END * KB])

        def area(kb, a, b, c=None, rows=P):
            size = a * b * (c or 1)
            v = mem[0:rows, int(kb * KB):int(kb * KB) + size]
            if c is None:
                return v.rearrange("p (a b) -> p a b", a=a)
            return v.rearrange("p (a b c) -> p a b c", a=a, b=b)

        def chunks(kb, n=KC):
            return area(kb, n, N)

        def tokens(kb):
            return area(kb, NT, D)

        def heads96(kb):
            return area(kb, H8, N, rows=D8)

        cnt = [area(CNT + 8 * r, NT, N) for r in range(4)]
        XT, XN = chunks(XT_), chunks(XN_)
        ring = area(WR_, RING, SLOT)
        qk = area(QK_, 4, N)
        sq = chunks(T_)
        iota_f = area(QK_, 1, N)[:, 0, :]
        iota_i = area(QK_ + 2, 1, N)[:, 0, :].bitcast(i32)
        edge_i = area(QK_ + 4, 4, EC).bitcast(i32)
        edge_f = area(QK_ + 5.25, 6, EC)
        feats = area(CNT, EC, 256)
        onehot32 = area(E_, 4, N)
        onehot_a = area(F_, 4, N // 2).bitcast(bf16)
        onehot_b = area(F_ + 4, 4, N // 2).bitcast(bf16)
        edge_sum, edge_sum_t = area(PQ_, NT, 256), area(PQ_ + 4, 2, N)
        fresh = [area(B_, NT, N), area(B_ + 8, NT, N), area(B_ + 16, NT, N), area(T_ + 8, NT, N)]
        group_sum, group_high = area(T_, NT, N), area(E_, NT, N)
        probs, probs_t = area(T_, NT, N), area(T_ + 8, NT, N)
        att96, h96 = heads96(C_), heads96(D_)
        pq0, pk0, kv0 = area(PQ_, 2, N), area(PQ_ + 4, NT, M_RF), area(E_, 2, 2 * D8)
        pq1, pk1, kv1 = area(PQ_, 2, 2, N), area(E_, NT, M_RF), area(F_, 2, 2, 2 * P)
        ktok = area(E_, NT, P)
        scores = area(T_, 3, NT, N)
        weights_t = [area(84, NT, N), area(CNT + 24, NT, N)]
        weights_t3 = area(D_, 3, NT, N)
        krow = area(PQ_, 3, N, rows=12)
        mask = [area(E_ + 8 * r, NT, N) for r in range(3)]
        hidden = chunks(A_, 24)
        scale_row = chunks(T_, ME)
        comb_t = area(PQ_, 1, N, rows=ME)[:, 0, :]
        shared_hidden = chunks(T_, SHARED // P)
        weights_g = [area(CNT + 8, NT, N), area(CNT + 16, NT, N)]
        x_ring = area(0, XRING, XSLOT)
        place_t = area(72, NPAIR, N)
        x_rows = tokens(T_)
        x_hidden, x_hidden_t = area(T_, FB, 512), area(T_ + 12, FC, P)
        choose = area(PQ_, 4, N, rows=NE)
        x_pair = area(PQ_, KC, P)
        x_slots = area(WR_, KC, NE * CAP)
        place = area(E_, NT, NE * CAP)
        x_out = area(E_, NPAIR, D)

        cols_at, n_cols = column_starts()
        cols = sb("cols", [P, n_cols])
        small = {name: sb(name, shape) for name, shape in SMALL}
        ident, ones = sb("ident", [P, P]), sb("ones", [P, P])
        neg_half, neg_half_pair = sb("neg_half", [P, M_RF]), sb("neg_half_pair", [P, 2, M_RF])
        EV = sb("EV", [P, 2, N])
        mean, rstd = sb("mean", [P, N]), sb("rstd", [P, N])
        diag = [buf[:, :].rearrange("p (t d) -> p t d", t=NT) for buf in (mean, rstd)]
        degree = [EV[:, 0, :], mean[:, :], rstd[:, :], area(F_, 1, N)[:, 0, :]]
        eps_col, shift_col, round_col, unround_col = (sb(n, [P, 1]) for n in ("eps_col", "shift_col", "round_col", "unround_col"))
        one_row, shift_row = sb("one_row", [1, P], bf16), sb("shift_row", [1, N], bf16)
        down8 = sb("down8", [P, ME])
        stat = sb("stat", [P, 256])
        logit, comb, gate_exp = sb("logit", [P, NT, ME]), sb("comb", [P, NT, ME]), sb("gate_exp", [P, NT, ME])
        kv_diag = sb("kv_diag", [P, 2, P])
        slot_iota = sb("slot_iota", [P, CAP])
        slot_of, score_of = sb("slot_of", [P, NT, NE]), sb("score_of", [P, NT, NE])
        slot_score = sb("slot_score", [P, NPAIR * NE])

        bank = [ctx.enter_context(nc.psum_tensor(f"bank{i}", [P, 512], f32)) for i in range(8)]

        tally = {n: Tally(sem(n), tables.setdefault(n, {})) for n in
                 ("bank_full", "bank_free", "tile_free", "x_tile_free", "agg_done", "act_done", "dve_done", "pool_done")}
        bank_full, bank_free, tile_free, x_tile_free, agg_done, act_done, dve_done, pool_done = (tally[n] for n in tally)
        w_in = [sem(f"w_in{i}") for i in range(RING)]
        x_tile_in = [sem(f"x_tile_in{i}") for i in range(XRING)]
        x_in, cols_in, small_in, edge_in = sem("x_in"), sem("cols_in"), sem("small_in"), sem("edge_in")
        feat_in = [sem(f"feat_in{i}") for i in range(4)]
        onehot_ready, onehot_used = sem("onehot_ready"), sem("onehot_used")
        spilled = [sem(f"spilled{r}") for r in range(REL4 + 1)]
        reloaded, out_done = [sem("reloaded4"), sem("reloaded1")], sem("out_done")

        def col(name, i, rows=P):
            at = cols_at[name] + i
            if isinstance(i, int):
                return cols[0:rows, at:at + 1]
            return cols[0:rows, bass.ds(at, 1)]

        @contextmanager
        def loop(eng, name, times, mine):
            starts = [t.n for t in mine]
            with eng.Fori(0, times) as it:
                for t in mine:
                    t.loop = (name, it)
                Tally.around = (name, it)
                yield it
            for t, start in zip(mine, starts):
                step = t.n - start
                t.found[("step", name)], t.found[("times", name)] = step, times
                t.known[("step", name)], t.known[("times", name)] = step, times
                t.n, t.loop = start + times * step, None
            Tally.around = None

        HB = [(2 * m + s, slice(64 * s, 64 * s + 64), s) for m in range(KC) for s in range(2)]
        RGAT1, RGAT2, GAT = ("rgat1", 4, 3), ("rgat2", 1, 3), ("gat", 12, 1)

        block = ctx.enter_context(nc.Block())

        @block.sync
        def _(sp):
            sp.dma_start(XT, io["xT"]).then_inc(x_in, 16)
            sp.dma_start(cols[:, :], io["cols"]).then_inc(cols_in, 16)
            for s in range(RING):
                sp.dma_start(ring[:, s, :], io["weights"][s]).then_inc(w_in[s], 16)
            with sp.Fori(0, io["weights"].shape[0] // RING - 1) as i:
                for s in range(RING):
                    sp.wait_ge(tile_free.sem, i * RING + (s + 1))
                    sp.dma_start(ring[:, s, :], io["weights"][bass.ds(i * RING + (RING + s), 1), :, :]
                                 .rearrange("a p n -> p (a n)")).then_inc(w_in[s], 16)
            with sp.Fori(1, io["experts"].shape[0] // XRING) as i:
                for s in range(XRING):
                    sp.wait_ge(x_tile_free.sem, i * XRING + (s + 1 - XRING))
                    sp.dma_start(x_ring[:, s, :], io["experts"][bass.ds(i * XRING + s, 1), :, :]
                                 .rearrange("a p n -> p (a n)")).then_inc(x_tile_in[s], 16)
            sp.wait_ge(dve_done.sem, dve_done.at("result"))
            sp.dma_start(io["out"], XT).then_inc(out_done, 16)
            sp.wait_ge(out_done, 16)

        @block.gpsimd
        def _(pool):
            for n in range(4):
                pool.dma_start(edge_i[:, n, :], io["edges"][n]).then_inc(edge_in, 16)
            for name, shape in SMALL:
                pool.dma_start(small[name][tuple(slice(None) for _ in shape)], io[name]).then_inc(small_in, 16)
            nc.gpsimd.iota(iota_i, pattern=[[1, N]], base=0, channel_multiplier=0)
            nc.gpsimd.memset(ident[:, :], 0.0)
            nc.gpsimd.memset(neg_half[:, :], -0.5)
            nc.gpsimd.memset(neg_half_pair[:, :, :], 0.0)
            nc.gpsimd.memset(kv_diag[:, :, :], 0.0)
            nc.gpsimd.memset(eps_col[:, :], 1e-5)
            nc.gpsimd.memset(shift_col[:, :], float(SHIFT))
            nc.gpsimd.memset(round_col[:, :], ROUND)
            nc.gpsimd.memset(unround_col[:, :], -ROUND * PACK)
            nc.gpsimd.memset(one_row[:, :], 1.0)
            nc.gpsimd.memset(shift_row[:, :], -float(SHIFT))
            for e in range(ME):
                nc.gpsimd.memset(down8[:, e:e + 1], float(ME - e))
            nc.gpsimd.memset(ones[:, :], 1.0).then_inc(pool_done.sem, pool_done.tick("zeros"))
            pool.wait_ge(pool_done.sem, pool_done.at("zeros"))
            nc.gpsimd.affine_select(out=ident[:, :], in_=ident[:, :], compare_op=ALU.not_equal, fill=1.0,
                                                   base=0, pattern=[[-1, P]], channel_multiplier=1).then_inc(
                                                           pool_done.sem, pool_done.tick("ident"))
            pool.wait_ge(pool_done.sem, pool_done.at("ident"))
            nc.gpsimd.memset(neg_half_pair[0:64, 0, :], -0.5).then_inc(pool_done.sem, pool_done.tick("upper"))
            pool.wait_ge(pool_done.sem, pool_done.at("upper"))
            nc.gpsimd.memset(neg_half_pair[64:128, 1, :], -0.5).then_inc(pool_done.sem, pool_done.tick("consts"))
            for p in range(len(PACKED)):
                low, high = (fresh[2 * p], fresh[2 * p + 1]) if p < 2 else (cnt[0], cnt[1])
                for g in range(len(GROUPS)):
                    n = len(GROUPS) * p + g
                    pool.wait_ge(act_done.sem, act_done.at(("high", n)))
                    if g == 0:
                        nc.gpsimd.tensor_tensor(low, group_sum, high, ALU.subtract).then_inc(
                            pool_done.sem, pool_done.tick(("unpacked", n)))
                        continue
                    nc.gpsimd.tensor_tensor(group_sum, group_sum, group_high, ALU.subtract).then_inc(
                        pool_done.sem, pool_done.tick(("low", n)))
                    pool.wait_ge(pool_done.sem, pool_done.at(("low", n)))
                    nc.gpsimd.tensor_tensor(low, low, group_sum, ALU.add).then_inc(pool_done.sem, pool_done.tick())
                    nc.gpsimd.tensor_tensor(high, high, group_high, ALU.add).then_inc(
                            pool_done.sem, pool_done.tick(("unpacked", n)))
                if p < 2:
                    pool.wait_ge(act_done.sem, act_done.at(("unweighted", p)))
                if p == 0:
                    nc.gpsimd.tensor_tensor(cnt[3], low, high, ALU.add).then_inc(pool_done.sem, pool_done.tick("count_half"))
                if p == 1:
                    nc.gpsimd.tensor_tensor(cnt[3], cnt[3], low, ALU.add).then_inc(pool_done.sem, pool_done.tick("count_most"))
                    pool.wait_ge(pool_done.sem, pool_done.at("count_most"))
                    nc.gpsimd.tensor_tensor(cnt[3], cnt[3], high, ALU.add).then_inc(pool_done.sem, pool_done.tick("count_all"))
            for r in range(REL4):
                pool.wait_ge(dve_done.sem, dve_done.at(("norm", r)))
                pool.dma_start(io["scratch"][r], fresh[r]).then_inc(spilled[r], 16)
            pool.wait_ge(bank_free.sem, bank_free.at(("count_t", NT - 1)))
            pool.dma_start(io["scratch"][REL4], cnt[2]).then_inc(spilled[REL4], 16)
            for done in spilled:
                pool.wait_ge(done, 16)
            pool.wait_ge(act_done.sem, act_done.at(("unweighted", 2)))
            nc.gpsimd.tensor_tensor(cnt[2], cnt[2], cnt[0], ALU.subtract).then_inc(pool_done.sem, pool_done.tick("count_rest"))
            pool.wait_ge(pool_done.sem, pool_done.at("count_rest"))
            nc.gpsimd.tensor_tensor(cnt[2], cnt[2], cnt[1], ALU.subtract).then_inc(pool_done.sem, pool_done.tick("counts"))
            pool.wait_ge(dve_done.sem, dve_done.at("rgat2_last"))
            for r in range(REL4):
                pool.dma_start(cnt[r], io["scratch"][r]).then_inc(reloaded[0], 16)
            pool.wait_ge(dve_done.sem, dve_done.at(("routb_x", KC - 1)))
            pool.dma_start(cnt[0], io["scratch"][REL4]).then_inc(reloaded[1], 16)

        @block.tensor
        def _(pe):
            state = {"tile": 0, "x_tile": 0, "pending": None}

            def mm(out, lhsT, rhs, start=True, stop=True, last=False, transpose=False):
                if transpose:
                    ins = nc.tensor.transpose(out, lhsT, ident[0:lhsT.shape[0], 0:lhsT.shape[0]])
                else:
                    ins = nc.tensor.matmul(out, lhsT, rhs, start=start, stop=stop)
                if state["pending"] and not last:
                    ins.then_inc(state["pending"].sem, state["pending"].tick())
                    state["pending"] = None
                return ins

            def open_bank():
                if bank_full.loop or bank_full.n >= NB:
                    pe.wait_ge(bank_free.sem, bank_full.now(1 - NB))
                return bank[bank_full.n % NB]

            def group(out, pairs, last=True):
                pairs = list(pairs)
                for n, (lhsT, rhs) in enumerate(pairs):
                    end = n == len(pairs) - 1
                    ins = mm(out, lhsT, rhs, n == 0, end, last and end)
                return ins

            def take_tile():
                t = state["tile"]
                value = 16 * (t // RING + 1)
                if tile_free.loop:
                    name, it = tile_free.loop
                    value = it * (16 * (tile_free.known.get(("step", name), RING) // RING)) + value
                pe.wait_ge(w_in[t % RING], value)
                state["tile"] += 1
                return t % RING

            def take_x_tile(it, per):
                t = state["x_tile"] % per
                pe.wait_ge(x_tile_in[t % XRING], it * (16 * per // XRING) + 16 * (t // XRING + 1))
                state["x_tile"] += 1
                return t % XRING

            def linear(label, n_out, tiles, moving, ready=None, width=P, extra=None):
                total = sum(n for n, _ in tiles) + (extra is not None)
                for m in range(n_out):
                    out = open_bank()[0:width, :]
                    k = 0
                    for n, rows in tiles:
                        slot = take_tile()
                        for j in range(n):
                            if m == 0 and ready:
                                ready(k)
                            k += 1
                            ins = mm(out, ring[0:rows, slot, j * width:(j + 1) * width], moving(k - 1),
                                     k == 1, k == total, k == total)
                        if k < total - (extra is not None):
                            state["pending"] = tile_free
                    if extra is not None:
                        ins = mm(out, ring[0:ME, slot, KC * P:KC * P + P], extra, False, True, True)
                    state["pending"] = tile_free
                    ins.then_inc(bank_full.sem, bank_full.tick((label, m)))

            def to_tokens(label, source, ready=None):
                for t in range(NT):
                    for half in range(2):
                        out = open_bank()
                        for j in range(3):
                            m = 3 * half + j
                            if ready and t == 0:
                                ready(m)
                            ins = mm(out[:, j * P:(j + 1) * P], source[:, m, t * P:(t + 1) * P], None,
                                     last=j == 2, transpose=True)
                        ins.then_inc(bank_full.sem, bank_full.tick((label, 2 * t + half)))

            def norm_sums(label, source, ready=None):
                out = open_bank()
                for k in range(KC):
                    if ready:
                        ready(k)
                    ins = mm(out[:, :], ones[:, :], source[:, k, :], k == 0, k == KC - 1, k == KC - 1)
                ins.then_inc(bank_full.sem, bank_full.tick((label, "sum")))
                out = open_bank()
                for k in range(KC):
                    pe.wait_ge(act_done.sem, act_done.at((label, "sq", k)))
                    ins = mm(out[:, :], ones[:, :], sq[:, k, :], k == 0, k == KC - 1, k == KC - 1)
                ins.then_inc(bank_full.sem, bank_full.tick((label, "var")))

            def after(what, label, back=0):
                return lambda k: pe.wait_ge(what.sem, what.at((label, k), back))

            def all_of(what, label, n=KC):
                pe.wait_ge(what.sem, what.at((label, n - 1)))

            def aggregate(label, node_rows, counts):
                for m in range(KC):
                    out = open_bank()
                    ins = group(out[:, :], [(node_rows[:, t, m * P:(m + 1) * P], counts[:, t, :]) for t in range(NT)])
                    ins.then_inc(bank_full.sem, bank_full.tick((label, m)))

            x_n = lambda k: XN[:, k, :]
            of = lambda source: (lambda k: source[:, k, :])
            WHOLE, BY96 = [(KC, P)], [(H8, D8)]

            pe.wait_ge(x_in, 16)
            pe.wait_ge(pool_done.sem, pool_done.at("consts"))
            norm_sums("ln0", XT)

            def edge_chunks(start, stop, n, product, opened):
                def four(at, first=False, last=False):
                    for b in range(4):
                        pe.wait_ge(onehot_ready, at + (b + 1))
                        for c in range(NT):
                            ins = product(at, b, c, first and b == 0, last and b == 3)
                        ins.then_inc(onehot_used, 1)
                if not opened:
                    four(n * EC + start, first=True)
                with pe.Fori(start // 4 + (not opened), stop // 4 - 1) as i:
                    four(i * 4 + n * EC)
                four(n * EC + stop - 4, last=True)

            def feature_product(at, b, c, first, last):
                return nc.tensor.matmul(bank[4 + c][:, 0:256], onehot32[:, b, c * P:(c + 1) * P],
                                        feats[:, at + b, :] if isinstance(at, int) else
                                        feats[:, bass.ds(at + b, 1), :].rearrange("p a f -> p (a f)"),
                                        start=first, stop=last)

            for g in range(4):
                pe.wait_ge(feat_in[g], 16)
            edge_chunks(0, EC, 0, feature_product, False)
            for f in range(2):
                out = open_bank()
                pe.wait_ge(act_done.sem, act_done.at("edge_sum"))
                for t in range(NT):
                    ins = mm(out[:, t * P:(t + 1) * P], edge_sum[:, t, f * P:(f + 1) * P], None, last=t == 3, transpose=True)
                ins.then_inc(bank_full.sem, bank_full.tick(("edge_sum_t", f)))
            for p in range(len(PACKED)):
                for g, (start, stop) in enumerate(GROUPS):
                    n = len(GROUPS) * p + g
                    banks = bank[4:] if n % 2 == 0 else bank[:4]
                    if n >= 2:
                        pe.wait_ge(act_done.sem, act_done.at(("group", n - 2)))
                    elif n == 1:
                        pe.wait_ge(bank_free.sem, bank_free.at(("edge_sum_t", 1)))
                    for c in range(NT):
                        nc.tensor.matmul(banks[c][:, :], one_row[:, :], shift_row[:, :], start=True, stop=False)

                    def count_product(at, b, c, first, last):
                        return nc.tensor.matmul(banks[c][:, :], onehot_a[:, b, c * P:(c + 1) * P], onehot_b[:, b, :],
                                                start=False, stop=last)

                    edge_chunks(start, stop, p + 1, count_product, True)
            pe.wait_ge(act_done.sem, act_done.at(("group", len(GROUPS) * len(PACKED) - 2)))
            pe.wait_ge(pool_done.sem, pool_done.at("count_all"))
            for c in range(NT):
                out = open_bank()
                for t in range(NT):
                    ins = mm(out[:, t * P:(t + 1) * P], cnt[3][:, t, c * P:(c + 1) * P], None, last=t == NT - 1, transpose=True)
                ins.then_inc(bank_full.sem, bank_full.tick(("count_t", c)))
            for r in range(REL4):
                out = open_bank()
                ins = group(out[:, :], [(ones[:, :], fresh[r][:, c, :]) for c in range(NT)])
                ins.then_inc(bank_full.sem, bank_full.tick(("degree", r)))

            pe.wait_ge(small_in, 16 * len(SMALL))

            def softmax_attention():
                linear("v0", KC, WHOLE, of(chunks(A_)), lambda k: pe.wait_ge(dve_done.sem, dve_done.at(("nodes", k))))
                to_tokens("v0_tok", chunks(C_), after(bank_free, "v0"))
                v_tok = tokens(B_)
                for h in range(H8):
                    if h == 0:
                        linear(("aq", h), 1, WHOLE, of(chunks(A_)), width=D8)
                        linear(("ak", h), 1, WHOLE, of(chunks(A_)), width=D8)
                    pe.wait_ge(bank_free.sem, bank_free.at((("ak", h), 0)))
                    for t in range(NT):
                        out = open_bank()
                        own = 2 * (h % 2)
                        ins = mm(out[:, :], qk[0:D8, own, t * P:(t + 1) * P], qk[0:D8, own + 1, :], last=True)
                        ins.then_inc(bank_full.sem, bank_full.tick(("scores", h, t)))
                    if h + 1 < H8:
                        linear(("aq", h + 1), 1, WHOLE, of(chunks(A_)), width=D8)
                        linear(("ak", h + 1), 1, WHOLE, of(chunks(A_)), width=D8)
                    pe.wait_ge(dve_done.sem, dve_done.at(("probs", h)))
                    for c in range(NT):
                        out = open_bank()
                        for t in range(NT):
                            ins = mm(out[:, t * P:(t + 1) * P], probs[:, t, c * P:(c + 1) * P], None,
                                     last=t == NT - 1, transpose=True)
                        ins.then_inc(bank_full.sem, bank_full.tick(("probs_t", h, c)))
                    out = open_bank()
                    if h == 0:
                        all_of(bank_free, "v0_tok", 8)
                    for c in range(NT):
                        pe.wait_ge(bank_free.sem, bank_free.at(("probs_t", h, c)))
                        ins = mm(out[0:D8, :], v_tok[:, c, h * D8:(h + 1) * D8], probs_t[:, c, :],
                                 c == 0, c == NT - 1, c == NT - 1)
                    ins.then_inc(bank_full.sem, bank_full.tick(("att", h)))
                linear("wo", KC, BY96, of(att96), lambda k: pe.wait_ge(bank_free.sem, bank_free.at(("att", k))))

            def performer96():
                linear("v1", KC, WHOLE, x_n)
                to_tokens("v1_tok", chunks(C_), after(bank_free, "v1"))
                v_tok = tokens(B_)
                for h in range(H8):
                    linear(("mq", h), 1, WHOLE, x_n, width=D8)
                    linear(("mk", h), 1, WHOLE, x_n, width=D8)
                    pe.wait_ge(act_done.sem, act_done.at(("m_sq", h)))
                    for m in range(2):
                        out = open_bank()
                        ins = group(out[:, :], [(small["rf0"][:, m * P:(m + 1) * P], qk[0:D8, 0, :]),
                                                (neg_half[0:D8, 0:P], qk[0:D8, 2, :])])
                        ins.then_inc(bank_full.sem, bank_full.tick(("m_phi_q", h, m)))
                    for j in range(2):
                        out = open_bank()
                        for t in (2 * j, 2 * j + 1):
                            node = slice(t * P, (t + 1) * P)
                            ins = group(out[:, (t % 2) * M_RF:(t % 2 + 1) * M_RF],
                                        [(qk[0:D8, 1, node], small["rf0"][:, :]), (qk[0:D8, 3, node], neg_half[0:D8, :])],
                                        t % 2 == 1)
                        ins.then_inc(bank_full.sem, bank_full.tick(("m_phi_k", h, j)))
                    pe.wait_ge(bank_free.sem, bank_free.at(("m_phi_k", h, 1)))
                    if h == 0:
                        all_of(bank_free, "v1_tok", 8)
                    out = open_bank()
                    for m in range(2):
                        feature = slice(m * P, (m + 1) * P)
                        group(out[:, m * 2 * D8:m * 2 * D8 + D8],
                              [(pk0[:, t, feature], v_tok[:, t, h * D8:(h + 1) * D8]) for t in range(NT)], False)
                        ins = group(out[:, m * 2 * D8 + D8:(m + 1) * 2 * D8],
                                    [(pk0[:, t, feature], ones[:, 0:D8]) for t in range(NT)], m == 1)
                    ins.then_inc(bank_full.sem, bank_full.tick(("m_kv", h)))
                    pe.wait_ge(bank_free.sem, bank_free.at(("m_kv", h)))
                    for j in range(2):
                        out = open_bank()
                        ins = group(out[0:D8, :], [(kv0[:, m, j * D8:(j + 1) * D8], pq0[:, m, :]) for m in range(2)])
                        ins.then_inc(bank_full.sem, bank_full.tick(("m_out", h, j)))
                linear("proj0", KC, BY96, of(att96), lambda k: pe.wait_ge(dve_done.sem, dve_done.at(("m_att", k))))

            def experts_of_one(tag, ln, source, gate, gate_bias):
                norm_sums(ln, XT, after(dve_done, source))
                out = open_bank()
                all_of(dve_done, ln)
                for t in range(NT):
                    pairs = [(XN[:, k, t * P:(t + 1) * P], gate[:, k, :]) for k in range(KC)]
                    if gate_bias is not None:
                        pairs.append((ones[0:1, :], gate_bias[0:1, :]))
                    ins = group(out[:, t * ME:(t + 1) * ME], pairs, t == NT - 1)
                ins.then_inc(bank_full.sem, bank_full.tick((tag, "logit")))
                linear((tag, "up0"), KC, WHOLE, x_n)
                out = open_bank()
                pe.wait_ge(dve_done.sem, dve_done.at((tag, "comb")))
                for t in range(NT):
                    ins = mm(out[0:ME, t * P:(t + 1) * P], comb[:, t, :], None, last=t == NT - 1, transpose=True)
                ins.then_inc(bank_full.sem, bank_full.tick((tag, "comb_t")))
                pe.wait_ge(bank_free.sem, bank_free.at((tag, "comb_t")))
                for e in range(ME):
                    out = open_bank()
                    ins = mm(out[:, :], ident[0:ME, e:e + 1].to_broadcast([ME, P]), comb_t, last=True)
                    ins.then_inc(bank_full.sem, bank_full.tick((tag, "scale", e)))
                linear((tag, "up1"), ME * MF // P - KC, WHOLE, x_n)
                linear((tag, "down"), KC, WHOLE * 4, of(hidden), after(dve_done, (tag, "hidden")), extra=comb_t)

            def performer64():
                linear("v2", KC, WHOLE, x_n, after(dve_done, "ln2"))
                to_tokens("v2_tok", chunks(D_), after(bank_free, "v2"))
                v_tok = tokens(B_)
                for p in range(KC):
                    linear(("nq", p), 1, WHOLE, x_n)
                    linear(("nk", p), 1, WHOLE, x_n)
                    pe.wait_ge(act_done.sem, act_done.at(("n_sq", p)))
                    if p == 0:
                        all_of(bank_free, "v2_tok", 8)
                    for s in range(2):
                        for m in range(2):
                            out = open_bank()
                            ins = group(out[:, :], [(small["rf1"][:, s, m * P:(m + 1) * P], qk[:, 0, :]),
                                                    (neg_half_pair[:, s, 0:P], qk[:, 2, :])])
                            ins.then_inc(bank_full.sem, bank_full.tick(("n_phi_q", p, s, m)))
                        for j in range(2):
                            out = open_bank()
                            for t in (2 * j, 2 * j + 1):
                                node = slice(t * P, (t + 1) * P)
                                ins = group(out[:, (t % 2) * M_RF:(t % 2 + 1) * M_RF],
                                            [(qk[:, 1, node], small["rf1"][:, s, :]),
                                             (qk[:, 3, node], neg_half_pair[:, s, :])], t % 2 == 1)
                            ins.then_inc(bank_full.sem, bank_full.tick(("n_phi_k", p, s, j)))
                        pe.wait_ge(bank_free.sem, bank_free.at(("n_phi_k", p, s, 1)))
                        out = open_bank()
                        for m in range(2):
                            feature = slice(m * P, (m + 1) * P)
                            group(out[:, m * 2 * P:m * 2 * P + P],
                                  [(pk1[:, t, feature], v_tok[:, t, p * P:(p + 1) * P]) for t in range(NT)], False)
                            ins = group(out[:, m * 2 * P + P:(m + 1) * 2 * P],
                                        [(pk1[:, t, feature], ones[:, :]) for t in range(NT)], m == 1)
                        ins.then_inc(bank_full.sem, bank_full.tick(("n_kv", p, s)))
                    for s in range(2):
                        pe.wait_ge(bank_free.sem, bank_free.at(("n_kv", p, s)))
                        for j in range(2):
                            out = open_bank()
                            ins = group(out[:, :], [(kv1[:, s, m, j * P:(j + 1) * P], pq1[:, s, m, :]) for m in range(2)])
                            ins.then_inc(bank_full.sem, bank_full.tick(("n_out", p, s, j)))
                linear("proj1", KC, WHOLE, of(chunks(A_)), after(dve_done, "n_att"))
                norm_sums("lny", chunks(C_), after(dve_done, "y"))

            def edge_logits(tag, heads, r, source, ready, q, k):
                out = open_bank()
                for t in range(NT):
                    if t == 0:
                        for j in range(KC):
                            ready(j)
                    ins = group(out[:, t * heads:(t + 1) * heads],
                                [(source[:, j, t * P:(t + 1) * P], q[:, j, :]) for j in range(KC)], t == NT - 1)
                ins.then_inc(bank_full.sem, bank_full.tick((tag, "q", r)))
                out = open_bank()
                ins = group(out[0:heads, :], [(k[:, j, :], source[:, j, :]) for j in range(KC)])
                ins.then_inc(bank_full.sem, bank_full.tick((tag, "k", r)))

            def edge_softmax_row(tag, heads, h, r):
                out = open_bank()
                pe.wait_ge(bank_free.sem, bank_free.at((tag, "k", r)))
                ins = mm(out[:, :], ident[0:heads, h:h + 1].to_broadcast([heads, P]), krow[0:heads, r, :], last=True)
                ins.then_inc(bank_full.sem, bank_full.tick((tag, "row", h, r)))

            def weights_transposed(tag, h, r, buf):
                pe.wait_ge(dve_done.sem, dve_done.at((tag, "diag", h)))
                for c in range(NT):
                    out = open_bank()
                    for t in range(NT):
                        ins = mm(out[:, t * P:(t + 1) * P], scores[:, buf, t, c * P:(c + 1) * P], diag[h % 2][:, t, :],
                                 last=t == NT - 1)
                    ins.then_inc(bank_full.sem, bank_full.tick((tag, "weights_t", h, r, c)))

            def rgat(which, source, tiles, ready, q, k):
                tag, heads, relations = which
                rows = [tokens(a) for a in (A_, B_, C_)]
                for r in range(relations):
                    linear((tag, "xr", r), KC, tiles, source, ready if r == 0 else None)
                    to_tokens((tag, "xr_tok", r), chunks(T_), after(bank_free, (tag, "xr", r)))
                    edge_logits(tag, heads, r, chunks(T_), lambda j: None, q, k)
                for r in range(relations):
                    edge_softmax_row(tag, heads, 0, r)
                all_of(bank_free, (tag, "xr_tok", relations - 1), 8)
                for h in range(heads):
                    for r in range(relations):
                        weights_transposed(tag, h, r, r)
                        if h + 1 < heads:
                            edge_softmax_row(tag, heads, h + 1, r)
                        if tag == "rgat1":
                            if r == 0 and h >= 2:
                                pe.wait_ge(act_done.sem, act_done.at((tag, "out", h - 2)))
                            for j in range(2):
                                f = (2 * h + j) * D8
                                for c in range(NT):
                                    pe.wait_ge(bank_free.sem, bank_free.at((tag, "weights_t", h, r, c)))
                                    ins = mm(bank[4 + 2 * (h % 2) + j][0:D8, :], rows[r][:, c, f:f + D8],
                                             weights_t[(relations * h + r) % 2][:, c, :],
                                             r == 0 and c == 0, r == 2 and c == NT - 1, True)
                            ins.then_inc(agg_done.sem, agg_done.tick((tag, relations * h + r)))
                    if tag == "rgat2":
                        for r in range(relations):
                            pe.wait_ge(bank_free.sem, bank_free.at((tag, "weights_t", h, r, NT - 1)))
                        for m in range(KC):
                            out = open_bank()
                            ins = group(out[:, :], [(rows[r][:, c, m * P:(m + 1) * P], weights_t3[:, r, c, :])
                                                    for r in range(relations) for c in range(NT)])
                            ins.then_inc(bank_full.sem, bank_full.tick((tag, "out", m)))

            def elu_attention():
                linear("v4", KC, WHOLE, x_n, after(dve_done, "ln4"))
                to_tokens("v4_tok", chunks(D_), after(bank_free, "v4"))
                v_tok = tokens(B_)
                for p in range(KC):
                    linear(("eq", p), 1, WHOLE, x_n)
                    linear(("ek", p), 1, WHOLE, x_n)
                    pe.wait_ge(dve_done.sem, dve_done.at(("e_k", p)))
                    out = open_bank()
                    for t in range(NT):
                        ins = mm(out[:, t * P:(t + 1) * P], qk[:, 1, t * P:(t + 1) * P], None, last=t == NT - 1, transpose=True)
                    ins.then_inc(bank_full.sem, bank_full.tick(("e_ktok", p)))
                    pe.wait_ge(bank_free.sem, bank_free.at(("e_ktok", p)))
                    if p == 0:
                        all_of(bank_free, "v4_tok", 8)
                    out = open_bank()
                    group(out[:, 0:P], [(ktok[:, t, :], v_tok[:, t, p * P:(p + 1) * P]) for t in range(NT)], False)
                    ins = group(out[:, P:2 * P], [(ktok[:, t, :], ones[:, :]) for t in range(NT)])
                    ins.then_inc(bank_full.sem, bank_full.tick(("e_kv", p)))
                    pe.wait_ge(bank_free.sem, bank_free.at(("e_kv", p)))
                    for j in range(2):
                        out = open_bank()
                        mm(out[:, :], kv_diag[:, j, :], qk[:, 0, :], last=True).then_inc(
                                bank_full.sem, bank_full.tick(("e_out", p, j)))
                linear("proj2", KC, WHOLE, of(chunks(A_)), after(dve_done, "e_att"))

            def rgcn_layer(tag, ready):
                x_rows = tokens(T_)
                g = [chunks(a) for a in (A_, B_, C_, D_)]
                for m in range(KC):
                    ready(m)
                for m in range(KC):
                    out = open_bank()
                    for t in range(NT):
                        ins = mm(out[:, t * P:(t + 1) * P], XN[:, m, t * P:(t + 1) * P], None, last=t == NT - 1, transpose=True)
                    ins.then_inc(bank_full.sem, bank_full.tick(((tag, "tok"), m)))
                all_of(bank_free, (tag, "tok"))
                for r in range(REL4):
                    aggregate((tag, "agg", r), x_rows, cnt[r])
                linear((tag, "out"), KC, WHOLE * 5, lambda k: XN[:, k, :] if k < KC else g[k // KC - 1][:, k % KC, :],
                       lambda k: pe.wait_ge(bank_free.sem, bank_free.at(((tag, "agg", k // KC - 1), k % KC))) if k >= KC else None)

            linear("nodes0", KC, WHOLE, x_n, after(dve_done, "ln0"))
            linear("edge_part", KC, [(2, P)], of(edge_sum_t), lambda k: pe.wait_ge(bank_free.sem, bank_free.at(("edge_sum_t", k))))
            for k in range(KC):
                pe.wait_ge(bank_free.sem, bank_free.at(("nodes0", k)))
            pe.wait_ge(dve_done.sem, dve_done.at("counts_looped"))
            with loop(pe, "gnn0", 3, (bank_full, tile_free)):
                to_tokens("tok0", chunks(A_), lambda m: pe.wait_ge(dve_done.sem, dve_done.at(("nodes", m), 1)))
                all_of(bank_free, "tok0", 8)
                aggregate("agg0", tokens(B_), cnt[3])
                linear("h0", KC, WHOLE * 2, lambda k: (chunks(A_) if k < KC else chunks(C_))[:, k % KC, :],
                       lambda k: pe.wait_ge(dve_done.sem, dve_done.at(("agg0_sum", k - KC))) if k >= KC else None)
                norm_sums("lnh", chunks(B_), after(bank_free, "h0"))
                linear("w2", KC, WHOLE, of(chunks(B_)), after(act_done, "relu0"))
            state["tile"] += 2 * 3 * KC
            softmax_attention()
            performer96()
            experts_of_one("moe0", "ln1", "proj0_x", small["L0_Ws"], small["L0_bs"])
            norm_sums("ln2", XT, after(dve_done, "moe0_x"))
            performer64()
            rgat(RGAT1, x_n, WHOLE, None, small["q1"], small["k1"])
            rgat(RGAT2, of(h96), BY96, lambda k: pe.wait_ge(dve_done.sem, dve_done.at((("rgat1", "elu"), k))), small["q2"], small["k2"])
            norm_sums("ln3", XT, after(dve_done, "rgat2_x"))
            linear("f1_up", MF // P, WHOLE, x_n, after(dve_done, "ln3"))
            linear("f1_down", KC, [(3, P)], of(chunks(A_)), after(bank_free, "f1_up"))
            norm_sums("ln4", XT, after(dve_done, "f1_x"))
            elu_attention()
            pe.wait_ge(reloaded[0], 16 * REL4)
            with loop(pe, "rgcn", 2, (bank_full, tile_free)):
                rgcn_layer("rgcn", lambda m: pe.wait_ge(dve_done.sem, dve_done.at((("rgcn", "x"), m), 1)))
            state["tile"] += 5 * KC
            rgcn_layer("rgcnb", lambda m: pe.wait_ge(dve_done.sem, dve_done.at((("rgcn", "x"), m))))
            experts_of_one("moe2", "ln5", "routb_x", small["L2_Ws"], None)

            def graph_attention():
                ft_t, ft_rows = chunks(B_), tokens(A_)
                for m in range(KC):
                    pe.wait_ge(dve_done.sem, dve_done.at(("ln6", m)))
                    out = open_bank()
                    mm(out[:, :], small["fc"][:, :], XN[:, m, :], last=True).then_inc(bank_full.sem, bank_full.tick(("ft", m)))
                to_tokens("ft_rows", ft_t, after(bank_free, "ft"))
                for m in range(KC):
                    out = open_bank()
                    mm(out[:, :], small["res"][:, :], XN[:, m, :], last=True).then_inc(bank_full.sem, bank_full.tick(("res", m)))
                tag, heads, relations = GAT
                edge_logits(tag, heads, 0, ft_t, lambda j: None, small["attn_r"], small["attn_l"])
                all_of(bank_free, "ft_rows", 8)

                def aggregated(h):
                    out = open_bank()
                    m = h // 2
                    for c in range(NT):
                        pe.wait_ge(bank_free.sem, bank_free.at((tag, "weights_t", h, 0, c)))
                        ins = mm(out[:, :], ft_rows[:, c, m * P:(m + 1) * P], weights_g[h % 2][:, c, :],
                                 c == 0, c == NT - 1, c == NT - 1)
                    ins.then_inc(bank_full.sem, bank_full.tick((tag, "agg", h)))

                for h in range(2):
                    edge_softmax_row(tag, heads, h, 0)
                for h in range(heads):
                    if h + 2 < heads:
                        edge_softmax_row(tag, heads, h + 2, 0)
                    weights_transposed(tag, h, 0, h % 3)
                    if h:
                        aggregated(h - 1)
                aggregated(heads - 1)

            def experts():
                out = open_bank()
                all_of(dve_done, "ln7")
                ins = group(out[0:NE, :], [(small["L3_gate"][:, k, :], XN[:, k, :]) for k in range(KC)])
                ins.then_inc(bank_full.sem, bank_full.tick("x_logit"))
                linear("shared_up", 2 * SHARED // P, WHOLE, x_n)
                linear("shared_down", KC, WHOLE * 2, of(shared_hidden), after(dve_done, "shared_hidden"))
                state["pending"] = None
                while state["tile"] % RING:
                    take_tile()
                to_tokens("x_rows", XN)
                for label, n in (("slots", 2), ("score", 1)):
                    out = open_bank()
                    pe.wait_ge(dve_done.sem, dve_done.at("x_slots"))
                    for t in range(NT):
                        ins = mm(out[:, t * NE:(t + 1) * NE], choose[:, n, t * P:(t + 1) * P], None, last=t == NT - 1, transpose=True)
                    ins.then_inc(bank_full.sem, bank_full.tick(("x_" + label, 0)))
                all_of(bank_free, "x_rows", 8)
                for m in range(KC):
                    for half in range(2):
                        out = open_bank()
                        pe.wait_ge(dve_done.sem, dve_done.at("x_place"))
                        some = slice(half * 512, half * 512 + 512)
                        ins = group(out[:, :], [(x_rows[:, t, m * P:(m + 1) * P], place[:, t, some]) for t in range(NT)])
                        ins.then_inc(bank_full.sem, bank_full.tick(("x_gather", m, half)))
                out = open_bank()
                for p in range(NPAIR):
                    ins = group(out[:, p * NE:(p + 1) * NE],
                                [(place[:, t, p * P:(p + 1) * P], score_of[:, t, :]) for t in range(NT)], p == NPAIR - 1)
                ins.then_inc(bank_full.sem, bank_full.tick("x_slot_score"))
                for p in range(NPAIR):
                    out = open_bank()
                    for t in range(NT):
                        ins = mm(out[:, t * P:(t + 1) * P], place[:, t, p * P:(p + 1) * P], None, last=t == NT - 1, transpose=True)
                    ins.then_inc(bank_full.sem, bank_full.tick(("x_place_t", p)))
                while bank_full.n % NB:
                    out = open_bank()
                    mm(out[:, 0:P], ones[:, :], ident[:, :], last=True).then_inc(bank_full.sem, bank_full.tick())
                pe.wait_ge(bank_free.sem, bank_free.at(("x_place_t", NPAIR - 1)))
                tiles = 2 * (2 * FB + FB)
                with loop(pe, "pairs", NPAIR, (bank_full, x_tile_free)) as pair:

                    pe.wait_ge(dve_done.sem, dve_done.at("x_pair"))
                    half_rows = [slice(CAP * e, CAP * e + CAP) for e in range(2)]
                    for b in range(FB):
                        for kind in ("x_gate", "x_up"):
                            out = open_bank()
                            slots = [take_x_tile(pair, tiles) for e in range(2)]
                            for k in range(KC):
                                for e, rows in enumerate(half_rows):
                                    ins = mm(out[rows, :], x_pair[:, k, rows], x_ring[:, slots[e], k * 512:(k + 1) * 512],
                                             k == 0, k == KC - 1, k == KC - 1)
                                    if k == KC - 1 and e == 0:
                                        ins.then_inc(x_tile_free.sem, x_tile_free.tick())
                            state["pending"] = x_tile_free
                            ins.then_inc(bank_full.sem, bank_full.tick((kind, b)))
                    for b in range(FB):
                        out = open_bank()
                        pe.wait_ge(dve_done.sem, dve_done.at(("x_h", b)))
                        for c in range(4):
                            ins = nc.tensor.transpose(out[:, c * P:(c + 1) * P], x_hidden[:, b, c * P:(c + 1) * P], ident[:, :])
                            if state["pending"]:
                                ins.then_inc(state["pending"].sem, state["pending"].tick())
                                state["pending"] = None
                        ins.then_inc(bank_full.sem, bank_full.tick(("x_h_t", b)))
                    for half in range(2):
                        out = open_bank()
                        for j in range(3):
                            slots = [take_x_tile(pair, tiles) for e in range(2)]
                            for k in range(8):
                                c = 8 * j + k
                                pe.wait_ge(bank_free.sem, bank_free.at(("x_h_t", c // 4)))
                                for e, rows in enumerate(half_rows):
                                    ins = mm(out[rows, 0:D // 2], x_hidden_t[:, c, rows],
                                             x_ring[:, slots[e], k * (D // 2):(k + 1) * (D // 2)], c == 0, c == FC - 1, k == 7)
                                    if k == 7 and e == 0:
                                        ins.then_inc(x_tile_free.sem, x_tile_free.tick())
                            state["pending"] = x_tile_free
                        ins.then_inc(bank_full.sem, bank_full.tick(("x_down", half)))
                    mm(bank[7][:, 0:1], ones[:, :], ident[:, 0:1])
                for m in range(KC):
                    out = open_bank()
                    pe.wait_ge(bank_free.sem, bank_free.at(("x_down", 1)))
                    ins = group(out[:, :], [(x_out[:, p, m * P:(m + 1) * P], place_t[:, p, :]) for p in range(NPAIR)])
                    ins.then_inc(bank_full.sem, bank_full.tick(("experts", m)))

            norm_sums("ln6", XT, after(dve_done, "moe2_x"))
            graph_attention()
            linear("xq", KC, WHOLE, x_n)
            linear("xk", KC, WHOLE, x_n)
            linear("xv", KC, WHOLE, x_n)
            linear("proj3", KC, WHOLE, of(chunks(T_)), after(dve_done, "xy"))
            norm_sums("ln7", XT, after(dve_done, "proj3_x"))
            experts()

        @block.scalar
        def _(act):
            ev_reader = [None, None]

            def filled():
                return bank[bank_free.n % NB]

            def linear(label, n_out, dst, func=ACT.Identity, bias=None, width=P, scale=1.0, before=None):
                for m in range(n_out):
                    act.wait_ge(bank_full.sem, bank_free.now(1))
                    src = filled()
                    if before:
                        before(m)
                    how = {} if bias is None else {"bias": bias(m)}
                    nc.scalar.activation(dst(m), src[0:width, :], func, scale=scale, **how).then_inc(
                            bank_free.sem, bank_free.tick((label, m)))

            def residual(label, bias=None):
                for m in range(KC):
                    act.wait_ge(bank_full.sem, bank_free.now(1))
                    src = filled()
                    if ev_reader[m % 2]:
                        act.wait_ge(dve_done.sem, dve_done.at(ev_reader[m % 2]))
                    how = {} if bias is None else {"bias": bias(m)}
                    nc.scalar.activation(EV[:, m % 2, :], src[:, :], ACT.Identity, **how).then_inc(
                            bank_free.sem, bank_free.tick((label, m)))
                    ev_reader[m % 2] = (label + "_x", m)

            def ev_free(n, label):
                if ev_reader[n]:
                    act.wait_ge(dve_done.sem, dve_done.at(ev_reader[n]))
                ev_reader[n] = label

            def to_tokens(label, dst):
                for t in range(NT):
                    for half in range(2):
                        act.wait_ge(bank_full.sem, bank_free.now(1))
                        nc.scalar.activation(dst[:, t, half * 3 * P:(half + 1) * 3 * P], filled()[:, 0:3 * P], ACT.Identity).then_inc(
                                bank_free.sem, bank_free.tick((label, 2 * t + half)))

            def norm(label, values):
                act.wait_ge(bank_full.sem, bank_free.now(1))
                nc.scalar.activation(mean[:, :], filled()[:, :], ACT.Identity, scale=1.0 / D).then_inc(
                        bank_free.sem, bank_free.tick((label, "sum")))
                for k in range(KC):
                    act.wait_ge(dve_done.sem, dve_done.at((label, "d", k)))
                    nc.scalar.activation(sq[:, k, :], values[:, k, :], ACT.Square).then_inc(
                            act_done.sem, act_done.tick((label, "sq", k)))
                act.wait_ge(bank_full.sem, bank_free.now(1))
                nc.scalar.activation(rstd[:, :], filled()[:, :], ACT.Sqrt, scale=1.0 / D, bias=eps_col[:, :]).then_inc(
                        bank_free.sem, bank_free.tick((label, "var")))

            def of(dst):
                return lambda m: dst[:, m, :]

            def bias_of(name, rows=P):
                return lambda m: col(name, m, rows)

            for g in range(4):
                n = EC // 4
                act.dma_start(feats[:, g * n:(g + 1) * n, :], io["feats"][:, g * n:(g + 1) * n, :]).then_inc(feat_in[g], 16)
            act.wait_ge(cols_in, 16)
            act.wait_ge(pool_done.sem, pool_done.at("consts"))
            norm("ln0", XN)
            act.wait_ge(onehot_used, EC)
            for t in range(NT):
                nc.scalar.activation(edge_sum[:, t, :], bank[4 + t][:, 0:256], ACT.Identity).then_inc(
                        act_done.sem, act_done.tick("edge_sum"))
            for f in range(2):
                act.wait_ge(bank_full.sem, bank_free.now(1))
                nc.scalar.activation(edge_sum_t[:, f, :], filled()[:, :], ACT.Identity).then_inc(
                        bank_free.sem, bank_free.tick(("edge_sum_t", f)))

            def unweighted(p):
                high = (fresh[1], fresh[3], cnt[1])[p]
                nc.scalar.activation(high, high, ACT.Identity, scale=1.0 / PACK).then_inc(
                        act_done.sem, act_done.tick(("unweighted", p)))

            for p in range(len(PACKED)):
                for g, (_, stop) in enumerate(GROUPS):
                    n = len(GROUPS) * p + g
                    banks = bank[4:] if n % 2 == 0 else bank[:4]
                    high = group_high if g else (fresh[1], fresh[3], cnt[1])[p]
                    act.wait_ge(onehot_used, EC * (p + 1) + stop)
                    if n:
                        act.wait_ge(pool_done.sem, pool_done.at(("unpacked", n - 1)))
                    if g == 0 and p:
                        unweighted(p - 1)
                    for c in range(NT):
                        nc.scalar.activation(high[:, c, :], banks[c][:, :], ACT.Identity, scale=1.0 / PACK, bias=round_col[:, :]).then_inc(
                            act_done.sem, act_done.tick(("rounded", n)))
                        nc.scalar.activation(group_sum[:, c, :], banks[c][:, :], ACT.Identity, bias=shift_col[:, :]).then_inc(
                            act_done.sem, act_done.tick(("group", n)))
                    act.wait_ge(act_done.sem, act_done.at(("rounded", n)))
                    nc.scalar.activation(high, high, ACT.Identity, scale=float(PACK), bias=unround_col[:, :]).then_inc(
                        act_done.sem, act_done.tick(("high", n)))
            for c in range(NT):
                act.wait_ge(bank_full.sem, bank_free.now(1))
                nc.scalar.activation(cnt[2][:, c, :], filled()[:, :], ACT.Identity).then_inc(
                        bank_free.sem, bank_free.tick(("count_t", c)))
            for r in range(REL4):
                act.wait_ge(bank_full.sem, bank_free.now(1))
                nc.scalar.activation(degree[r], filled()[:, :], ACT.Identity).then_inc(
                        bank_free.sem, bank_free.tick(("degree", r)))
            act.wait_ge(pool_done.sem, pool_done.at(("unpacked", len(PACKED) * len(GROUPS) - 1)))
            unweighted(2)

            def softmax_attention():
                linear("v0", KC, of(chunks(C_)), bias=bias_of("L0_gnn_bv"))
                to_tokens("v0_tok", tokens(B_))
                s = float(D8) ** -0.5

                def queries_and_keys(h):
                    for j, (name, b) in enumerate((("aq", "L0_gnn_bq"), ("ak", "L0_gnn_bk"))):
                        linear((name, h), 1, lambda m: qk[0:D8, 2 * (h % 2) + j, :], bias=lambda m: col(b, h, D8), width=D8)

                queries_and_keys(0)
                for h in range(H8):
                    for t in range(NT):
                        act.wait_ge(bank_full.sem, bank_free.now(1))
                        src = filled()
                        act.wait_ge(dve_done.sem, dve_done.at(("neg_max", h, t)))
                        nc.scalar.activation(probs[:, t, :], src[:, :], ACT.Exp, bias=stat[:, 4 + t:5 + t], scale=s, accum_out=stat[:, 8 + t:9 + t]).then_inc(
                                bank_free.sem, bank_free.tick(("exp", h, t)))
                    if h + 1 < H8:
                        queries_and_keys(h + 1)
                    for c in range(NT):
                        act.wait_ge(bank_full.sem, bank_free.now(1))
                        nc.scalar.activation(probs_t[:, c, :], filled()[:, :], ACT.Identity).then_inc(
                                bank_free.sem, bank_free.tick(("probs_t", h, c)))
                    act.wait_ge(bank_full.sem, bank_free.now(1))
                    nc.scalar.activation(att96[:, h, :], filled()[0:D8, :], ACT.Identity).then_inc(
                            bank_free.sem, bank_free.tick(("att", h)))
                residual("wo", bias_of("L0_gnn_bo"))

            def performer96():
                s = float(D8) ** -0.5
                linear("v1", KC, of(chunks(C_)), bias=bias_of("L0_mix_bv"))
                to_tokens("v1_tok", tokens(B_))
                act.wait_ge(dve_done.sem, dve_done.at("scaled_bias"))
                for h in range(H8):
                    for j, name in enumerate(("mq", "mk")):
                        linear((name, h), 1, lambda m: qk[0:D8, j, :], bias=lambda m: stat[0:D8, 32 + 8 * j + h:33 + 8 * j + h],
                               width=D8, scale=s)
                    act.wait_ge(bank_free.sem, bank_free.at((("mk", h), 0)))
                    for j in range(2):
                        nc.scalar.activation(qk[0:D8, 2 + j, :], qk[0:D8, j, :], ACT.Square).then_inc(
                                act_done.sem, act_done.tick(("m_sq", h)))
                    for m in range(2):
                        act.wait_ge(bank_full.sem, bank_free.now(1))
                        nc.scalar.activation(pq0[:, m, :], filled()[:, :], ACT.Exp).then_inc(
                                bank_free.sem, bank_free.tick(("m_phi_q", h, m)))
                    for j in range(2):
                        act.wait_ge(bank_full.sem, bank_free.now(1))
                        nc.scalar.activation(pk0[:, 2 * j:2 * j + 2, :], filled()[:, :].rearrange("p (t m) -> p t m", t=2), ACT.Exp).then_inc(
                                bank_free.sem, bank_free.tick(("m_phi_k", h, j)))
                    act.wait_ge(bank_full.sem, bank_free.now(1))
                    nc.scalar.activation(kv0, filled()[:, 0:4 * D8].rearrange("p (m c) -> p m c", m=2), ACT.Identity).then_inc(
                            bank_free.sem, bank_free.tick(("m_kv", h)))
                    act.wait_ge(bank_full.sem, bank_free.now(1))
                    nc.scalar.activation(att96[:, h, :], filled()[0:D8, :], ACT.Identity).then_inc(
                            bank_free.sem, bank_free.tick(("m_out", h, 0)))
                    act.wait_ge(bank_full.sem, bank_free.now(1))
                    src = filled()
                    ev_free(h % 2, ("m_att", h))
                    nc.scalar.activation(EV[0:D8, h % 2, :], src[0:D8, :], ACT.Identity).then_inc(
                            bank_free.sem, bank_free.tick(("m_out", h, 1)))
                residual("proj0", bias_of("L0_mix_proj_b"))

            def experts_of_one(tag, ln, func, bias):
                norm(ln, XN)
                act.wait_ge(bank_full.sem, bank_free.now(1))
                nc.scalar.activation(logit[:, :, :], filled()[:, 0:NT * ME].rearrange("p (t e) -> p t e", t=NT), ACT.Identity).then_inc(
                        bank_free.sem, bank_free.tick((tag, "logit")))
                act.wait_ge(dve_done.sem, dve_done.at((tag, "shifted")))
                nc.scalar.activation(gate_exp[:, :, :], gate_exp[:, :, :], ACT.Exp).then_inc(
                        act_done.sem, act_done.tick((tag, "exp")))
                linear((tag, "up0"), KC, of(hidden), func, lambda m: col(bias, m))
                act.wait_ge(bank_full.sem, bank_free.now(1))
                nc.scalar.activation(comb_t, filled()[0:ME, :], ACT.Identity).then_inc(
                        bank_free.sem, bank_free.tick((tag, "comb_t")))
                for e in range(ME):
                    act.wait_ge(bank_full.sem, bank_free.now(1))
                    nc.scalar.activation(scale_row[:, e, :], filled()[:, :], ACT.Identity).then_inc(
                            bank_free.sem, bank_free.tick((tag, "scale", e)))
                linear((tag, "up1"), ME * MF // P - KC, lambda m: hidden[:, KC + m, :], func, lambda m: col(bias, KC + m))
                residual(tag)

            def performer64():
                linear("v2", KC, of(chunks(D_)))
                to_tokens("v2_tok", tokens(B_))
                for p in range(KC):
                    for j, name in enumerate(("nq", "nk")):
                        linear((name, p), 1, lambda m: qk[:, j, :])
                    act.wait_ge(bank_free.sem, bank_free.at((("nk", p), 0)))
                    for j in range(2):
                        nc.scalar.activation(qk[:, 2 + j, :], qk[:, j, :], ACT.Square).then_inc(
                                act_done.sem, act_done.tick(("n_sq", p)))
                    for s in range(2):
                        for m in range(2):
                            act.wait_ge(bank_full.sem, bank_free.now(1))
                            nc.scalar.activation(pq1[:, s, m, :], filled()[:, :], ACT.Exp).then_inc(
                                    bank_free.sem, bank_free.tick(("n_phi_q", p, s, m)))
                        for j in range(2):
                            act.wait_ge(bank_full.sem, bank_free.now(1))
                            nc.scalar.activation(pk1[:, 2 * j:2 * j + 2, :], filled()[:, :].rearrange("p (t m) -> p t m", t=2), ACT.Exp).then_inc(
                                    bank_free.sem, bank_free.tick(("n_phi_k", p, s, j)))
                        act.wait_ge(bank_full.sem, bank_free.now(1))
                        nc.scalar.activation(kv1[:, s, :, :], filled()[:, :].rearrange("p (m c) -> p m c", m=2), ACT.Identity, scale=1.0 / M_RF).then_inc(
                                bank_free.sem, bank_free.tick(("n_kv", p, s)))
                    ev_free(p % 2, ("n_att", p))
                    for s in range(2):
                        half = slice(64 * s, 64 * s + 64)
                        act.wait_ge(bank_full.sem, bank_free.now(1))
                        nc.scalar.activation(chunks(A_)[half, p, :], filled()[half, :], ACT.Identity).then_inc(
                                bank_free.sem, bank_free.tick(("n_out", p, s, 0)))
                        act.wait_ge(bank_full.sem, bank_free.now(1))
                        nc.scalar.activation(EV[half, p % 2, :], filled()[half, :], ACT.Identity).then_inc(
                                bank_free.sem, bank_free.tick(("n_out", p, s, 1)))
                linear("proj1", KC, of(chunks(C_)), bias=bias_of("L1_mix_b_proj"))
                norm("lny", chunks(C_))

            def edge_logits(tag, heads, r):
                act.wait_ge(bank_full.sem, bank_free.now(1))
                nc.scalar.activation(stat[:, 64 + r * NT * heads:64 + (r + 1) * NT * heads], filled()[:, 0:NT * heads], ACT.Identity).then_inc(
                        bank_free.sem, bank_free.tick((tag, "q", r)))
                act.wait_ge(bank_full.sem, bank_free.now(1))
                nc.scalar.activation(krow[0:heads, r, :], filled()[0:heads, :], ACT.Identity).then_inc(
                        bank_free.sem, bank_free.tick((tag, "k", r)))

            def edge_scores(tag, heads, h, r, buf):
                act.wait_ge(bank_full.sem, bank_free.now(1))
                src = filled()
                act.wait_ge(bank_free.sem, bank_free.at((tag, "q", r)))
                for t in range(NT):
                    at = 64 + (r * NT + t) * heads + h
                    ins = nc.scalar.activation(scores[:, buf, t, :], src[:, :], ACT.Identity, bias=stat[:, at:at + 1])
                    if t < NT - 1:
                        ins.then_inc(act_done.sem, act_done.tick((tag, "sum", h, r, t)))
                ins.then_inc(bank_free.sem, bank_free.tick((tag, "row", h, r)))

            def rgat(which, xr):
                tag, heads, relations = which
                for r in range(relations):
                    linear((tag, "xr", r), KC, of(chunks(T_)))
                    to_tokens((tag, "xr_tok", r), tokens((A_, B_, C_)[r]))
                    edge_logits(tag, heads, r)

                def exps(h):
                    act.wait_ge(dve_done.sem, dve_done.at((tag, "neg_max", h)))
                    for r in range(relations):
                        for t in range(NT):
                            nc.scalar.activation(scores[:, r, t, :], scores[:, r, t, :], ACT.Exp, bias=stat[:, 20 + t:21 + t]).then_inc(
                                act_done.sem, act_done.tick((tag, "exp", h, r, t)))

                for r in range(relations):
                    edge_scores(tag, heads, 0, r, r)
                exps(0)
                for h in range(heads):
                    for r in range(relations):
                        n = relations * h + r
                        for c in range(NT):
                            dst = weights_t[n % 2] if tag == "rgat1" else weights_t3[:, r]
                            act.wait_ge(bank_full.sem, bank_free.now(1))
                            src = filled()
                            if tag == "rgat1" and c == 0 and n >= 2:
                                act.wait_ge(agg_done.sem, agg_done.at((tag, n - 2)))
                            nc.scalar.activation(dst[:, c, :], src[:, :], ACT.Identity).then_inc(
                                bank_free.sem, bank_free.tick((tag, "weights_t", h, r, c)))
                        if h + 1 < heads:
                            edge_scores(tag, heads, h + 1, r, r)
                    if tag == "rgat1":
                        act.wait_ge(agg_done.sem, agg_done.at((tag, relations * h + relations - 1)))
                        for j in range(2):
                            nc.scalar.activation(h96[:, 2 * h + j, :], bank[4 + 2 * (h % 2) + j][0:D8, :], ACT.Identity,
                                                 bias=col("L1_gnn_b1", 2 * h + j, D8)).then_inc(
                                                         act_done.sem, act_done.tick((tag, "out", h)))
                    if h + 1 < heads:
                        exps(h + 1)
                    if tag == "rgat1":
                        for j in range(2):
                            act.wait_ge(dve_done.sem, dve_done.at((tag, "low", 2 * h + j)))
                            nc.scalar.activation(EV[0:D8, j, :], EV[0:D8, j, :], ACT.Exp).then_inc(
                                act_done.sem, act_done.tick((tag, "elu_exp", 2 * h + j)))
                if tag == "rgat2":
                    for m in range(KC):
                        act.wait_ge(bank_full.sem, bank_free.now(1))
                        src = filled()
                        ev_free(m % 2, ("rgat2_x", m))
                        nc.scalar.activation(EV[:, m % 2, :], src[:, :], ACT.Identity, bias=col("L1_gnn_b2", m)).then_inc(
                                bank_free.sem, bank_free.tick((tag, "out", m)))

            def elu_attention():
                linear("v4", KC, of(chunks(D_)))
                to_tokens("v4_tok", tokens(B_))
                for p in range(KC):
                    for j, name in enumerate(("eq", "ek")):
                        linear((name, p), 1, lambda m: qk[:, j, :])
                        act.wait_ge(dve_done.sem, dve_done.at(("e_low", p, j)))
                        nc.scalar.activation(qk[:, 2 + j, :], qk[:, 2 + j, :], ACT.Exp).then_inc(
                                act_done.sem, act_done.tick(("e_exp", p, j)))
                    act.wait_ge(bank_full.sem, bank_free.now(1))
                    nc.scalar.activation(ktok, filled()[:, :].rearrange("p (t f) -> p t f", t=NT), ACT.Identity).then_inc(
                            bank_free.sem, bank_free.tick(("e_ktok", p)))
                    act.wait_ge(bank_full.sem, bank_free.now(1))
                    src = filled()
                    for s in range(2):
                        half = slice(64 * s, 64 * s + 64)
                        ins = nc.scalar.activation(kv_diag[half, :, half],
                                                   src[half, 0:2 * P].rearrange("p (j f) -> p j f", j=2)[:, :, half], ACT.Identity)
                        if s == 0:
                            ins.then_inc(act_done.sem, act_done.tick())
                    ins.then_inc(bank_free.sem, bank_free.tick(("e_kv", p)))
                    act.wait_ge(bank_full.sem, bank_free.now(1))
                    nc.scalar.activation(chunks(A_)[:, p, :], filled()[:, :], ACT.Identity).then_inc(
                            bank_free.sem, bank_free.tick(("e_out", p, 0)))
                    act.wait_ge(bank_full.sem, bank_free.now(1))
                    src = filled()
                    ev_free(p % 2, ("e_att", p))
                    nc.scalar.activation(EV[:, p % 2, :], src[:, :], ACT.Identity).then_inc(
                            bank_free.sem, bank_free.tick(("e_out", p, 1)))
                residual("proj2", bias_of("L2_mix_b_proj"))

            def rgcn_layer(tag, layer):
                put_tok = tokens(T_)
                for m in range(KC):
                    act.wait_ge(bank_full.sem, bank_free.now(1))
                    nc.scalar.activation(put_tok[:, :, m * P:(m + 1) * P], filled()[:, :].rearrange("p (t f) -> p t f", t=NT), ACT.Identity).then_inc(
                            bank_free.sem, bank_free.tick(((tag, "tok"), m)))
                for r in range(REL4):
                    linear((tag, "agg", r), KC, of(chunks((A_, B_, C_, D_)[r])))
                if layer is not None:
                    linear((tag, "out"), KC, of(chunks(T_)), ACT.Relu, lambda m: col("L2_gnn_b", layer * KC + m))

            linear("nodes0", KC, of(chunks(A_)), bias=bias_of("L0_gnn_bn"))
            linear("edge_part", KC, of(chunks(D_)))
            for done in spilled:
                act.wait_ge(done, 16)
            with loop(act, "gnn0", 3, (bank_free, act_done)) as layer:
                to_tokens("tok0", tokens(B_))
                linear("agg0", KC, of(chunks(C_)))
                linear("h0", KC, of(chunks(B_)), bias=lambda m: col("L0_gnn_b1", layer * KC + m))
                norm("lnh", chunks(B_))
                for m in range(KC):
                    act.wait_ge(dve_done.sem, dve_done.at(("lnh", m)))
                    nc.scalar.activation(chunks(B_)[:, m, :], chunks(B_)[:, m, :], ACT.Relu, bias=col("L0_gnn_ln_b", layer * KC + m), scale=col("L0_gnn_ln_g", layer * KC + m)).then_inc(
                            act_done.sem, act_done.tick(("relu0", m)))
                linear("w2", KC, of(chunks(C_)), bias=lambda m: col("L0_gnn_b2", layer * KC + m))
            softmax_attention()
            performer96()
            experts_of_one("moe0", "ln1", ACT.Gelu, "L0_ffn_b1")
            norm("ln2", XN)
            performer64()
            act.wait_ge(dve_done.sem, dve_done.at("y_read"))
            rgat(RGAT1, XN)
            rgat(RGAT2, h96)
            norm("ln3", XN)
            linear("f1_up", MF // P, of(chunks(A_)), ACT.Gelu, bias_of("L1_ffn_in_bias"))
            residual("f1")
            norm("ln4", XN)
            elu_attention()
            with loop(act, "rgcn", 2, (bank_free, act_done)) as layer:
                rgcn_layer("rgcn", layer)
            rgcn_layer("rgcnb", None)
            residual("routb", lambda m: col("L2_gnn_b", 2 * KC + m))
            experts_of_one("moe2", "ln5", ACT.Silu, "L2_ffn_b1")

            def graph_attention():
                tag, heads, relations = GAT
                linear("ft", KC, of(chunks(B_)))
                to_tokens("ft_rows", tokens(A_))
                linear("res", KC, of(chunks(C_)))
                edge_logits(tag, heads, 0)

                def exps(h):
                    act.wait_ge(dve_done.sem, dve_done.at((tag, "neg_max", h)))
                    at = 128 * (h % 2) + 20
                    for t in range(NT):
                        w = scores[:, h % 3, t, :]
                        nc.scalar.activation(w, w, ACT.Exp, bias=stat[:, at + t:at + t + 1]).then_inc(
                            act_done.sem, act_done.tick((tag, "exp", h, 0, t)))

                def aggregated(h):
                    half = slice(64 * (h % 2), 64 * (h % 2) + 64)
                    act.wait_ge(bank_full.sem, bank_free.now(1))
                    nc.scalar.activation(chunks(D_)[half, h // 2, :], filled()[half, :], ACT.Identity).then_inc(
                        bank_free.sem, bank_free.tick((tag, "agg", h)))

                for h in range(2):
                    edge_scores(tag, heads, h, 0, h)
                exps(0)
                for h in range(heads):
                    if h + 2 < heads:
                        edge_scores(tag, heads, h + 2, 0, (h + 2) % 3)
                    if h + 1 < heads:
                        exps(h + 1)
                    for c in range(NT):
                        act.wait_ge(bank_full.sem, bank_free.now(1))
                        nc.scalar.activation(weights_g[h % 2][:, c, :], filled()[:, :], ACT.Identity).then_inc(
                            bank_free.sem, bank_free.tick((tag, "weights_t", h, 0, c)))
                    if h:
                        aggregated(h - 1)
                aggregated(heads - 1)

            def feature_mix():
                for j, (name, dst) in enumerate((("xq", A_), ("xk", B_))):
                    for m in range(KC):
                        act.wait_ge(bank_full.sem, bank_free.now(1))
                        nc.scalar.activation(chunks(dst)[:, m, :], filled()[:, :], ACT.Identity, accum_out=stat[:, 6 * j + m:6 * j + m + 1]).then_inc(
                                bank_free.sem, bank_free.tick((name, m)))
                act.wait_ge(dve_done.sem, dve_done.at(("gat_x", KC - 1)))
                linear("xv", KC, of(chunks(C_)))
                act.wait_ge(dve_done.sem, dve_done.at("x_squares"))
                nc.scalar.activation(stat[:, 24:36], stat[:, 12:24], ACT.Sqrt).then_inc(act_done.sem, act_done.tick("x_norms"))
                residual("proj3", bias_of("L3_mix_b_proj"))

            def experts():
                act.wait_ge(dve_done.sem, dve_done.at(("xy", KC - 1)))
                for s in range(XRING):
                    act.dma_start(x_ring[:, s, :], io["experts"][s]).then_inc(x_tile_in[s], 16)
                act.wait_ge(bank_full.sem, bank_free.now(1))
                src = filled()
                nc.scalar.activation(choose[:, 1, :], src[0:NE, :], ACT.Sigmoid)
                nc.scalar.activation(choose[:, 0, :], src[0:NE, :], ACT.Identity).then_inc(
                        bank_free.sem, bank_free.tick("x_logit"))
                for m in range(SHARED // P):
                    act.wait_ge(bank_full.sem, bank_free.now(1))
                    nc.scalar.activation(shared_hidden[:, m, :], filled()[:, :], ACT.Silu).then_inc(
                            bank_free.sem, bank_free.tick(("shared_gate", m)))
                    act.wait_ge(bank_full.sem, bank_free.now(1))
                    src = filled()
                    ev_free(m % 2, ("shared_hidden", m))
                    nc.scalar.activation(EV[:, m % 2, :], src[:, :], ACT.Identity).then_inc(
                            bank_free.sem, bank_free.tick(("shared_up", m)))
                residual("shared")
                to_tokens("x_rows", x_rows)
                for label, dst in (("slots", slot_of), ("score", score_of)):
                    act.wait_ge(bank_full.sem, bank_free.now(1))
                    nc.scalar.activation(dst[:, :, :], filled()[:, 0:NT * NE].rearrange("p (t e) -> p t e", t=NT), ACT.Identity).then_inc(
                            bank_free.sem, bank_free.tick(("x_" + label, 0)))
                for m in range(KC):
                    for half in range(2):
                        act.wait_ge(bank_full.sem, bank_free.now(1))
                        nc.scalar.activation(x_slots[:, m, half * 512:half * 512 + 512], filled()[:, :], ACT.Identity).then_inc(
                                bank_free.sem, bank_free.tick(("x_gather", m, half)))
                act.wait_ge(bank_full.sem, bank_free.now(1))
                nc.scalar.activation(slot_score[:, :], filled()[:, 0:NPAIR * NE], ACT.Identity).then_inc(
                        bank_free.sem, bank_free.tick("x_slot_score"))
                for p in range(NPAIR):
                    act.wait_ge(bank_full.sem, bank_free.now(1))
                    nc.scalar.activation(place_t[:, p, :], filled()[:, :], ACT.Identity).then_inc(
                            bank_free.sem, bank_free.tick(("x_place_t", p)))
                while bank_free.n % NB:
                    own = slice((bank_free.n % NB) * P, (bank_free.n % NB + 1) * P)
                    act.wait_ge(bank_full.sem, bank_free.now(1))
                    nc.scalar.activation(mean[:, own], filled()[:, 0:P], ACT.Identity).then_inc(bank_free.sem, bank_free.tick())
                for n in range(2):
                    ev_free(n, None)
                act.wait_ge(bank_free.sem, bank_free.at("x_slot_score"))
                with loop(act, "pairs", NPAIR, (bank_free, act_done)) as pair:

                    for b in range(FB):
                        act.wait_ge(bank_full.sem, bank_free.now(1))
                        nc.scalar.activation(x_hidden[:, b, :], filled()[:, :], ACT.Silu).then_inc(
                            bank_free.sem, bank_free.tick(("x_gate", b)))
                        act.wait_ge(bank_full.sem, bank_free.now(1))
                        src = filled()
                        if b >= 2:
                            act.wait_ge(dve_done.sem, dve_done.at(("x_h", b - 2)))
                        nc.scalar.activation(EV[:, b % 2, :], src[:, :], ACT.Identity).then_inc(
                            bank_free.sem, bank_free.tick(("x_up", b)))
                    for b in range(FB):
                        act.wait_ge(bank_full.sem, bank_free.now(1))
                        nc.scalar.activation(x_hidden_t[:, 4 * b:4 * b + 4, :], filled()[:, :].rearrange("p (c s) -> p c s", c=4),
                                             ACT.Identity).then_inc(bank_free.sem, bank_free.tick(("x_h_t", b)))
                    for half in range(2):
                        act.wait_ge(bank_full.sem, bank_free.now(1))
                        src = filled()
                        for e in range(2):
                            rows = slice(CAP * e, CAP * e + CAP)
                            ins = nc.scalar.activation(
                                x_out[rows, bass.ds(pair, 1), half * (D // 2):(half + 1) * (D // 2)].rearrange("p a f -> p (a f)"),
                                src[rows, 0:D // 2], ACT.Identity, scale=slot_score[rows, bass.ds(pair * (NE + 2) + e, 1)])
                        ins.then_inc(bank_free.sem, bank_free.tick(("x_down", half)))
                residual("experts")

            norm("ln6", XN)
            graph_attention()
            feature_mix()
            norm("ln7", XN)
            experts()

        @block.vector
        def _(dve):
            v = nc.vector

            def norm(label, src, dst, ready=None):
                dve.wait_ge(bank_free.sem, bank_free.at((label, "sum")))
                for k in range(KC):
                    v.tensor_tensor(dst[:, k, :], src[:, k, :], mean[:, :], ALU.subtract).then_inc(
                            dve_done.sem, dve_done.tick((label, "d", k)))
                dve.wait_ge(bank_free.sem, bank_free.at((label, "var")))
                v.reciprocal(rstd[:, :], rstd[:, :]).then_inc(dve_done.sem, dve_done.tick())
                dve.wait_ge(dve_done.sem, dve_done.now())
                for k in range(KC):
                    v.tensor_tensor(dst[:, k, :], dst[:, k, :], rstd[:, :], ALU.mult).then_inc(
                            dve_done.sem, dve_done.tick((label, k)))

            def residual(label, full=None):
                for m in range(KC):
                    dve.wait_ge(bank_free.sem, bank_free.at((full or label, m)))
                    v.tensor_tensor(XT[:, m, :], XT[:, m, :], EV[:, m % 2, :], ALU.add).then_inc(
                            dve_done.sem, dve_done.tick((label + "_x", m)))

            dve.wait_ge(x_in, 16)
            norm("ln0", XT, XN)
            dve.wait_ge(edge_in, 64)
            dve.wait_ge(pool_done.sem, pool_done.at("consts"))
            v.tensor_copy(iota_f, iota_i).then_inc(dve_done.sem, dve_done.tick())
            v.tensor_copy(slot_iota[:, :], iota_i[:, 0:CAP]).then_inc(dve_done.sem, dve_done.tick())
            v.tensor_copy(edge_f[:, 0:2, :], edge_i[:, 0:2, :]).then_inc(dve_done.sem, dve_done.tick())
            for p, (first, second) in enumerate(PACKED):
                kinds = edge_i[:, 3 if p < 2 else 2, :]
                v.tensor_scalar(edge_f[:, 2 + p, :], kinds, float(second), float(PACK), ALU.is_equal, ALU.mult).then_inc(
                    dve_done.sem, dve_done.tick())
                v.tensor_scalar(edge_f[:, 5, :], kinds, float(first), None, ALU.is_equal).then_inc(dve_done.sem, dve_done.tick())
                dve.wait_ge(dve_done.sem, dve_done.now())
                v.tensor_tensor(edge_f[:, 2 + p, :], edge_f[:, 2 + p, :], edge_f[:, 5, :], ALU.add).then_inc(
                    dve_done.sem, dve_done.tick())
                dve.wait_ge(dve_done.sem, dve_done.now())

            def key(n, c):
                if isinstance(c, int):
                    return edge_f[:, n, c:c + 1]
                return edge_f[:, n, bass.ds(c, 1)]

            def feature_rows(c, b):
                return v.tensor_scalar(onehot32[:, b, :], iota_f, key(1, c), None, ALU.is_equal)

            for b in range(4):
                feature_rows(b, b).then_inc(onehot_ready, 1)
            with dve.Fori(1, EC // 4) as i:
                for b in range(4):
                    dve.wait_ge(onehot_used, i * 4 + (b - 3))
                    feature_rows(i * 4 + b, b).then_inc(onehot_ready, 1)

            for p in range(len(PACKED)):
                before = EC * (p + 1)
                a, b_ = (0, 1) if p < 2 else (1, 0)
                with dve.Fori(0, EC // 4) as i:
                    for b in range(4):
                        dve.wait_ge(onehot_used, i * 4 + (before + b - 3))
                        v.tensor_scalar(onehot_a[:, b, :], iota_f, key(a, i * 4 + b), None, ALU.is_equal)
                        v.tensor_scalar(onehot_b[:, b, :], iota_f, key(b_, i * 4 + b), key(2 + p, i * 4 + b),
                                        ALU.is_equal, ALU.mult).then_inc(onehot_ready, 1)
            for r in range(REL4):
                dve.wait_ge(bank_free.sem, bank_free.at(("degree", r)))
                if r == 0:
                    v.tensor_copy(EV[:, 1, :], degree[r]).then_inc(dve_done.sem, dve_done.tick())
                else:
                    v.tensor_tensor(EV[:, 1, :], EV[:, 1, :], degree[r], ALU.add).then_inc(dve_done.sem, dve_done.tick())
                dve.wait_ge(dve_done.sem, dve_done.now())
                v.tensor_scalar(degree[r], degree[r], 1.0, None, ALU.max).then_inc(dve_done.sem, dve_done.tick())
                dve.wait_ge(dve_done.sem, dve_done.now())
                v.reciprocal(degree[r], degree[r]).then_inc(dve_done.sem, dve_done.tick())
                dve.wait_ge(dve_done.sem, dve_done.now())
                v.tensor_tensor(fresh[r], fresh[r], degree[r].rearrange("p (a n) -> p a n", a=1).to_broadcast([P, NT, N]), ALU.mult).then_inc(
                    dve_done.sem, dve_done.tick(("norm", r)))
            dve.wait_ge(dve_done.sem, dve_done.now())
            dve.wait_ge(bank_free.sem, bank_free.at(("count_t", NT - 1)))
            for c in range(NT):
                own = slice(c * P, (c + 1) * P)
                v.tensor_tensor(EV[:, 0, own], ident[:, :], EV[:, 1, own], ALU.mult).then_inc(dve_done.sem, dve_done.tick())
            dve.wait_ge(dve_done.sem, dve_done.now())
            for c in range(NT):
                own = slice(c * P, (c + 1) * P)
                v.tensor_tensor(cnt[3][:, c, own], cnt[3][:, c, own], EV[:, 0, own], ALU.add).then_inc(
                        dve_done.sem, dve_done.tick("counts_looped"))
            dve.wait_ge(dve_done.sem, dve_done.now())
            dve.wait_ge(cols_in, 16)

            def softmax_attention():
                s = float(D8) ** -0.5
                for h in range(H8):
                    for t in range(NT):
                        dve.wait_ge(bank_full.sem, bank_full.at(("scores", h, t)))
                        j = bank_full.at(("scores", h, t)) - 1
                        v.reduce_max(stat[:, t:t + 1], bank[j % NB][:, :], axis=AX.X).then_inc(dve_done.sem, dve_done.tick())
                        dve.wait_ge(dve_done.sem, dve_done.now())
                        v.tensor_scalar(stat[:, 4 + t:5 + t], stat[:, t:t + 1], -s, None, ALU.mult).then_inc(
                                dve_done.sem, dve_done.tick(("neg_max", h, t)))
                    for t in range(NT):
                        dve.wait_ge(bank_free.sem, bank_free.at(("exp", h, t)))
                    v.reciprocal(stat[:, 12:16], stat[:, 8:12]).then_inc(dve_done.sem, dve_done.tick())
                    dve.wait_ge(dve_done.sem, dve_done.now())
                    for t in range(NT):
                        v.tensor_scalar(probs[:, t, :], probs[:, t, :], stat[:, 12 + t:13 + t], None, ALU.mult).then_inc(
                                dve_done.sem, dve_done.tick(("probs", h)))
                for m in range(KC):
                    dve.wait_ge(bank_free.sem, bank_free.at(("wo", m)))
                    v.tensor_tensor(EV[:, m % 2, :], EV[:, m % 2, :], chunks(A_)[:, m, :], ALU.add).then_inc(
                            dve_done.sem, dve_done.tick())
                    dve.wait_ge(dve_done.sem, dve_done.now())
                    v.tensor_tensor(XT[:, m, :], XT[:, m, :], EV[:, m % 2, :], ALU.add).then_inc(
                            dve_done.sem, dve_done.tick(("wo_x", m)))

            def divide(out, den, label):
                dve.wait_ge(dve_done.sem, dve_done.now())
                v.reciprocal(den, den).then_inc(dve_done.sem, dve_done.tick())
                dve.wait_ge(dve_done.sem, dve_done.now())
                v.tensor_tensor(out, out, den, ALU.mult).then_inc(dve_done.sem, dve_done.tick(label))

            def performer96():
                for h in range(H8):
                    dve.wait_ge(bank_free.sem, bank_free.at(("m_out", h, 1)))
                    v.tensor_scalar(EV[0:D8, h % 2, :], EV[0:D8, h % 2, :], 1e-6, None, ALU.max).then_inc(
                            dve_done.sem, dve_done.tick())
                    divide(att96[:, h, :], EV[0:D8, h % 2, :], ("m_att", h))
                residual("proj0")

            def experts_of_one(tag, ln):
                norm(ln, XT, XN)
                dve.wait_ge(bank_free.sem, bank_free.at((tag, "logit")))
                top, total = stat[:, 0:NT], stat[:, 8:8 + NT]
                wide = lambda x: x.rearrange("p (t a) -> p t a", a=1).to_broadcast([P, NT, ME])
                v.reduce_max(top, logit[:, :, :], axis=AX.X).then_inc(dve_done.sem, dve_done.tick())
                dve.wait_ge(dve_done.sem, dve_done.now())
                v.tensor_tensor(gate_exp[:, :, :], logit[:, :, :], wide(top), ALU.subtract).then_inc(
                        dve_done.sem, dve_done.tick())
                dve.wait_ge(dve_done.sem, dve_done.now())
                v.tensor_scalar(comb[:, :, :], gate_exp[:, :, :], 0.0, None, ALU.is_equal).then_inc(
                        dve_done.sem, dve_done.tick((tag, "shifted")))
                dve.wait_ge(dve_done.sem, dve_done.now())
                for t in range(NT):
                    v.tensor_tensor(comb[:, t, :], comb[:, t, :], down8[:, :], ALU.mult).then_inc(dve_done.sem, dve_done.tick())
                dve.wait_ge(dve_done.sem, dve_done.now())
                v.reduce_max(top, comb[:, :, :], axis=AX.X).then_inc(dve_done.sem, dve_done.tick())
                dve.wait_ge(dve_done.sem, dve_done.now())
                v.tensor_tensor(comb[:, :, :], comb[:, :, :], wide(top), ALU.is_equal).then_inc(dve_done.sem, dve_done.tick())
                dve.wait_ge(act_done.sem, act_done.at((tag, "exp")))
                v.reduce_sum(total, gate_exp[:, :, :], axis=AX.X).then_inc(dve_done.sem, dve_done.tick())
                dve.wait_ge(dve_done.sem, dve_done.now())
                v.reciprocal(total, total).then_inc(dve_done.sem, dve_done.tick())
                dve.wait_ge(dve_done.sem, dve_done.now())
                v.tensor_tensor(comb[:, :, :], comb[:, :, :], wide(total), ALU.mult).then_inc(
                        dve_done.sem, dve_done.tick((tag, "comb")))
                for e in range(ME):
                    dve.wait_ge(bank_free.sem, bank_free.at((tag, "scale", e)))
                for m in range(ME * MF // P):
                    dve.wait_ge(bank_free.sem, bank_free.at(((tag, "up0"), m) if m < KC else ((tag, "up1"), m - KC)))
                    v.tensor_tensor(hidden[:, m, :], hidden[:, m, :], scale_row[:, m * P // MF, :], ALU.mult).then_inc(
                            dve_done.sem, dve_done.tick(((tag, "hidden"), m)))
                residual(tag)

            def performer64():
                for p in range(KC):
                    dve.wait_ge(bank_free.sem, bank_free.at(("n_out", p, 1, 1)))
                    v.tensor_scalar(EV[:, p % 2, :], EV[:, p % 2, :], 1e-6, None, ALU.add).then_inc(dve_done.sem, dve_done.tick())
                    divide(chunks(A_)[:, p, :], EV[:, p % 2, :], ("n_att", p))
                Y = chunks(C_)
                for m in range(KC):
                    dve.wait_ge(bank_free.sem, bank_free.at(("proj1", m)))
                    v.tensor_tensor(Y[:, m, :], Y[:, m, :], XN[:, m, :], ALU.add).then_inc(dve_done.sem, dve_done.tick(("y", m)))
                norm("lny", Y, Y)
                dve.wait_ge(dve_done.sem, dve_done.now())
                for m in range(KC):
                    v.scalar_tensor_tensor(XT[:, m, :], Y[:, m, :], col("L1_mix_gamma", m), XT[:, m, :], ALU.mult, ALU.add).then_inc(
                            dve_done.sem, dve_done.tick("y_read"))
                dve.wait_ge(dve_done.sem, dve_done.now())
                for m in range(KC):
                    v.tensor_scalar(XT[:, m, :], XT[:, m, :], col("L1_mix_beta", m), None, ALU.add).then_inc(
                            dve_done.sem, dve_done.tick())

            def edge_max(tag, h, relations, buf, at):
                top = stat[:, at:at + 3 * NT].rearrange("p (t r) -> p t r", t=NT)
                for r in range(relations):
                    dve.wait_ge(bank_free.sem, bank_free.at((tag, "row", h, r)))
                    wide = scores[:, buf + r, :, :]
                    v.scalar_tensor_tensor(wide, wide, 0.2, wide, ALU.mult, ALU.max).then_inc(dve_done.sem, dve_done.tick())
                    dve.wait_ge(dve_done.sem, dve_done.now())
                    for t in range(NT):
                        s = scores[:, buf + r, t, :]
                        v.tensor_tensor_reduce(out=s, in0=s, in1=mask[r][:, t, :], scale=1.0, scalar=-3e38,
                                                    op0=ALU.add, op1=ALU.max, accum_out=top[:, t, r:r + 1]).then_inc(
                                                            dve_done.sem, dve_done.tick())
                dve.wait_ge(dve_done.sem, dve_done.now())
                v.reduce_max(stat[:, at + 16:at + 16 + NT], top[:, :, 0:relations], axis=AX.X).then_inc(
                        dve_done.sem, dve_done.tick())
                dve.wait_ge(dve_done.sem, dve_done.now())
                v.tensor_scalar(stat[:, at + 20:at + 20 + NT], stat[:, at + 16:at + 16 + NT], -1.0, None, ALU.mult).then_inc(
                        dve_done.sem, dve_done.tick((tag, "neg_max", h)))

            def edge_weights(tag, h, relations, buf, counts, eps_add, at):
                z = stat[:, at + 24:at + 24 + 3 * NT].rearrange("p (t r) -> p t r", t=NT)
                total, inverse = stat[:, at + 36:at + 36 + NT], stat[:, at + 40:at + 40 + NT]
                for r in range(relations):
                    for t in range(NT):
                        dve.wait_ge(act_done.sem, act_done.at((tag, "exp", h, r, t)))
                        s = scores[:, buf + r, t, :]
                        v.tensor_tensor_reduce(out=s, in0=s, in1=counts[r][:, t, :], scale=1.0, scalar=0.0,
                                                    op0=ALU.mult, op1=ALU.add, accum_out=z[:, t, r:r + 1]).then_inc(
                                                            dve_done.sem, dve_done.tick())
                dve.wait_ge(dve_done.sem, dve_done.now())
                v.reduce_sum(total, z[:, :, 0:relations], axis=AX.X).then_inc(dve_done.sem, dve_done.tick())
                dve.wait_ge(dve_done.sem, dve_done.now())
                op, by = (ALU.add, 1e-16) if eps_add else (ALU.max, 1e-30)
                v.tensor_scalar(total, total, by, None, op).then_inc(dve_done.sem, dve_done.tick())
                dve.wait_ge(dve_done.sem, dve_done.now())
                v.reciprocal(inverse, total).then_inc(dve_done.sem, dve_done.tick())
                dve.wait_ge(dve_done.sem, dve_done.now())
                if h >= 2:
                    dve.wait_ge(bank_free.sem, bank_free.at((tag, "weights_t", h - 2, relations - 1, NT - 1)))
                for t in range(NT):
                    v.tensor_scalar(diag[h % 2][:, t, :], ident[:, :], inverse[:, t:t + 1], None, ALU.mult).then_inc(
                        dve_done.sem, dve_done.tick((tag, "diag", h)))

            def no_edge(r):
                v.tensor_scalar(mask[r], cnt[r], 0.0, -BIG, ALU.is_equal, ALU.mult).then_inc(dve_done.sem, dve_done.tick())

            def rgat(which):
                tag, heads, relations = which

                def elu_end(h):
                    for j in range(2):
                        x = h96[:, 2 * h + j, :]
                        dve.wait_ge(act_done.sem, act_done.at((tag, "elu_exp", 2 * h + j)))
                        v.tensor_scalar(EV[0:D8, j, :], EV[0:D8, j, :], -1.0, None, ALU.add).then_inc(
                                dve_done.sem, dve_done.tick())
                        dve.wait_ge(dve_done.sem, dve_done.now())
                        v.scalar_tensor_tensor(x, x, 0.0, EV[0:D8, j, :], ALU.max, ALU.add).then_inc(
                            dve_done.sem, dve_done.tick(((tag, "elu"), 2 * h + j)))

                edge_max(tag, 0, relations, 0, 0)
                for h in range(heads):
                    edge_weights(tag, h, relations, 0, cnt, True, 0)
                    if tag == "rgat1" and h:
                        elu_end(h - 1)
                    if h + 1 < heads:
                        edge_max(tag, h + 1, relations, 0, 0)
                    if tag == "rgat1":
                        dve.wait_ge(act_done.sem, act_done.at((tag, "out", h)))
                        dve.wait_ge(dve_done.sem, dve_done.now())
                        for j in range(2):
                            v.tensor_scalar(EV[0:D8, j, :], h96[:, 2 * h + j, :], 0.0, None, ALU.min).then_inc(
                                dve_done.sem, dve_done.tick((tag, "low", 2 * h + j)))
                if tag == "rgat1":
                    elu_end(heads - 1)

            def elu_attention():
                for p in range(KC):
                    for j, name in enumerate(("eq", "ek")):
                        dve.wait_ge(bank_free.sem, bank_free.at(((name, p), 0)))
                        v.tensor_scalar(qk[:, 2 + j, :], qk[:, j, :], 0.0, None, ALU.min).then_inc(
                                dve_done.sem, dve_done.tick(("e_low", p, j)))
                    for j in range(2):
                        dve.wait_ge(act_done.sem, act_done.at(("e_exp", p, j)))
                        v.scalar_tensor_tensor(qk[:, j, :], qk[:, j, :], 0.0, qk[:, 2 + j, :], ALU.max, ALU.add).then_inc(
                                dve_done.sem, dve_done.tick(("e_q" if j == 0 else "e_k", p)))
                    dve.wait_ge(bank_free.sem, bank_free.at(("e_out", p, 1)))
                    divide(chunks(A_)[:, p, :], EV[:, p % 2, :], ("e_att", p))
                residual("proj2")

            for j, name in enumerate(("L0_mix_bq", "L0_mix_bk")):
                at = cols_at[name]
                v.tensor_scalar(stat[0:D8, 32 + 8 * j:40 + 8 * j], cols[0:D8, at:at + H8], float(D8) ** -0.5, None, ALU.mult).then_inc(
                        dve_done.sem, dve_done.tick("scaled_bias"))
            for m in range(KC):
                dve.wait_ge(bank_free.sem, bank_free.at(("edge_part", m)))
                v.scalar_tensor_tensor(chunks(D_)[:, m, :], EV[:, 1, :], col("L0_gnn_be", m), chunks(D_)[:, m, :],
                                            ALU.mult, ALU.add).then_inc(dve_done.sem, dve_done.tick())
            dve.wait_ge(dve_done.sem, dve_done.now())
            with loop(dve, "gnn0", 3, (dve_done,)):
                for m in range(KC):
                    dve.wait_ge(bank_free.sem, bank_free.at(("agg0", m)))
                    v.tensor_tensor(chunks(C_)[:, m, :], chunks(C_)[:, m, :], chunks(D_)[:, m, :], ALU.add).then_inc(
                            dve_done.sem, dve_done.tick(("agg0_sum", m)))
                norm("lnh", chunks(B_), chunks(B_))
                for m in range(KC):
                    dve.wait_ge(bank_free.sem, bank_free.at(("w2", m)))
                    v.tensor_tensor(chunks(A_)[:, m, :], chunks(A_)[:, m, :], chunks(C_)[:, m, :], ALU.add).then_inc(
                            dve_done.sem, dve_done.tick(("nodes", m)))
            softmax_attention()
            performer96()
            experts_of_one("moe0", "ln1")
            norm("ln2", XT, XN)
            performer64()
            dve.wait_ge(pool_done.sem, pool_done.at("counts"))
            for r in range(REL3):
                no_edge(r)
            dve.wait_ge(dve_done.sem, dve_done.now())
            rgat(RGAT1)
            rgat(RGAT2)
            for m in range(KC):
                dve.wait_ge(bank_free.sem, bank_free.at(("rgat2", "out", m)))
                v.tensor_tensor(XT[:, m, :], XT[:, m, :], EV[:, m % 2, :], ALU.add).then_inc(
                        dve_done.sem, dve_done.tick(("rgat2_x", m)))
            v.tensor_copy(stat[:, 0:1], stat[:, 1:2]).then_inc(dve_done.sem, dve_done.tick("rgat2_last"))
            norm("ln3", XT, XN)
            residual("f1")
            norm("ln4", XT, XN)
            elu_attention()
            with loop(dve, "rgcn", 2, (dve_done,)):
                dve.wait_ge(bank_free.sem, bank_free.at((("rgcn", "out"), KC - 1)))
                for m in range(KC):
                    v.tensor_copy(XN[:, m, :], chunks(T_)[:, m, :]).then_inc(dve_done.sem, dve_done.tick((("rgcn", "x"), m)))
            residual("routb")
            experts_of_one("moe2", "ln5")
            def graph_attention():
                tag, heads, relations = GAT
                dve.wait_ge(reloaded[1], 16)
                no_edge(0)
                dve.wait_ge(dve_done.sem, dve_done.now())

                def joined(m):
                    x = chunks(D_)[:, m, :]
                    dve.wait_ge(bank_free.sem, bank_free.at((tag, "agg", 2 * m + 1)))
                    v.tensor_tensor(x, x, chunks(C_)[:, m, :], ALU.add).then_inc(dve_done.sem, dve_done.tick())
                    dve.wait_ge(dve_done.sem, dve_done.now())
                    v.scalar_tensor_tensor(XT[:, m, :], x, 0.0, XT[:, m, :], ALU.max, ALU.add).then_inc(
                        dve_done.sem, dve_done.tick(("gat_x", m)))

                edge_max(tag, 0, 1, 0, 0)
                for h in range(heads):
                    if h + 1 < heads:
                        edge_max(tag, h + 1, 1, (h + 1) % 3, 128 * ((h + 1) % 2))
                    edge_weights(tag, h, 1, h % 3, cnt, False, 128 * (h % 2))
                    if h % 2 and h > 2:
                        joined(h // 2 - 1)
                joined(KC - 1)

            def feature_mix():
                q, k, val, kk, y = chunks(A_), chunks(B_), chunks(C_), chunks(D_), chunks(T_)
                dve.wait_ge(dve_done.sem, dve_done.now())
                for j, (name, x, dst) in enumerate((("xq", q, y), ("xk", k, kk))):
                    for m in range(KC):
                        dve.wait_ge(bank_free.sem, bank_free.at((name, m)))
                        at = 12 + 6 * j + m
                        v.tensor_tensor_reduce(out=dst[:, m, :], in0=x[:, m, :], in1=x[:, m, :], scale=1.0, scalar=0.0,
                                                    op0=ALU.mult, op1=ALU.add, accum_out=stat[:, at:at + 1]).then_inc(
                                                            dve_done.sem, dve_done.tick("x_squares"))
                dve.wait_ge(dve_done.sem, dve_done.now())
                for m in range(KC):
                    v.tensor_tensor(q[:, m, :], q[:, m, :], kk[:, m, :], ALU.mult).then_inc(dve_done.sem, dve_done.tick())
                dve.wait_ge(act_done.sem, act_done.at("x_norms"))
                nq, nk, sums, both, coef = (stat[:, a:a + KC] for a in (24, 30, 36, 42, 48))
                v.tensor_tensor(sums, stat[:, 0:6], stat[:, 6:12], ALU.mult).then_inc(dve_done.sem, dve_done.tick())
                v.tensor_tensor(both, nq, nk, ALU.mult).then_inc(dve_done.sem, dve_done.tick())
                dve.wait_ge(dve_done.sem, dve_done.now())
                v.reciprocal(coef, both).then_inc(dve_done.sem, dve_done.tick())
                dve.wait_ge(dve_done.sem, dve_done.now())
                v.tensor_tensor(sums, sums, coef, ALU.mult).then_inc(dve_done.sem, dve_done.tick())
                dve.wait_ge(dve_done.sem, dve_done.now())
                v.tensor_scalar(sums, sums, float(N), None, ALU.add).then_inc(dve_done.sem, dve_done.tick())
                dve.wait_ge(dve_done.sem, dve_done.now())
                v.tensor_tensor(sums, sums, both, ALU.mult).then_inc(dve_done.sem, dve_done.tick())
                dve.wait_ge(dve_done.sem, dve_done.now())
                v.tensor_tensor(sums, sums, nk, ALU.mult).then_inc(dve_done.sem, dve_done.tick())
                dve.wait_ge(dve_done.sem, dve_done.now())
                v.reciprocal(coef, sums).then_inc(dve_done.sem, dve_done.tick())
                dve.wait_ge(dve_done.sem, dve_done.now())
                for m in range(KC):
                    dve.wait_ge(bank_free.sem, bank_free.at(("xv", m)))
                    v.scalar_tensor_tensor(y[:, m, :], val[:, m, :], coef[:, m:m + 1], q[:, m, :], ALU.mult, ALU.mult).then_inc(
                            dve_done.sem, dve_done.tick(("xy", m)))
                residual("proj3")

            def experts():
                logits, taken, ranks = choose[:, 0, :], choose[:, 2, :], choose[:, 3, :]
                dve.wait_ge(bank_free.sem, bank_free.at("x_logit"))
                v.tensor_scalar(logits, logits, 17.33, -103.97, ALU.min, ALU.max).then_inc(dve_done.sem, dve_done.tick())
                v.memset(ranks, 1.0).then_inc(dve_done.sem, dve_done.tick())
                dve.wait_ge(dve_done.sem, dve_done.now())
                for n in range(CAP // 8):
                    v.max(stat[0:NE, 0:8], logits).then_inc(dve_done.sem, dve_done.tick())
                    dve.wait_ge(dve_done.sem, dve_done.now())
                    v.match_replace(logits, stat[0:NE, 0:8], logits, -BIG).then_inc(dve_done.sem, dve_done.tick())
                    dve.wait_ge(dve_done.sem, dve_done.now())
                v.tensor_scalar(taken, logits, -BIG, None, ALU.is_equal).then_inc(dve_done.sem, dve_done.tick())
                dve.wait_ge(dve_done.sem, dve_done.now())
                v.tensor_tensor_scan(logits, ranks, taken, 0.0, ALU.mult, ALU.add).then_inc(dve_done.sem, dve_done.tick())
                dve.wait_ge(dve_done.sem, dve_done.now())
                v.tensor_tensor(taken, taken, logits, ALU.mult).then_inc(dve_done.sem, dve_done.tick())
                dve.wait_ge(dve_done.sem, dve_done.now())
                v.tensor_scalar(taken, taken, -1.0, None, ALU.add).then_inc(dve_done.sem, dve_done.tick("x_slots"))
                for m in range(SHARED // P):
                    dve.wait_ge(bank_free.sem, bank_free.at(("shared_up", m)))
                    v.tensor_tensor(shared_hidden[:, m, :], shared_hidden[:, m, :], EV[:, m % 2, :], ALU.mult).then_inc(
                            dve_done.sem, dve_done.tick(("shared_hidden", m)))
                residual("shared")
                dve.wait_ge(bank_free.sem, bank_free.at(("x_slots", 0)))
                for t in range(NT):
                    slots = place[:, t, :].rearrange("p (e s) -> p e s", e=NE)
                    v.tensor_tensor(slots, slot_iota[:, :].rearrange("p (a s) -> p a s", a=1).to_broadcast([P, NE, CAP]),
                                         slot_of[:, t, :].rearrange("p (e a) -> p e a", a=1).to_broadcast([P, NE, CAP]), ALU.is_equal).then_inc(
                                                 dve_done.sem, dve_done.tick("x_place"))
                dve.wait_ge(bank_free.sem, bank_free.at(("x_gather", KC - 1, 1)))
                with loop(dve, "pairs", NPAIR, (dve_done,)) as pair:
                    dve.wait_ge(bank_full.sem, bank_full.at(("x_up", FB - 1), 1))
                    v.tensor_copy(x_pair, x_slots[:, :, bass.ds(pair * P, P)]).then_inc(dve_done.sem, dve_done.tick("x_pair"))
                    for b in range(FB):
                        dve.wait_ge(bank_free.sem, bank_free.at(("x_up", b)))
                        v.tensor_tensor(x_hidden[:, b, :], x_hidden[:, b, :], EV[:, b % 2, :], ALU.mult).then_inc(
                            dve_done.sem, dve_done.tick(("x_h", b)))
                residual("experts")

            norm("ln6", XT, XN)
            graph_attention()
            feature_mix()
            norm("ln7", XT, XN)
            experts()
            dve.wait_ge(dve_done.sem, dve_done.now())
            v.tensor_copy(stat[:, 0:1], stat[:, 0:1]).then_inc(dve_done.sem, dve_done.tick("result"))



def by_chunk(a, width=P):
    k, n = a.shape
    out = np.zeros((P, k // width, n), np.float32)
    out[:width] = a.reshape(k // width, width, n).transpose(1, 0, 2)
    return out


def weight_tiles(w, width_out=P, rows=P, rest=None):
    k, n = w.shape
    blocks = k // rows
    per = H8 if rows == D8 else min(KC, blocks)
    v = by_chunk(w, rows).reshape(P, blocks // per, per, n // width_out, width_out).transpose(3, 1, 0, 2, 4)
    out = np.zeros((n // width_out, blocks // per, P, SLOT), np.float32)
    out[..., :per * width_out] = v.reshape(n // width_out, blocks // per, P, per * width_out)
    if rest is not None:
        r = rest.reshape(rest.shape[0], n // width_out, width_out).transpose(1, 0, 2)
        out[:, -1, :rest.shape[0], KC * P:KC * P + width_out] = r
    return out.reshape(-1, P, SLOT)


def interleave(parts):
    per = [p.reshape(KC, -1, P, SLOT) for p in parts]
    return np.concatenate(per, axis=1).reshape(-1, P, SLOT)


def weight_stream(a):
    out = []
    out.append(weight_tiles(a["L0_gnn_Wn"].T))
    out.append(weight_tiles(a["L0_gnn_We"].T))
    for l in range(3):
        out.append(weight_tiles(a["L0_gnn_W1"][l].T))
        out.append(weight_tiles(a["L0_gnn_W2"][l].T))
    qkv = a["L0_gnn_Wqkv"].T
    out.append(weight_tiles(qkv[:, 2 * D:]))
    q, k = weight_tiles(qkv[:, :D], D8), weight_tiles(qkv[:, D:2 * D], D8)
    out.append(np.stack([q, k], 1).reshape(-1, P, SLOT))
    out.append(weight_tiles(a["L0_gnn_Wo"].T, P, D8))
    qkv = a["L0_mix_qkv_w"].T
    out.append(weight_tiles(qkv[:, 2 * D:]))
    q, k = weight_tiles(qkv[:, :D], D8), weight_tiles(qkv[:, D:2 * D], D8)
    out.append(np.stack([q, k], 1).reshape(-1, P, SLOT))
    out.append(weight_tiles(a["L0_mix_proj_w"].T, P, D8))
    out += moe_tiles(a, "L0_ffn")
    qkv = a["L1_mix_W_qkv"]
    out.append(weight_tiles(qkv[:, 2 * D:]))
    q, k = weight_tiles(qkv[:, :D]), weight_tiles(qkv[:, D:2 * D])
    out.append(np.stack([q, k], 1).reshape(-1, P, SLOT))
    out.append(weight_tiles(a["L1_mix_W_proj"]))
    out += [weight_tiles(w) for w in a["L1_gnn_W1"]]
    out += [weight_tiles(w, P, D8) for w in a["L1_gnn_W2"]]
    out.append(weight_tiles(a["L1_ffn_in_weight"].T))
    out.append(weight_tiles(a["L1_ffn_out_weight"]))
    qkv = a["L2_mix_w_qkv"]
    out.append(weight_tiles(qkv[:, 2 * D:]))
    q, k = weight_tiles(qkv[:, :D]), weight_tiles(qkv[:, D:2 * D])
    out.append(np.stack([q, k], 1).reshape(-1, P, SLOT))
    out.append(weight_tiles(a["L2_mix_w_proj"]))
    for l in "123":
        out.append(interleave([weight_tiles(a["L2_gnn_root" + l])] + [weight_tiles(w) for w in a["L2_gnn_W" + l]]))
    out += moe_tiles(a, "L2_ffn")
    out += late_tiles(a)
    out = np.concatenate(out)
    pad = -len(out) % RING
    return np.concatenate([out, np.zeros((pad, P, SLOT), np.float32)]) if pad else out


def moe_tiles(a, name):
    up = a[name + "_W1"].transpose(1, 0, 2).reshape(D, ME * MF)
    return [weight_tiles(up), weight_tiles(a[name + "_W2"].reshape(ME * MF, D), rest=a[name + "_b2"])]


def late_tiles(a):
    out = []
    qkv = a["L3_mix_w_qkv"]
    out += [weight_tiles(qkv[:, n * D:(n + 1) * D]) for n in range(3)] + [weight_tiles(a["L3_mix_w_proj"])]
    gate, up = weight_tiles(a["L3_ffn_Ws_g"].T), weight_tiles(a["L3_ffn_Ws_u"].T)
    out += [np.stack([gate, up], 1).reshape(-1, P, SLOT), weight_tiles(a["L3_ffn_Ws_d"].T)]
    return out


def expert_tiles(a):
    flat = np.empty((NPAIR, 36, P, XSLOT), np.float32)
    up = flat[:, :24].reshape(NPAIR, FB, 2, 2, P, KC, 512)
    for n, name in enumerate(("L3_ffn_Wg", "L3_ffn_Wu")):
        w = a[name].reshape(NPAIR, 2, FB, 512, KC, P)
        up[:, :, n] = w.transpose(0, 2, 1, 5, 4, 3)
    w = a["L3_ffn_Wd"].reshape(NPAIR, 2, 2, D // 2, 3, 8, P)
    flat[:, 24:] = w.transpose(0, 2, 4, 1, 6, 5, 3).reshape(NPAIR, 12, P, XSLOT)
    return flat.reshape(-1, P, XSLOT)


def column_table(a):
    bq = a["L0_gnn_bqkv"].reshape(3, D)
    mq = a["L0_mix_qkv_b"].reshape(3, D)
    own = {"L0_gnn_bq": bq[0], "L0_gnn_bk": bq[1], "L0_gnn_bv": bq[2], "L0_mix_bq": mq[0], "L0_mix_bk": mq[1],
           "L0_mix_bv": mq[2], "L2_gnn_b": np.concatenate([a["L2_gnn_b" + l] for l in "123"])}
    starts, total = column_starts()
    out = np.zeros((P, total), np.float32)
    for name, n, width in COLS:
        x = (own[name] if name in own else a[name]).reshape(n // width, width)
        out[:width, starts[name]:starts[name] + n // width] = x.T
    return out


def two_heads(w):
    out = np.zeros((P, P), np.float32)
    out[:64, :64] = w
    out[64:, 64:] = w
    return out


def head_columns(v):
    out = np.zeros((D, 12), np.float32)
    for h in range(12):
        out[64 * h:64 * h + 64, h] = v[h]
    return by_chunk(out)


def kernel(**inputs):
    import concourse.bacc as bacc
    from concourse.bass_utils import run_bass_kernel_spmd

    a = {k: np.asarray(v) for k, v in inputs.items()}
    rf1 = np.zeros((P, 2, M_RF), np.float32)
    rf1[:64, 0] = a["L1_mix_random_features"].T
    rf1[64:, 1] = a["L1_mix_random_features"].T
    edges = np.stack([a[k].reshape(EC, P).T for k in ("src", "dst", "edge_type_3", "edge_type_4")])
    arrays = {
        "xT": by_chunk(a["x"].T), "cols": column_table(a), "weights": weight_stream(a), "edges": edges,
        "feats": a["edge_attr_256"].reshape(EC, P, 256).transpose(1, 0, 2),
        "L0_Ws": by_chunk(a["L0_ffn_Ws"]), "L0_bs": a["L0_ffn_bs"].reshape(1, ME), "L2_Ws": by_chunk(a["L2_ffn_Wg"]),
        "L3_gate": by_chunk(a["L3_ffn_gate_weight"].T), "rf0": a["L0_mix_rf"].T, "rf1": rf1,
        "q1": by_chunk(a["L1_gnn_q1"]), "k1": by_chunk(a["L1_gnn_k1"]), "q2": by_chunk(a["L1_gnn_q2"]),
        "k2": by_chunk(a["L1_gnn_k2"]), "fc": two_heads(a["L3_gnn_W_fc"].T), "res": two_heads(a["L3_gnn_W_res"].T),
        "attn_l": head_columns(a["L3_gnn_attn_l"]), "attn_r": head_columns(a["L3_gnn_attn_r"]),
        **late_arrays(a),
    }
    arrays = {k: np.ascontiguousarray(v) for k, v in arrays.items()}
    tables = {}
    for _ in range(2):
        nc = bacc.Bacc("TRN2", target_bir_lowering=False, num_devices=1)
        io = {k: nc.dram_tensor("in_" + k, v.shape, mybir.dt.from_np(v.dtype), kind="ExternalInput").ap()
              for k, v in arrays.items()}
        io["scratch"] = nc.dram_tensor("scratch", (REL4 + 1, P, NT, N), mybir.dt.float32, kind="Internal").ap()
        io["out"] = nc.dram_tensor("out", (P, KC, N), mybir.dt.float32, kind="ExternalOutput").ap()
        program(nc, io, tables)
    r = run_bass_kernel_spmd(nc, [{"in_" + k: v for k, v in arrays.items()}], core_ids=[0])
    return r.results[0]["out"].transpose(2, 1, 0).reshape(N, D)


def late_arrays(a):
    return {"experts": expert_tiles(a)}
```

```python
import numpy as np
import concourse.bass as bass
from concourse import mybir
from contextlib import ExitStack, contextmanager


N, D, P = 512, 768, 128
E, EC = 8704, 8704 // 128
KC, NT = D // P, N // P
H8, D8 = 8, 96
M_RF = 256
SLOT, RING = 1024, 6
NB = 4
ME, MF = 8, 384
LEAD = 2
NE, CAP, FX = 16, 64, 3072
NPAIR = NE // 2
FB, FC = FX // 512, FX // P
XSLOT, XRING = KC * 512, 6
SHARED = 1536
REL3, REL4 = 3, 4
BIG = 1e30
PACK, GROUPS = 4096, [(0, 24), (24, 48), (48, EC)]
FEAT_PARTS = [(0, 16), (16, 32), (32, 48), (48, EC)]
PACKED = [(0, 1), (2, 3), (0, 1)]
SHIFT = 24 * P // 2
ROUND = 1.5 * 2 ** 23

COLS = [("L0_gnn_bn", D, P), ("L0_gnn_be", D, P), ("L0_gnn_b1", 3 * D, P), ("L0_gnn_ln_g", 3 * D, P),
        ("L0_gnn_ln_b", 3 * D, P), ("L0_gnn_b2", 3 * D, P), ("L0_gnn_bq", D, D8), ("L0_gnn_bk", D, D8),
        ("L0_gnn_bv", D, P), ("L0_gnn_bo", D, P), ("L0_mix_bq", D, D8), ("L0_mix_bk", D, D8),
        ("L0_mix_bv", D, P), ("L0_mix_proj_b", D, P), ("L0_ffn_b1", ME * MF, P), ("L1_gnn_b1", D, P),
        ("L1_gnn_b2", D, P), ("L1_mix_b_proj", D, P), ("L1_mix_gamma", D, P), ("L1_mix_beta", D, P),
        ("L1_ffn_in_bias", MF, P), ("L2_gnn_b", 3 * D, P), ("L2_mix_b_proj", D, P),
        ("L2_ffn_b1", ME * MF, P), ("L3_mix_b_proj", D, P)]

SMALL = [("L0_Ws", (P, KC, ME)), ("L0_bs", (1, ME)), ("L2_Ws", (P, KC, ME)), ("L3_gate", (P, KC, NE)),
         ("rf0", (D8, M_RF)), ("rf1", (P, 2, M_RF)), ("q1", (P, KC, 4)), ("k1", (P, KC, 4)),
         ("q2", (P, KC, 1)), ("k2", (P, KC, 1)), ("fc", (P, P)), ("res", (P, P)),
         ("attn_l", (P, KC, 12)), ("attn_r", (P, KC, 12))]


def column_starts():
    at, out = 0, {}
    for name, n, width in COLS:
        out[name] = at
        at += n // width
    return out, at


class Tally:
    around = None

    def __init__(self, sem, known):
        self.sem, self.known, self.found = sem, dict(known), known
        self.n, self.loop, self.final = 0, None, bool(known)

    def tick(self, label=None):
        self.n += 1
        if label is not None:
            self.found[label] = (self.n, self.loop[0] if self.loop else None)
        return 1

    def now(self, ahead=0):
        if not self.loop:
            return self.n + ahead
        name, it = self.loop
        return it * self.known.get(("step", name), 1) + (self.n + ahead)

    def at(self, label, back=0):
        n, name = self.known[label] if self.final else (1, None)
        if name is None:
            return n
        step, times = self.known[("step", name)], self.known[("times", name)]
        if Tally.around and Tally.around[0] == name:
            return Tally.around[1] * step + (n - back * step)
        return n + (times - 1) * step


def program(nc, io, tables):
    f32, bf16, i32 = mybir.dt.float32, mybir.dt.bfloat16, mybir.dt.int32
    ALU, ACT, AX = mybir.AluOpType, mybir.ActivationFunctionType, mybir.AxisListType
    ctx = ExitStack()
    with ctx:
        def sb(name, shape, dt=f32):
            return ctx.enter_context(nc.sbuf_tensor(name, list(shape), dt))

        def sem(name):
            return ctx.enter_context(nc.semaphore(name))

        KB = 256
        CNT, A_, B_, C_, D_, XN_, T_, QK_, PQ_, XT_, WR_, E_, F_, END = (
            0, 32, 44, 56, 68, 80, 92, 108, 116, 124, 136, 160, 172, 184)
        mem = sb("mem", [P, END * KB])

        def area(kb, a, b, c=None, rows=P):
            size = a * b * (c or 1)
            v = mem[0:rows, int(kb * KB):int(kb * KB) + size]
            if c is None:
                return v.rearrange("p (a b) -> p a b", a=a)
            return v.rearrange("p (a b c) -> p a b c", a=a, b=b)

        def chunks(kb, n=KC):
            return area(kb, n, N)

        def tokens(kb):
            return area(kb, NT, D)

        def heads96(kb):
            return area(kb, H8, N, rows=D8)

        cnt = [area(CNT + 8 * r, NT, N) for r in range(4)]
        XT, XN = chunks(XT_), chunks(XN_)
        ring = area(WR_, RING, SLOT)
        qk = [area(QK_, 4, N), area(T_, 4, N)]
        sq = chunks(T_)
        iota_f = area(QK_, 1, N)[:, 0, :]
        iota_i = area(QK_ + 2, 1, N)[:, 0, :].bitcast(i32)
        edge_i = area(QK_ + 4, 4, EC).bitcast(i32)
        edge_f = area(QK_ + 5.25, 6, EC)
        feats = area(CNT, EC, 256)
        onehot32 = area(E_, 4, N)
        onehot_a = area(F_, 4, N // 2).bitcast(bf16)
        onehot_b = area(F_ + 4, 4, N // 2).bitcast(bf16)
        edge_sum, edge_sum_t = area(PQ_, NT, 256), area(PQ_ + 4, 2, N)
        fresh = [area(B_, NT, N), area(B_ + 8, NT, N), area(B_ + 16, NT, N), area(T_ + 8, NT, N)]
        group_sum, group_high = area(T_, NT, N), area(E_, NT, N)
        probs, probs_t = area(T_, NT, N), area(T_ + 8, NT, N)
        att96 = heads96(C_)
        rgat1_out = chunks(D_)
        pq0, pk0, kv0 = area(PQ_, 2, N), area(PQ_ + 4, NT, M_RF), area(E_, 2, 2 * D8)
        pq1, pk1, kv1 = area(PQ_, 2, 2, N), area(E_, NT, M_RF), area(F_, 2, 2, 2 * P)
        ktok = area(E_, NT, P)
        scores = area(T_, 3, NT, N)
        weights_t = [area(84, NT, N), area(CNT + 24, NT, N), area(E_ + 12, NT, N)]
        weights_t3 = area(D_, 3, NT, N)
        krow = area(PQ_, 3, N, rows=12)
        mask = [area(E_ + 4 * r, NT, N // 2).bitcast(bf16) for r in range(3)]
        hidden = chunks(A_, 24)
        scale_row = chunks(T_, ME)
        comb_t = area(PQ_, 1, N, rows=ME)[:, 0, :]
        shared_hidden = chunks(T_, SHARED // P)
        weights_g = [area(CNT + 8, NT, N), area(CNT + 16, NT, N)]
        x_ring = area(0, XRING, XSLOT)
        place_t = area(72, NPAIR, N)
        x_rows = tokens(T_)
        x_hidden, x_hidden_t = area(WR_, FB, 512), area(WR_ + 12, FC, P)
        choose = area(PQ_, 4, N, rows=NE)
        x_pair = area(PQ_, KC, P)
        place = area(E_, NT, NE * CAP)
        x_out = area(F_ + 4, 1, D)[:, 0, :]

        cols_at, n_cols = column_starts()
        cols = sb("cols", [P, n_cols])
        small = {name: sb(name, shape) for name, shape in SMALL}
        ident, ones = sb("ident", [P, P]), sb("ones", [P, P])
        neg_half, neg_half_pair = sb("neg_half", [P, M_RF]), sb("neg_half_pair", [P, 2, M_RF])
        EV = sb("EV", [P, 2, N])
        mean, rstd = sb("mean", [P, N]), sb("rstd", [P, N])
        x_back = [mean[:, :], rstd[:, :]]
        diag = [buf[:, :].rearrange("p (t d) -> p t d", t=NT) for buf in (mean, rstd)]
        degree = [EV[:, 0, :], mean[:, :], rstd[:, :], area(F_, 1, N)[:, 0, :]]
        eps_col, shift_col, round_col, unround_col, warm_col = (
            sb(n, [P, 1]) for n in ("eps_col", "shift_col", "round_col", "unround_col", "warm_col"))
        one_row, shift_row = sb("one_row", [1, P], bf16), sb("shift_row", [1, N], bf16)
        down8 = sb("down8", [P, ME])
        stat = sb("stat", [P, 256])
        logit, comb, gate_exp = sb("logit", [P, NT, ME]), sb("comb", [P, NT, ME]), sb("gate_exp", [P, NT, ME])
        kv_diag = sb("kv_diag", [P, 2, P])
        slot_iota = sb("slot_iota", [P, CAP])
        slot_of, score_of = sb("slot_of", [P, NT, NE]), sb("score_of", [P, NT, NE])
        slot_score, pair_score = sb("slot_score", [P, NPAIR * NE]), sb("pair_score", [P, 1])

        bank = [ctx.enter_context(nc.psum_tensor(f"bank{i}", [P, 512], f32)) for i in range(8)]

        tally = {n: Tally(sem(n), tables.setdefault(n, {})) for n in
                 ("bank_full", "bank_free", "tile_free", "x_tile_free", "agg_done", "act_done", "dve_done", "pool_done")}
        bank_full, bank_free, tile_free, x_tile_free, agg_done, act_done, dve_done, pool_done = (tally[n] for n in tally)
        w_in = [sem(f"w_in{i}") for i in range(RING)]
        x_tile_in = [sem(f"x_tile_in{i}") for i in range(XRING)]
        x_in, cols_in, small_in, edge_in = sem("x_in"), sem("cols_in"), sem("small_in"), sem("edge_in")
        feat_in = [sem(f"feat_in{i}") for i in range(4)]
        onehot_ready, onehot_used = sem("onehot_ready"), sem("onehot_used")
        spilled = [sem(f"spilled{r}") for r in range(REL4 + 1)]
        reloaded, out_done = [sem("reloaded4"), sem("reloaded1")], sem("out_done")

        def col(name, i, rows=P):
            at = cols_at[name] + i
            if isinstance(i, int):
                return cols[0:rows, at:at + 1]
            return cols[0:rows, bass.ds(at, 1)]

        @contextmanager
        def loop(eng, name, times, mine):
            starts = [t.n for t in mine]
            with eng.Fori(0, times) as it:
                for t in mine:
                    t.loop = (name, it)
                Tally.around = (name, it)
                yield it
            for t, start in zip(mine, starts):
                step = t.n - start
                t.found[("step", name)], t.found[("times", name)] = step, times
                t.known[("step", name)], t.known[("times", name)] = step, times
                t.n, t.loop = start + times * step, None
            Tally.around = None

        HB = [(2 * m + s, slice(64 * s, 64 * s + 64), s) for m in range(KC) for s in range(2)]
        PIECES = [[(3 * h // 2, slice(0, P)), (3 * h // 2 + 1, slice(0, 64))] if h % 2 == 0 else
                  [(3 * h // 2, slice(64, P)), (3 * h // 2 + 1, slice(0, P))] for h in range(4)]
        RGAT1, RGAT2, GAT = ("rgat1", 4, 3), ("rgat2", 1, 3), ("gat", 12, 1)

        block = ctx.enter_context(nc.Block())

        @block.sync
        def _(sp):
            sp.dma_start(XT, io["xT"]).then_inc(x_in, 16)
            sp.dma_start(cols[:, :], io["cols"]).then_inc(cols_in, 16)
            for s in range(RING):
                sp.dma_start(ring[:, s, :], io["weights"][s]).then_inc(w_in[s], 16)
            with sp.Fori(0, io["weights"].shape[0] // RING - 1) as i:
                for s in range(RING):
                    sp.wait_ge(tile_free.sem, i * RING + (s + 1))
                    sp.dma_start(ring[:, s, :], io["weights"][bass.ds(i * RING + (RING + s), 1), :, :]
                                 .rearrange("a p n -> p (a n)")).then_inc(w_in[s], 16)
            with sp.Fori(1, io["experts"].shape[0] // XRING) as i:
                for s in range(XRING):
                    sp.wait_ge(x_tile_free.sem, i * XRING + (s + 1 - XRING))
                    sp.dma_start(x_ring[:, s, :], io["experts"][bass.ds(i * XRING + s, 1), :, :]
                                 .rearrange("a p n -> p (a n)")).then_inc(x_tile_in[s], 16)
            sp.wait_ge(dve_done.sem, dve_done.at("result"))
            sp.dma_start(io["out"], XT).then_inc(out_done, 16)
            sp.wait_ge(out_done, 16)

        @block.gpsimd
        def _(pool):
            nc.gpsimd.iota(iota_i, pattern=[[1, N]], base=0, channel_multiplier=0)
            nc.gpsimd.memset(ident[:, :], 0.0)
            nc.gpsimd.memset(neg_half[:, :], -0.5)
            nc.gpsimd.memset(neg_half_pair[:, :, :], 0.0)
            nc.gpsimd.memset(kv_diag[:, :, :], 0.0)
            nc.gpsimd.memset(eps_col[:, :], 1e-5)
            nc.gpsimd.memset(shift_col[:, :], float(SHIFT))
            nc.gpsimd.memset(round_col[:, :], ROUND)
            nc.gpsimd.memset(unround_col[:, :], -ROUND * PACK)
            nc.gpsimd.memset(one_row[:, :], 1.0)
            nc.gpsimd.memset(shift_row[:, :], -float(SHIFT))
            for e in range(ME):
                nc.gpsimd.memset(down8[:, e:e + 1], float(ME - e))
            nc.gpsimd.memset(ones[:, :], 1.0).then_inc(pool_done.sem, pool_done.tick("zeros"))
            pool.wait_ge(pool_done.sem, pool_done.at("zeros"))
            nc.gpsimd.affine_select(out=ident[:, :], in_=ident[:, :], compare_op=ALU.not_equal, fill=1.0,
                                                   base=0, pattern=[[-1, P]], channel_multiplier=1).then_inc(
                                                           pool_done.sem, pool_done.tick("ident"))
            pool.wait_ge(pool_done.sem, pool_done.at("ident"))
            nc.gpsimd.memset(neg_half_pair[0:64, 0, :], -0.5).then_inc(pool_done.sem, pool_done.tick("upper"))
            pool.wait_ge(pool_done.sem, pool_done.at("upper"))
            nc.gpsimd.memset(neg_half_pair[64:128, 1, :], -0.5).then_inc(pool_done.sem, pool_done.tick("consts"))
            for name, shape in SMALL:
                pool.dma_start(small[name][tuple(slice(None) for _ in shape)], io[name]).then_inc(small_in, 16)
            for p in range(len(PACKED)):
                low, high = (fresh[2 * p], fresh[2 * p + 1]) if p < 2 else (cnt[0], cnt[1])
                for g in range(len(GROUPS)):
                    n = len(GROUPS) * p + g
                    pool.wait_ge(act_done.sem, act_done.at(("high", n)))
                    if g == 0:
                        nc.gpsimd.tensor_tensor(low, group_sum, high, ALU.subtract).then_inc(
                            pool_done.sem, pool_done.tick(("unpacked", n)))
                        continue
                    nc.gpsimd.tensor_tensor(group_sum, group_sum, group_high, ALU.subtract).then_inc(
                        pool_done.sem, pool_done.tick(("low", n)))
                    pool.wait_ge(pool_done.sem, pool_done.at(("low", n)))
                    nc.gpsimd.tensor_tensor(low, low, group_sum, ALU.add).then_inc(pool_done.sem, pool_done.tick())
                    nc.gpsimd.tensor_tensor(high, high, group_high, ALU.add).then_inc(
                            pool_done.sem, pool_done.tick(("unpacked", n)))
                if p < 2:
                    pool.wait_ge(act_done.sem, act_done.at(("unweighted", p)))
                if p == 0:
                    nc.gpsimd.tensor_tensor(cnt[3], low, high, ALU.add).then_inc(pool_done.sem, pool_done.tick("count_half"))
                if p == 1:
                    nc.gpsimd.tensor_tensor(cnt[3], cnt[3], low, ALU.add).then_inc(pool_done.sem, pool_done.tick("count_most"))
                    pool.wait_ge(pool_done.sem, pool_done.at("count_most"))
                    nc.gpsimd.tensor_tensor(cnt[3], cnt[3], high, ALU.add).then_inc(pool_done.sem, pool_done.tick("count_all"))
            for r in range(REL4):
                pool.wait_ge(dve_done.sem, dve_done.at(("norm", r)))
                pool.dma_start(io["scratch"][r], fresh[r]).then_inc(spilled[r], 16)
            pool.wait_ge(bank_free.sem, bank_free.at(("count_t", NT - 1)))
            pool.dma_start(io["scratch"][REL4], cnt[2]).then_inc(spilled[REL4], 16)
            for done in spilled:
                pool.wait_ge(done, 16)
            pool.wait_ge(act_done.sem, act_done.at(("unweighted", 2)))
            nc.gpsimd.tensor_tensor(cnt[2], cnt[2], cnt[0], ALU.subtract).then_inc(pool_done.sem, pool_done.tick("count_rest"))
            pool.wait_ge(pool_done.sem, pool_done.at("count_rest"))
            nc.gpsimd.tensor_tensor(cnt[2], cnt[2], cnt[1], ALU.subtract).then_inc(pool_done.sem, pool_done.tick("counts"))
            pool.wait_ge(dve_done.sem, dve_done.at("rgat2_last"))
            for r in range(REL4):
                pool.dma_start(cnt[r], io["scratch"][r]).then_inc(reloaded[0], 16)
            pool.wait_ge(dve_done.sem, dve_done.at(("routb_x", KC - 1)))
            pool.dma_start(cnt[0], io["scratch"][REL4]).then_inc(reloaded[1], 16)

        @block.tensor
        def _(pe):
            state = {"tile": 0, "x_tile": 0, "pending": None}

            def mm(out, lhsT, rhs, start=True, stop=True, last=False, transpose=False):
                if transpose:
                    ins = nc.tensor.transpose(out, lhsT, ident[0:lhsT.shape[0], 0:lhsT.shape[0]])
                else:
                    ins = nc.tensor.matmul(out, lhsT, rhs, start=start, stop=stop)
                if state["pending"] and not last:
                    ins.then_inc(state["pending"].sem, state["pending"].tick())
                    state["pending"] = None
                return ins

            def open_bank():
                if bank_full.loop or bank_full.n >= NB:
                    pe.wait_ge(bank_free.sem, bank_full.now(1 - NB))
                return bank[bank_full.n % NB]

            def group(out, pairs, last=True):
                pairs = list(pairs)
                for n, (lhsT, rhs) in enumerate(pairs):
                    end = n == len(pairs) - 1
                    ins = mm(out, lhsT, rhs, n == 0, end, last and end)
                return ins

            def take_tile():
                t = state["tile"]
                value = 16 * (t // RING + 1)
                if tile_free.loop:
                    name, it = tile_free.loop
                    value = it * (16 * (tile_free.known.get(("step", name), RING) // RING)) + value
                pe.wait_ge(w_in[t % RING], value)
                state["tile"] += 1
                return t % RING

            def take_x_tile(it, per):
                t = state["x_tile"] % per
                pe.wait_ge(x_tile_in[t % XRING], it * (16 * per // XRING) + 16 * (t // XRING + 1))
                state["x_tile"] += 1
                return t % XRING

            def linear(label, n_out, tiles, moving, ready=None, width=P, extra=None):
                total = sum(n for n, _ in tiles) + (extra is not None)
                for m in range(n_out):
                    out = open_bank()[0:width, :]
                    k = 0
                    for n, rows in tiles:
                        slot = take_tile()
                        for j in range(n):
                            if m == 0 and ready:
                                ready(k)
                            k += 1
                            ins = mm(out, ring[0:rows, slot, j * width:(j + 1) * width], moving(k - 1),
                                     k == 1, k == total, k == total)
                        if k < total - (extra is not None):
                            state["pending"] = tile_free
                    if extra is not None:
                        ins = mm(out, ring[0:ME, slot, KC * P:KC * P + P], extra, False, True, True)
                    state["pending"] = tile_free
                    ins.then_inc(bank_full.sem, bank_full.tick((label, m)))

            def to_tokens(label, source, ready=None):
                blocks = [(t, m) for t in range(NT) for m in range(KC)]
                for n in range(KC):
                    out = open_bank()
                    for j, (t, m) in enumerate(blocks[4 * n:4 * n + 4]):
                        if ready and t == 0:
                            ready(m)
                        ins = mm(out[:, j * P:(j + 1) * P], source[:, m, t * P:(t + 1) * P], None, last=j == 3, transpose=True)
                    ins.then_inc(bank_full.sem, bank_full.tick((label, n)))

            def norm_sums(label, source, last_ready):
                pe.wait_ge(dve_done.sem, dve_done.at((label, "part")))
                mm(bank[7][:, :], ones[:, :], mean[:, :], True, False)
                last_ready(KC - 1)
                ins = mm(bank[7][:, :], ones[:, :], source[:, KC - 1, :], False, True, True)
                ins.then_inc(agg_done.sem, agg_done.tick((label, "sum")))
                for k in range(KC):
                    pe.wait_ge(act_done.sem, act_done.at((label, "sq", k)))
                    ins = mm(bank[6][:, :], ones[:, :], sq[:, k, :], k == 0, k == KC - 1, k == KC - 1)
                ins.then_inc(agg_done.sem, agg_done.tick((label, "var")))

            def after(what, label, back=0):
                return lambda k: pe.wait_ge(what.sem, what.at((label, k), back))

            def all_of(what, label, n=KC):
                pe.wait_ge(what.sem, what.at((label, n - 1)))

            def aggregate(label, node_rows, counts):
                for m in range(KC):
                    out = open_bank()
                    ins = group(out[:, :], [(node_rows[:, t, m * P:(m + 1) * P], counts[:, t, :]) for t in range(NT)])
                    ins.then_inc(bank_full.sem, bank_full.tick((label, m)))

            x_n = lambda k: XN[:, k, :]
            of = lambda source: (lambda k: source[:, k, :])
            WHOLE, BY96 = [(KC, P)], [(H8, D8)]

            pe.wait_ge(x_in, 16)
            pe.wait_ge(pool_done.sem, pool_done.at("consts"))
            norm_sums("ln0", XT, lambda k: None)

            def edge_chunks(start, stop, n, product, opens, closes):
                def four(at, first=False, last=False):
                    for b in range(4):
                        pe.wait_ge(onehot_ready, at + (b + 1))
                        for c in range(NT):
                            ins = product(at, b, c, first and b == 0, last and b == 3)
                        ins.then_inc(onehot_used, 1)
                if opens:
                    four(n * EC + start, first=True)
                with pe.Fori(start // 4 + opens, stop // 4 - closes) as i:
                    four(i * 4 + n * EC)
                if closes:
                    four(n * EC + stop - 4, last=True)

            def feature_product(at, b, c, first, last):
                return nc.tensor.matmul(bank[4 + c][:, 0:256], onehot32[:, b, c * P:(c + 1) * P],
                                        feats[:, at + b, :] if isinstance(at, int) else
                                        feats[:, bass.ds(at + b, 1), :].rearrange("p a f -> p (a f)"),
                                        start=first, stop=last)

            pe.wait_ge(act_done.sem, act_done.at(("ln0", "std")))
            for g, (start, stop) in enumerate(FEAT_PARTS):
                pe.wait_ge(feat_in[g], 16)
                edge_chunks(start, stop, 0, feature_product, g == 0, g == len(FEAT_PARTS) - 1)
            for f in range(2):
                out = open_bank()
                pe.wait_ge(act_done.sem, act_done.at("edge_sum"))
                for t in range(NT):
                    ins = mm(out[:, t * P:(t + 1) * P], edge_sum[:, t, f * P:(f + 1) * P], None, last=t == 3, transpose=True)
                ins.then_inc(bank_full.sem, bank_full.tick(("edge_sum_t", f)))
            for p in range(len(PACKED)):
                for g, (start, stop) in enumerate(GROUPS):
                    n = len(GROUPS) * p + g
                    banks = bank[4:] if n % 2 == 0 else bank[:4]
                    if n >= 2:
                        pe.wait_ge(act_done.sem, act_done.at(("group", n - 2)))
                    elif n == 1:
                        pe.wait_ge(bank_free.sem, bank_free.at(("edge_sum_t", 1)))
                    for c in range(NT):
                        nc.tensor.matmul(banks[c][:, :], one_row[:, :], shift_row[:, :], start=True, stop=False)

                    def count_product(at, b, c, first, last):
                        return nc.tensor.matmul(banks[c][:, :], onehot_a[:, b, c * P:(c + 1) * P], onehot_b[:, b, :],
                                                start=False, stop=last)

                    edge_chunks(start, stop, p + 1, count_product, False, True)
            pe.wait_ge(act_done.sem, act_done.at(("group", len(GROUPS) * len(PACKED) - 2)))
            pe.wait_ge(pool_done.sem, pool_done.at("count_all"))
            for c in range(NT):
                out = open_bank()
                for t in range(NT):
                    ins = mm(out[:, t * P:(t + 1) * P], cnt[3][:, t, c * P:(c + 1) * P], None, last=t == NT - 1, transpose=True)
                ins.then_inc(bank_full.sem, bank_full.tick(("count_t", c)))
            for r in range(REL4):
                out = open_bank()
                ins = group(out[:, :], [(ones[:, :], fresh[r][:, c, :]) for c in range(NT)])
                ins.then_inc(bank_full.sem, bank_full.tick(("degree", r)))

            pe.wait_ge(small_in, 16 * len(SMALL))

            def softmax_attention():
                linear("v0", KC, WHOLE, of(chunks(A_)), lambda k: pe.wait_ge(dve_done.sem, dve_done.at(("nodes", k))))
                to_tokens("v0_tok", chunks(C_), after(bank_free, "v0"))
                v_tok = tokens(B_)
                for h in range(H8):
                    if h == 0:
                        linear(("aq", h), 1, WHOLE, of(chunks(A_)), width=D8)
                        linear(("ak", h), 1, WHOLE, of(chunks(A_)), width=D8)
                    pe.wait_ge(bank_free.sem, bank_free.at((("ak", h), 0)))
                    for t in range(NT):
                        out = open_bank()
                        own = 2 * (h % 2)
                        ins = mm(out[:, :], qk[0][0:D8, own, t * P:(t + 1) * P], qk[0][0:D8, own + 1, :], last=True)
                        ins.then_inc(bank_full.sem, bank_full.tick(("scores", h, t)))
                    if h + 1 < H8:
                        linear(("aq", h + 1), 1, WHOLE, of(chunks(A_)), width=D8)
                        linear(("ak", h + 1), 1, WHOLE, of(chunks(A_)), width=D8)
                    pe.wait_ge(dve_done.sem, dve_done.at(("probs", h)))
                    for c in range(NT):
                        out = open_bank()
                        for t in range(NT):
                            ins = mm(out[:, t * P:(t + 1) * P], probs[:, t, c * P:(c + 1) * P], None,
                                     last=t == NT - 1, transpose=True)
                        ins.then_inc(bank_full.sem, bank_full.tick(("probs_t", h, c)))
                    out = open_bank()
                    if h == 0:
                        all_of(bank_free, "v0_tok")
                    for c in range(NT):
                        pe.wait_ge(bank_free.sem, bank_free.at(("probs_t", h, c)))
                        ins = mm(out[0:D8, :], v_tok[:, c, h * D8:(h + 1) * D8], probs_t[:, c, :],
                                 c == 0, c == NT - 1, c == NT - 1)
                    ins.then_inc(bank_full.sem, bank_full.tick(("att", h)))
                linear("wo", KC, BY96, of(att96), lambda k: pe.wait_ge(bank_free.sem, bank_free.at(("att", k))))

            def performer96():
                linear("v1", KC, WHOLE, x_n)
                to_tokens("v1_tok", chunks(C_), after(bank_free, "v1"))
                v_tok = tokens(B_)
                for h in range(H8):
                    if h == 0:
                        linear(("mq", h), 1, WHOLE, x_n, width=D8)
                        linear(("mk", h), 1, WHOLE, x_n, width=D8)
                    own = qk[h % 2]
                    pe.wait_ge(act_done.sem, act_done.at(("m_sq", h)))
                    for m in range(2):
                        out = open_bank()
                        ins = group(out[:, :], [(small["rf0"][:, m * P:(m + 1) * P], own[0:D8, 0, :]),
                                                (neg_half[0:D8, 0:P], own[0:D8, 2, :])])
                        ins.then_inc(bank_full.sem, bank_full.tick(("m_phi_q", h, m)))
                    for j in range(2):
                        out = open_bank()
                        for t in (2 * j, 2 * j + 1):
                            node = slice(t * P, (t + 1) * P)
                            ins = group(out[:, (t % 2) * M_RF:(t % 2 + 1) * M_RF],
                                        [(own[0:D8, 1, node], small["rf0"][:, :]), (own[0:D8, 3, node], neg_half[0:D8, :])],
                                        t % 2 == 1)
                        ins.then_inc(bank_full.sem, bank_full.tick(("m_phi_k", h, j)))
                    if h + 1 < H8:
                        linear(("mq", h + 1), 1, WHOLE, x_n, width=D8)
                        linear(("mk", h + 1), 1, WHOLE, x_n, width=D8)
                    pe.wait_ge(bank_free.sem, bank_free.at(("m_phi_k", h, 1)))
                    if h == 0:
                        all_of(bank_free, "v1_tok")
                    out = open_bank()
                    for m in range(2):
                        feature = slice(m * P, (m + 1) * P)
                        group(out[:, m * 2 * D8:m * 2 * D8 + D8],
                              [(pk0[:, t, feature], v_tok[:, t, h * D8:(h + 1) * D8]) for t in range(NT)], False)
                        ins = group(out[:, m * 2 * D8 + D8:(m + 1) * 2 * D8],
                                    [(pk0[:, t, feature], ones[:, 0:D8]) for t in range(NT)], m == 1)
                    ins.then_inc(bank_full.sem, bank_full.tick(("m_kv", h)))
                    pe.wait_ge(bank_free.sem, bank_free.at(("m_kv", h)))
                    for j in range(2):
                        out = open_bank()
                        ins = group(out[0:D8, :], [(kv0[:, m, j * D8:(j + 1) * D8], pq0[:, m, :]) for m in range(2)])
                        ins.then_inc(bank_full.sem, bank_full.tick(("m_out", h, j)))
                linear("proj0", KC, BY96, of(att96), lambda k: pe.wait_ge(dve_done.sem, dve_done.at(("m_att", k))))

            def experts_of_one(tag, ln, source, gate, gate_bias):
                norm_sums(ln, XT, after(dve_done, source))
                linear((tag, "up0"), LEAD, WHOLE, x_n, after(dve_done, ln))
                out = open_bank()
                for t in range(NT):
                    pairs = [(XN[:, k, t * P:(t + 1) * P], gate[:, k, :]) for k in range(KC)]
                    if gate_bias is not None:
                        pairs.append((ones[0:1, :], gate_bias[0:1, :]))
                    ins = group(out[:, t * ME:(t + 1) * ME], pairs, t == NT - 1)
                ins.then_inc(bank_full.sem, bank_full.tick((tag, "logit")))
                linear((tag, "up1"), KC, WHOLE, x_n)
                out = open_bank()
                pe.wait_ge(dve_done.sem, dve_done.at((tag, "comb")))
                for t in range(NT):
                    ins = mm(out[0:ME, t * P:(t + 1) * P], comb[:, t, :], None, last=t == NT - 1, transpose=True)
                ins.then_inc(bank_full.sem, bank_full.tick((tag, "comb_t")))
                pe.wait_ge(bank_free.sem, bank_free.at((tag, "comb_t")))
                for e in range(ME):
                    out = open_bank()
                    ins = mm(out[:, :], ident[0:ME, e:e + 1].to_broadcast([ME, P]), comb_t, last=True)
                    ins.then_inc(bank_full.sem, bank_full.tick((tag, "scale", e)))
                linear((tag, "up2"), ME * MF // P - KC - LEAD, WHOLE, x_n)
                linear((tag, "down"), KC, WHOLE * 4, of(hidden), after(dve_done, (tag, "hidden")), extra=comb_t)

            def performer64():
                linear("v2", KC, WHOLE, x_n, after(dve_done, "ln2"))
                to_tokens("v2_tok", chunks(D_), after(bank_free, "v2"))
                v_tok = tokens(B_)
                for p in range(KC):
                    if p == 0:
                        linear(("nq", p), 1, WHOLE, x_n)
                        linear(("nk", p), 1, WHOLE, x_n)
                    own = qk[p % 2]
                    pe.wait_ge(act_done.sem, act_done.at(("n_sq", p)))
                    if p == 0:
                        all_of(bank_free, "v2_tok")
                    for s in range(2):
                        for m in range(2):
                            out = open_bank()
                            ins = group(out[:, :], [(small["rf1"][:, s, m * P:(m + 1) * P], own[:, 0, :]),
                                                    (neg_half_pair[:, s, 0:P], own[:, 2, :])])
                            ins.then_inc(bank_full.sem, bank_full.tick(("n_phi_q", p, s, m)))
                        for j in range(2):
                            out = open_bank()
                            for t in (2 * j, 2 * j + 1):
                                node = slice(t * P, (t + 1) * P)
                                ins = group(out[:, (t % 2) * M_RF:(t % 2 + 1) * M_RF],
                                            [(own[:, 1, node], small["rf1"][:, s, :]),
                                             (own[:, 3, node], neg_half_pair[:, s, :])], t % 2 == 1)
                            ins.then_inc(bank_full.sem, bank_full.tick(("n_phi_k", p, s, j)))
                        if s == 1 and p + 1 < KC:
                            linear(("nq", p + 1), 1, WHOLE, x_n)
                            linear(("nk", p + 1), 1, WHOLE, x_n)
                        pe.wait_ge(bank_free.sem, bank_free.at(("n_phi_k", p, s, 1)))
                        out = open_bank()
                        for m in range(2):
                            feature = slice(m * P, (m + 1) * P)
                            group(out[:, m * 2 * P:m * 2 * P + P],
                                  [(pk1[:, t, feature], v_tok[:, t, p * P:(p + 1) * P]) for t in range(NT)], False)
                            ins = group(out[:, m * 2 * P + P:(m + 1) * 2 * P],
                                        [(pk1[:, t, feature], ones[:, :]) for t in range(NT)], m == 1)
                        ins.then_inc(bank_full.sem, bank_full.tick(("n_kv", p, s)))
                    for j in range(2):
                        out = open_bank()
                        for m in range(2):
                            for s in range(2):
                                pe.wait_ge(bank_free.sem, bank_free.at(("n_kv", p, s)))
                                half = slice(64 * s, 64 * s + 64)
                                ins = mm(out[half, :], kv1[:, s, m, j * P + 64 * s:j * P + 64 * s + 64], pq1[:, s, m, :],
                                         m == 0, m == 1, m == 1)
                        ins.then_inc(bank_full.sem, bank_full.tick(("n_out", p, j)))
                linear("proj1", KC, WHOLE, of(chunks(A_)), after(dve_done, "n_att"))
                norm_sums("lny", chunks(C_), after(dve_done, "y"))

            def edge_logits(tag, heads, r, source, ready, q, k):
                out = open_bank()
                for t in range(NT):
                    if t == 0:
                        for j in range(KC):
                            ready(j)
                    ins = group(out[:, t * heads:(t + 1) * heads],
                                [(source[:, j, t * P:(t + 1) * P], q[:, j, :]) for j in range(KC)], t == NT - 1)
                ins.then_inc(bank_full.sem, bank_full.tick((tag, "q", r)))
                out = open_bank()
                ins = group(out[0:heads, :], [(k[:, j, :], source[:, j, :]) for j in range(KC)])
                ins.then_inc(bank_full.sem, bank_full.tick((tag, "k", r)))

            def edge_softmax_row(tag, heads, h, r):
                out = open_bank()
                pe.wait_ge(bank_free.sem, bank_free.at((tag, "k", r)))
                ins = mm(out[:, :], ident[0:heads, h:h + 1].to_broadcast([heads, P]), krow[0:heads, r, :], last=True)
                ins.then_inc(bank_full.sem, bank_full.tick((tag, "row", h, r)))

            def weights_transposed(tag, h, r, buf):
                pe.wait_ge(dve_done.sem, dve_done.at((tag, "diag", h)))
                for c in range(NT):
                    out = open_bank()
                    for t in range(NT):
                        ins = mm(out[:, t * P:(t + 1) * P], scores[:, buf, t, c * P:(c + 1) * P], diag[h % 2][:, t, :],
                                 last=t == NT - 1)
                    ins.then_inc(bank_full.sem, bank_full.tick((tag, "weights_t", h, r, c)))

            def rgat(which, source, tiles, ready, q, k):
                tag, heads, relations = which
                xr = chunks(D_ if tag == "rgat1" else E_ + 12)
                rows = [tokens(a) for a in (A_, B_, C_)]
                for r in range(relations):
                    linear((tag, "xr", r), KC, tiles, source, ready if r == 0 else None)
                    if r < relations - 1:
                        to_tokens((tag, "xr_tok", r), xr, after(bank_free, (tag, "xr", r)))
                    edge_logits(tag, heads, r, xr, after(bank_free, (tag, "xr", r)), q, k)
                    edge_softmax_row(tag, heads, 0, r)
                to_tokens((tag, "xr_tok", relations - 1), xr)
                all_of(bank_free, (tag, "xr_tok", relations - 1))
                for h in range(heads):
                    for r in range(relations):
                        weights_transposed(tag, h, r, r)
                        if h + 1 < heads:
                            edge_softmax_row(tag, heads, h + 1, r)
                    if tag == "rgat1":
                        if h >= 2:
                            pe.wait_ge(act_done.sem, act_done.at((tag, "out", h - 2)))
                        for r in range(relations):
                            for j, (m, part) in enumerate(PIECES[h]):
                                f = slice(m * P + part.start, m * P + part.stop)
                                for c in range(NT):
                                    pe.wait_ge(bank_free.sem, bank_free.at((tag, "weights_t", h, r, c)))
                                    ins = mm(bank[4 + 2 * (h % 2) + j][part, :], rows[r][:, c, f], weights_t[r][:, c, :],
                                             r == 0 and c == 0, r == 2 and c == NT - 1, True)
                            ins.then_inc(agg_done.sem, agg_done.tick((tag, relations * h + r)))
                    if tag == "rgat2":
                        for r in range(relations):
                            pe.wait_ge(bank_free.sem, bank_free.at((tag, "weights_t", h, r, NT - 1)))
                        for m in range(KC):
                            out = open_bank()
                            ins = group(out[:, :], [(rows[r][:, c, m * P:(m + 1) * P], weights_t3[:, r, c, :])
                                                    for r in range(relations) for c in range(NT)])
                            ins.then_inc(bank_full.sem, bank_full.tick((tag, "out", m)))

            def elu_attention():
                linear("v4", KC, WHOLE, x_n, after(dve_done, "ln4"))
                to_tokens("v4_tok", chunks(D_), after(bank_free, "v4"))
                v_tok = tokens(B_)
                for p in range(KC):
                    if p == 0:
                        linear(("eq", p), 1, WHOLE, x_n)
                        linear(("ek", p), 1, WHOLE, x_n)
                    own = qk[p % 2]
                    pe.wait_ge(dve_done.sem, dve_done.at(("e_k", p)))
                    out = open_bank()
                    for t in range(NT):
                        ins = mm(out[:, t * P:(t + 1) * P], own[:, 1, t * P:(t + 1) * P], None, last=t == NT - 1, transpose=True)
                    ins.then_inc(bank_full.sem, bank_full.tick(("e_ktok", p)))
                    if p + 1 < KC:
                        linear(("eq", p + 1), 1, WHOLE, x_n)
                        linear(("ek", p + 1), 1, WHOLE, x_n)
                    pe.wait_ge(bank_free.sem, bank_free.at(("e_ktok", p)))
                    if p == 0:
                        all_of(bank_free, "v4_tok")
                    out = open_bank()
                    group(out[:, 0:P], [(ktok[:, t, :], v_tok[:, t, p * P:(p + 1) * P]) for t in range(NT)], False)
                    ins = group(out[:, P:2 * P], [(ktok[:, t, :], ones[:, :]) for t in range(NT)])
                    ins.then_inc(bank_full.sem, bank_full.tick(("e_kv", p)))
                    pe.wait_ge(bank_free.sem, bank_free.at(("e_kv", p)))
                    for j in range(2):
                        out = open_bank()
                        mm(out[:, :], kv_diag[:, j, :], own[:, 0, :], last=True).then_inc(
                                bank_full.sem, bank_full.tick(("e_out", p, j)))
                linear("proj2", KC, WHOLE, of(chunks(A_)), after(dve_done, "e_att"))

            def rgcn_layer(tag, ready):
                x_rows = tokens(T_)
                g = [chunks(a) for a in (A_, B_, C_, D_)]
                for m in range(KC):
                    ready(m)
                for m in range(KC):
                    out = open_bank()
                    for t in range(NT):
                        ins = mm(out[:, t * P:(t + 1) * P], XN[:, m, t * P:(t + 1) * P], None, last=t == NT - 1, transpose=True)
                    ins.then_inc(bank_full.sem, bank_full.tick(((tag, "tok"), m)))
                all_of(bank_free, (tag, "tok"))
                for r in range(REL4):
                    aggregate((tag, "agg", r), x_rows, cnt[r])
                linear((tag, "out"), KC, WHOLE * 5, lambda k: XN[:, k, :] if k < KC else g[k // KC - 1][:, k % KC, :],
                       lambda k: pe.wait_ge(bank_free.sem, bank_free.at(((tag, "agg", k // KC - 1), k % KC))) if k >= KC else None)

            linear("nodes0", KC, WHOLE, x_n, after(dve_done, "ln0"))
            linear("edge_part", KC, [(2, P)], of(edge_sum_t), lambda k: pe.wait_ge(bank_free.sem, bank_free.at(("edge_sum_t", k))))
            for k in range(KC):
                pe.wait_ge(bank_free.sem, bank_free.at(("nodes0", k)))
            pe.wait_ge(dve_done.sem, dve_done.at("counts_looped"))
            with loop(pe, "gnn0", 3, (bank_full, tile_free, agg_done)):
                to_tokens("tok0", chunks(A_), lambda m: pe.wait_ge(dve_done.sem, dve_done.at(("nodes", m), 1)))
                all_of(bank_free, "tok0")
                aggregate("agg0", tokens(B_), cnt[3])
                linear("h0", KC, WHOLE * 2, lambda k: (chunks(A_) if k < KC else chunks(C_))[:, k % KC, :],
                       lambda k: pe.wait_ge(dve_done.sem, dve_done.at(("agg0_sum", k - KC))) if k >= KC else None)
                norm_sums("lnh", chunks(B_), after(bank_free, "h0"))
                linear("w2", KC, WHOLE, of(chunks(B_)), after(act_done, "relu0"))
            state["tile"] += 2 * 3 * KC
            softmax_attention()
            performer96()
            experts_of_one("moe0", "ln1", "proj0_x", small["L0_Ws"], small["L0_bs"])
            norm_sums("ln2", XT, after(dve_done, "moe0_x"))
            performer64()
            rgat(RGAT1, x_n, WHOLE, None, small["q1"], small["k1"])
            rgat(RGAT2, of(rgat1_out), WHOLE, lambda k: pe.wait_ge(dve_done.sem, dve_done.at(("rgat1", "elu", k))), small["q2"], small["k2"])
            norm_sums("ln3", XT, after(dve_done, "rgat2_x"))
            linear("f1_up", MF // P, WHOLE, x_n, after(dve_done, "ln3"))
            linear("f1_down", KC, [(3, P)], of(chunks(A_)), after(bank_free, "f1_up"))
            norm_sums("ln4", XT, after(dve_done, "f1_x"))
            elu_attention()
            pe.wait_ge(reloaded[0], 16 * REL4)
            with loop(pe, "rgcn", 2, (bank_full, tile_free)):
                rgcn_layer("rgcn", lambda m: pe.wait_ge(dve_done.sem, dve_done.at((("rgcn", "x"), m), 1)))
            state["tile"] += 5 * KC
            rgcn_layer("rgcnb", lambda m: pe.wait_ge(dve_done.sem, dve_done.at((("rgcn", "x"), m))))
            experts_of_one("moe2", "ln5", "routb_x", small["L2_Ws"], None)

            def graph_attention():
                ft_t, ft_rows = chunks(B_), tokens(A_)
                for m in range(KC):
                    pe.wait_ge(dve_done.sem, dve_done.at(("ln6", m)))
                    out = open_bank()
                    mm(out[:, :], small["fc"][:, :], XN[:, m, :], last=True).then_inc(bank_full.sem, bank_full.tick(("ft", m)))
                tag, heads, relations = GAT
                edge_logits(tag, heads, 0, ft_t, after(bank_free, "ft"), small["attn_r"], small["attn_l"])
                for h in range(2):
                    edge_softmax_row(tag, heads, h, 0)
                to_tokens("ft_rows", ft_t)
                for m in range(KC):
                    out = open_bank()
                    mm(out[:, :], small["res"][:, :], XN[:, m, :], last=True).then_inc(bank_full.sem, bank_full.tick(("res", m)))
                all_of(bank_free, "ft_rows")

                def aggregated(h):
                    out = open_bank()
                    m = h // 2
                    for c in range(NT):
                        pe.wait_ge(bank_free.sem, bank_free.at((tag, "weights_t", h, 0, c)))
                        ins = mm(out[:, :], ft_rows[:, c, m * P:(m + 1) * P], weights_g[h % 2][:, c, :],
                                 c == 0, c == NT - 1, c == NT - 1)
                    ins.then_inc(bank_full.sem, bank_full.tick((tag, "agg", h)))

                for h in range(heads):
                    if h + 2 < heads:
                        edge_softmax_row(tag, heads, h + 2, 0)
                    weights_transposed(tag, h, 0, h % 3)
                    if h:
                        aggregated(h - 1)
                aggregated(heads - 1)

            def experts():
                out = open_bank()
                for k in range(KC):
                    pe.wait_ge(dve_done.sem, dve_done.at(("ln7", k)))
                    ins = mm(out[0:NE, :], small["L3_gate"][:, k, :], XN[:, k, :], k == 0, k == KC - 1, k == KC - 1)
                ins.then_inc(bank_full.sem, bank_full.tick("x_logit"))
                linear("shared_up", 2 * SHARED // P, WHOLE, x_n)
                for label, n in (("slots", 2), ("score", 1)):
                    out = open_bank()
                    pe.wait_ge(dve_done.sem, dve_done.at("x_slots"))
                    for t in range(NT):
                        ins = mm(out[:, t * NE:(t + 1) * NE], choose[:, n, t * P:(t + 1) * P], None, last=t == NT - 1, transpose=True)
                    ins.then_inc(bank_full.sem, bank_full.tick(("x_" + label, 0)))
                linear("shared_down", KC, WHOLE * 2, of(shared_hidden), after(dve_done, "shared_hidden"))
                state["pending"] = None
                while state["tile"] % RING:
                    take_tile()
                to_tokens("x_rows", XN)
                all_of(bank_free, "x_rows")
                pe.wait_ge(bank_free.sem, bank_free.at(("x_score", 0)))
                pe.wait_ge(dve_done.sem, dve_done.at("x_place"))
                out = open_bank()
                for p in range(NPAIR):
                    ins = group(out[:, p * NE:(p + 1) * NE],
                                [(place[:, t, p * P:(p + 1) * P], score_of[:, t, :]) for t in range(NT)], p == NPAIR - 1)
                ins.then_inc(bank_full.sem, bank_full.tick("x_slot_score"))
                for p in range(NPAIR):
                    out = open_bank()
                    for t in range(NT):
                        ins = mm(out[:, t * P:(t + 1) * P], place[:, t, p * P:(p + 1) * P], None, last=t == NT - 1, transpose=True)
                    ins.then_inc(bank_full.sem, bank_full.tick(("x_place_t", p)))
                while bank_full.n % NB:
                    out = open_bank()
                    mm(out[:, 0:P], ones[:, :], ident[:, :], last=True).then_inc(bank_full.sem, bank_full.tick())
                pe.wait_ge(bank_free.sem, bank_free.at(("x_place_t", NPAIR - 1)))
                tiles = 2 * (2 * FB + FB)
                with loop(pe, "pairs", NPAIR, (bank_full, x_tile_free)) as pair:
                    for j in range(2):
                        out = open_bank()
                        for m in range(3 * j, 3 * j + 3):
                            ins = group(out[:, m % 3 * P:(m % 3 + 1) * P],
                                        [(x_rows[:, t, m * P:(m + 1) * P], place[:, t, bass.ds(pair * P, P)]) for t in range(NT)], m % 3 == 2)
                        ins.then_inc(bank_full.sem, bank_full.tick(("x_gather", j)))
                    pe.wait_ge(bank_free.sem, bank_free.at(("x_gather", 1)))
                    half_rows = [slice(CAP * e, CAP * e + CAP) for e in range(2)]
                    for b in range(FB):
                        for kind in ("x_gate", "x_up"):
                            out = open_bank()
                            slots = [take_x_tile(pair, tiles) for e in range(2)]
                            for k in range(KC):
                                for e, rows in enumerate(half_rows):
                                    ins = mm(out[rows, :], x_pair[:, k, rows], x_ring[:, slots[e], k * 512:(k + 1) * 512],
                                             k == 0, k == KC - 1, k == KC - 1)
                                    if k == KC - 1 and e == 0:
                                        ins.then_inc(x_tile_free.sem, x_tile_free.tick())
                            state["pending"] = x_tile_free
                            ins.then_inc(bank_full.sem, bank_full.tick((kind, b)))
                    for b in range(FB):
                        out = open_bank()
                        pe.wait_ge(dve_done.sem, dve_done.at(("x_h", b)))
                        for c in range(4):
                            ins = nc.tensor.transpose(out[:, c * P:(c + 1) * P], x_hidden[:, b, c * P:(c + 1) * P], ident[:, :])
                            if state["pending"]:
                                ins.then_inc(state["pending"].sem, state["pending"].tick())
                                state["pending"] = None
                        ins.then_inc(bank_full.sem, bank_full.tick(("x_h_t", b)))
                    for half in range(2):
                        out = open_bank()
                        for j in range(3):
                            slots = [take_x_tile(pair, tiles) for e in range(2)]
                            for k in range(8):
                                c = 8 * j + k
                                pe.wait_ge(bank_free.sem, bank_free.at(("x_h_t", c // 4)))
                                for e, rows in enumerate(half_rows):
                                    ins = mm(out[rows, 0:D // 2], x_hidden_t[:, c, rows],
                                             x_ring[:, slots[e], k * (D // 2):(k + 1) * (D // 2)], c == 0, c == FC - 1, k == 7)
                                    if k == 7 and e == 0:
                                        ins.then_inc(x_tile_free.sem, x_tile_free.tick())
                            state["pending"] = x_tile_free
                        ins.then_inc(bank_full.sem, bank_full.tick(("x_down", half)))
                    pe.wait_ge(bank_free.sem, bank_free.at(("x_down", 1)))
                    for m in range(KC):
                        out = open_bank()
                        if state["pending"]:
                            mm(bank[7][:, 0:1], ones[:, :], ident[:, 0:1])
                        ins = mm(out[:, :], x_out[:, m * P:(m + 1) * P],
                                 place_t[:, bass.ds(pair, 1), :].rearrange("p a n -> p (a n)"), last=True)
                        ins.then_inc(bank_full.sem, bank_full.tick(("experts", m)))

            norm_sums("ln6", XT, after(dve_done, "moe2_x"))
            graph_attention()
            linear("xq", KC, WHOLE, x_n)
            linear("xk", KC, WHOLE, x_n)
            linear("xv", KC, WHOLE, x_n)
            linear("proj3", KC, WHOLE, of(chunks(T_)), after(dve_done, "xy"))
            norm_sums("ln7", XT, after(dve_done, "proj3_x"))
            experts()

        @block.scalar
        def _(act):
            ev_reader = [None, None]

            def filled():
                return bank[bank_free.n % NB]

            def linear(label, n_out, dst, func=ACT.Identity, bias=None, width=P, scale=1.0, before=None):
                for m in range(n_out):
                    act.wait_ge(bank_full.sem, bank_free.now(1))
                    src = filled()
                    if before:
                        before(m)
                    how = {} if bias is None else {"bias": bias(m)}
                    nc.scalar.activation(dst(m), src[0:width, :], func, scale=scale, **how).then_inc(
                            bank_free.sem, bank_free.tick((label, m)))

            def residual(label, bias=None):
                for m in range(KC):
                    act.wait_ge(bank_full.sem, bank_free.now(1))
                    src = filled()
                    if ev_reader[m % 2]:
                        act.wait_ge(dve_done.sem, dve_done.at(ev_reader[m % 2]))
                    how = {} if bias is None else {"bias": bias(m)}
                    nc.scalar.activation(EV[:, m % 2, :], src[:, :], ACT.Identity, **how).then_inc(
                            bank_free.sem, bank_free.tick((label, m)))
                    ev_reader[m % 2] = (label + "_x", m)

            def ev_free(n, label):
                if ev_reader[n]:
                    act.wait_ge(dve_done.sem, dve_done.at(ev_reader[n]))
                ev_reader[n] = label

            def to_tokens(label, dst):
                flat = dst.rearrange("p t f -> p (t f)")
                for n in range(KC):
                    act.wait_ge(bank_full.sem, bank_free.now(1))
                    nc.scalar.activation(flat[:, n * 4 * P:(n + 1) * 4 * P], filled()[:, :], ACT.Identity).then_inc(
                        bank_free.sem, bank_free.tick((label, n)))

            def norm(label, values):
                act.wait_ge(act_done.sem, act_done.now())
                nc.scalar.activation(warm_col[:, :], eps_col[:, :], ACT.Sqrt).then_inc(act_done.sem, act_done.tick())
                for k in range(KC):
                    act.wait_ge(dve_done.sem, dve_done.at((label, "d", k)))
                    nc.scalar.activation(sq[:, k, :], values[:, k, :], ACT.Square).then_inc(
                            act_done.sem, act_done.tick((label, "sq", k)))
                act.wait_ge(agg_done.sem, agg_done.at((label, "var")))
                nc.scalar.activation(rstd[:, :], bank[6][:, :], ACT.Sqrt, scale=1.0 / D, bias=eps_col[:, :]).then_inc(
                    act_done.sem, act_done.tick((label, "std")))

            def of(dst):
                return lambda m: dst[:, m, :]

            def bias_of(name, rows=P):
                return lambda m: col(name, m, rows)

            for n in range(4):
                act.dma_start(edge_i[:, n, :], io["edges"][n]).then_inc(edge_in, 16)
            for g, (start, stop) in enumerate(FEAT_PARTS):
                act.dma_start(feats[:, start:stop, :], io["feats"][:, start:stop, :]).then_inc(feat_in[g], 16)
            act.wait_ge(cols_in, 16)
            act.wait_ge(pool_done.sem, pool_done.at("consts"))
            norm("ln0", XN)
            act.wait_ge(onehot_used, EC)
            for t in range(NT):
                nc.scalar.activation(edge_sum[:, t, :], bank[4 + t][:, 0:256], ACT.Identity).then_inc(
                        act_done.sem, act_done.tick("edge_sum"))
            for f in range(2):
                act.wait_ge(bank_full.sem, bank_free.now(1))
                nc.scalar.activation(edge_sum_t[:, f, :], filled()[:, :], ACT.Identity).then_inc(
                        bank_free.sem, bank_free.tick(("edge_sum_t", f)))

            def unweighted(p):
                high = (fresh[1], fresh[3], cnt[1])[p]
                nc.scalar.activation(high, high, ACT.Identity, scale=1.0 / PACK).then_inc(
                        act_done.sem, act_done.tick(("unweighted", p)))

            for p in range(len(PACKED)):
                for g, (_, stop) in enumerate(GROUPS):
                    n = len(GROUPS) * p + g
                    banks = bank[4:] if n % 2 == 0 else bank[:4]
                    high = group_high if g else (fresh[1], fresh[3], cnt[1])[p]
                    act.wait_ge(onehot_used, EC * (p + 1) + stop)
                    if n:
                        act.wait_ge(pool_done.sem, pool_done.at(("unpacked", n - 1)))
                    if g == 0 and p:
                        unweighted(p - 1)
                    for c in range(NT):
                        nc.scalar.activation(high[:, c, :], banks[c][:, :], ACT.Identity, scale=1.0 / PACK, bias=round_col[:, :]).then_inc(
                            act_done.sem, act_done.tick(("rounded", n)))
                        nc.scalar.activation(group_sum[:, c, :], banks[c][:, :], ACT.Identity, bias=shift_col[:, :]).then_inc(
                            act_done.sem, act_done.tick(("group", n)))
                    act.wait_ge(act_done.sem, act_done.at(("rounded", n)))
                    nc.scalar.activation(high, high, ACT.Identity, scale=float(PACK), bias=unround_col[:, :]).then_inc(
                        act_done.sem, act_done.tick(("high", n)))
            for c in range(NT):
                act.wait_ge(bank_full.sem, bank_free.now(1))
                nc.scalar.activation(cnt[2][:, c, :], filled()[:, :], ACT.Identity).then_inc(
                        bank_free.sem, bank_free.tick(("count_t", c)))
            for r in range(REL4):
                act.wait_ge(bank_full.sem, bank_free.now(1))
                nc.scalar.activation(degree[r], filled()[:, :], ACT.Identity).then_inc(
                        bank_free.sem, bank_free.tick(("degree", r)))
            act.wait_ge(pool_done.sem, pool_done.at(("unpacked", len(PACKED) * len(GROUPS) - 1)))
            unweighted(2)

            def softmax_attention():
                linear("v0", KC, of(chunks(C_)), bias=bias_of("L0_gnn_bv"))
                to_tokens("v0_tok", tokens(B_))
                s = float(D8) ** -0.5

                def queries_and_keys(h):
                    for j, (name, b) in enumerate((("aq", "L0_gnn_bq"), ("ak", "L0_gnn_bk"))):
                        linear((name, h), 1, lambda m: qk[0][0:D8, 2 * (h % 2) + j, :], bias=lambda m: col(b, h, D8), width=D8)

                queries_and_keys(0)
                for h in range(H8):
                    for t in range(NT):
                        act.wait_ge(bank_full.sem, bank_free.now(1))
                        src = filled()
                        act.wait_ge(dve_done.sem, dve_done.at(("neg_max", h, t)))
                        nc.scalar.activation(probs[:, t, :], src[:, :], ACT.Exp, bias=stat[:, 4 + t:5 + t], scale=s, accum_out=stat[:, 8 + t:9 + t]).then_inc(
                                bank_free.sem, bank_free.tick(("exp", h, t)))
                    if h + 1 < H8:
                        queries_and_keys(h + 1)
                    for c in range(NT):
                        act.wait_ge(bank_full.sem, bank_free.now(1))
                        nc.scalar.activation(probs_t[:, c, :], filled()[:, :], ACT.Identity).then_inc(
                                bank_free.sem, bank_free.tick(("probs_t", h, c)))
                    act.wait_ge(bank_full.sem, bank_free.now(1))
                    nc.scalar.activation(att96[:, h, :], filled()[0:D8, :], ACT.Identity).then_inc(
                            bank_free.sem, bank_free.tick(("att", h)))
                residual("wo", bias_of("L0_gnn_bo"))

            def performer96():
                s = float(D8) ** -0.5
                linear("v1", KC, of(chunks(C_)), bias=bias_of("L0_mix_bv"))
                to_tokens("v1_tok", tokens(B_))
                act.wait_ge(dve_done.sem, dve_done.at("scaled_bias"))

                def queries_and_keys(h):
                    own = qk[h % 2]
                    for j, name in enumerate(("mq", "mk")):
                        linear((name, h), 1, lambda m: own[0:D8, j, :], bias=lambda m: stat[0:D8, 32 + 8 * j + h:33 + 8 * j + h],
                               width=D8, scale=s)
                    act.wait_ge(bank_free.sem, bank_free.at((("mk", h), 0)))
                    for j in range(2):
                        nc.scalar.activation(own[0:D8, 2 + j, :], own[0:D8, j, :], ACT.Square).then_inc(
                                act_done.sem, act_done.tick(("m_sq", h)))

                queries_and_keys(0)
                for h in range(H8):
                    for m in range(2):
                        act.wait_ge(bank_full.sem, bank_free.now(1))
                        nc.scalar.activation(pq0[:, m, :], filled()[:, :], ACT.Exp).then_inc(
                                bank_free.sem, bank_free.tick(("m_phi_q", h, m)))
                    for j in range(2):
                        act.wait_ge(bank_full.sem, bank_free.now(1))
                        nc.scalar.activation(pk0[:, 2 * j:2 * j + 2, :], filled()[:, :].rearrange("p (t m) -> p t m", t=2), ACT.Exp).then_inc(
                                bank_free.sem, bank_free.tick(("m_phi_k", h, j)))
                    if h + 1 < H8:
                        queries_and_keys(h + 1)
                    act.wait_ge(bank_full.sem, bank_free.now(1))
                    nc.scalar.activation(kv0, filled()[:, 0:4 * D8].rearrange("p (m c) -> p m c", m=2), ACT.Identity).then_inc(
                            bank_free.sem, bank_free.tick(("m_kv", h)))
                    act.wait_ge(bank_full.sem, bank_free.now(1))
                    nc.scalar.activation(att96[:, h, :], filled()[0:D8, :], ACT.Identity).then_inc(
                            bank_free.sem, bank_free.tick(("m_out", h, 0)))
                    act.wait_ge(bank_full.sem, bank_free.now(1))
                    src = filled()
                    ev_free(h % 2, ("m_att", h))
                    nc.scalar.activation(EV[0:D8, h % 2, :], src[0:D8, :], ACT.Identity).then_inc(
                            bank_free.sem, bank_free.tick(("m_out", h, 1)))
                residual("proj0", bias_of("L0_mix_proj_b"))

            def experts_of_one(tag, ln, func, bias):
                norm(ln, XN)
                linear((tag, "up0"), LEAD, of(hidden), func, lambda m: col(bias, m))
                act.wait_ge(bank_full.sem, bank_free.now(1))
                nc.scalar.activation(logit[:, :, :], filled()[:, 0:NT * ME].rearrange("p (t e) -> p t e", t=NT), ACT.Identity).then_inc(
                        bank_free.sem, bank_free.tick((tag, "logit")))
                act.wait_ge(dve_done.sem, dve_done.at((tag, "shifted")))
                nc.scalar.activation(gate_exp[:, :, :], gate_exp[:, :, :], ACT.Exp).then_inc(
                        act_done.sem, act_done.tick((tag, "exp")))
                linear((tag, "up1"), KC, lambda m: hidden[:, LEAD + m, :], func, lambda m: col(bias, LEAD + m))
                act.wait_ge(bank_full.sem, bank_free.now(1))
                nc.scalar.activation(comb_t, filled()[0:ME, :], ACT.Identity).then_inc(
                        bank_free.sem, bank_free.tick((tag, "comb_t")))
                for e in range(ME):
                    act.wait_ge(bank_full.sem, bank_free.now(1))
                    nc.scalar.activation(scale_row[:, e, :], filled()[:, :], ACT.Identity).then_inc(
                            bank_free.sem, bank_free.tick((tag, "scale", e)))
                rest = LEAD + KC
                linear((tag, "up2"), ME * MF // P - rest, lambda m: hidden[:, rest + m, :], func, lambda m: col(bias, rest + m))
                residual(tag)

            def performer64():
                linear("v2", KC, of(chunks(D_)))
                to_tokens("v2_tok", tokens(B_))

                def queries_and_keys(p):
                    own = qk[p % 2]
                    for j, name in enumerate(("nq", "nk")):
                        linear((name, p), 1, lambda m: own[:, j, :])
                    act.wait_ge(bank_free.sem, bank_free.at((("nk", p), 0)))
                    for j in range(2):
                        nc.scalar.activation(own[:, 2 + j, :], own[:, j, :], ACT.Square).then_inc(
                                act_done.sem, act_done.tick(("n_sq", p)))

                queries_and_keys(0)
                for p in range(KC):
                    for s in range(2):
                        for m in range(2):
                            act.wait_ge(bank_full.sem, bank_free.now(1))
                            nc.scalar.activation(pq1[:, s, m, :], filled()[:, :], ACT.Exp).then_inc(
                                    bank_free.sem, bank_free.tick(("n_phi_q", p, s, m)))
                        for j in range(2):
                            act.wait_ge(bank_full.sem, bank_free.now(1))
                            nc.scalar.activation(pk1[:, 2 * j:2 * j + 2, :], filled()[:, :].rearrange("p (t m) -> p t m", t=2), ACT.Exp).then_inc(
                                    bank_free.sem, bank_free.tick(("n_phi_k", p, s, j)))
                        if s == 1 and p + 1 < KC:
                            queries_and_keys(p + 1)
                        act.wait_ge(bank_full.sem, bank_free.now(1))
                        nc.scalar.activation(kv1[:, s, :, :], filled()[:, :].rearrange("p (m c) -> p m c", m=2), ACT.Identity, scale=1.0 / M_RF).then_inc(
                                bank_free.sem, bank_free.tick(("n_kv", p, s)))
                    ev_free(p % 2, ("n_att", p))
                    act.wait_ge(bank_full.sem, bank_free.now(1))
                    nc.scalar.activation(chunks(A_)[:, p, :], filled()[:, :], ACT.Identity).then_inc(
                            bank_free.sem, bank_free.tick(("n_out", p, 0)))
                    act.wait_ge(bank_full.sem, bank_free.now(1))
                    nc.scalar.activation(EV[:, p % 2, :], filled()[:, :], ACT.Identity).then_inc(
                            bank_free.sem, bank_free.tick(("n_out", p, 1)))
                linear("proj1", KC, of(chunks(C_)), bias=bias_of("L1_mix_b_proj"))
                norm("lny", chunks(C_))

            def edge_logits(tag, heads, r):
                act.wait_ge(bank_full.sem, bank_free.now(1))
                nc.scalar.activation(stat[:, 64 + r * NT * heads:64 + (r + 1) * NT * heads], filled()[:, 0:NT * heads], ACT.Identity).then_inc(
                        bank_free.sem, bank_free.tick((tag, "q", r)))
                act.wait_ge(bank_full.sem, bank_free.now(1))
                nc.scalar.activation(krow[0:heads, r, :], filled()[0:heads, :], ACT.Identity).then_inc(
                        bank_free.sem, bank_free.tick((tag, "k", r)))

            def edge_scores(tag, heads, h, r, buf):
                act.wait_ge(bank_full.sem, bank_free.now(1))
                src = filled()
                act.wait_ge(bank_free.sem, bank_free.at((tag, "q", r)))
                for t in range(NT):
                    at = 64 + (r * NT + t) * heads + h
                    ins = nc.scalar.activation(scores[:, buf, t, :], src[:, :], ACT.Identity, bias=stat[:, at:at + 1])
                    if t < NT - 1:
                        ins.then_inc(act_done.sem, act_done.tick((tag, "sum", h, r, t)))
                ins.then_inc(bank_free.sem, bank_free.tick((tag, "row", h, r)))

            def rgat(which):
                tag, heads, relations = which
                for r in range(relations):
                    linear((tag, "xr", r), KC, of(chunks(D_ if tag == "rgat1" else E_ + 12)))
                    if r < relations - 1:
                        to_tokens((tag, "xr_tok", r), tokens((A_, B_, C_)[r]))
                    edge_logits(tag, heads, r)
                    edge_scores(tag, heads, 0, r, r)
                to_tokens((tag, "xr_tok", relations - 1), tokens((A_, B_, C_)[relations - 1]))

                def exps(h):
                    act.wait_ge(dve_done.sem, dve_done.at((tag, "neg_max", h)))
                    for r in range(relations):
                        for t in range(NT):
                            nc.scalar.activation(scores[:, r, t, :], scores[:, r, t, :], ACT.Exp, bias=stat[:, 20 + t:21 + t]).then_inc(
                                act_done.sem, act_done.tick((tag, "exp", h, r, t)))

                exps(0)
                for h in range(heads):
                    for r in range(relations):
                        n = relations * h + r
                        for c in range(NT):
                            dst = weights_t[r] if tag == "rgat1" else weights_t3[:, r]
                            act.wait_ge(bank_full.sem, bank_free.now(1))
                            src = filled()
                            if tag == "rgat1" and c == 0 and h:
                                act.wait_ge(agg_done.sem, agg_done.at((tag, n - relations)))
                            nc.scalar.activation(dst[:, c, :], src[:, :], ACT.Identity).then_inc(
                                bank_free.sem, bank_free.tick((tag, "weights_t", h, r, c)))
                        if h + 1 < heads:
                            edge_scores(tag, heads, h + 1, r, r)
                    if h + 1 < heads:
                        exps(h + 1)
                    if tag == "rgat1":
                        act.wait_ge(agg_done.sem, agg_done.at((tag, relations * h + relations - 1)))
                        for j, (m, part) in enumerate(PIECES[h]):
                            nc.scalar.activation(rgat1_out[part, m, :], bank[4 + 2 * (h % 2) + j][part, :], ACT.Identity,
                                                 bias=cols[part, cols_at["L1_gnn_b1"] + m:cols_at["L1_gnn_b1"] + m + 1]).then_inc(
                                act_done.sem, act_done.tick((tag, "out", h)))
                        for j, (m, part) in enumerate(PIECES[h]):
                            act.wait_ge(dve_done.sem, dve_done.at((tag, "low", h, j)))
                            nc.scalar.activation(EV[part, j, :], EV[part, j, :], ACT.Exp).then_inc(
                                act_done.sem, act_done.tick((tag, "elu_exp", h, j)))
                if tag == "rgat2":
                    for m in range(KC):
                        act.wait_ge(bank_full.sem, bank_free.now(1))
                        src = filled()
                        ev_free(m % 2, ("rgat2_x", m))
                        nc.scalar.activation(EV[:, m % 2, :], src[:, :], ACT.Identity, bias=col("L1_gnn_b2", m)).then_inc(
                                bank_free.sem, bank_free.tick((tag, "out", m)))

            def elu_attention():
                linear("v4", KC, of(chunks(D_)))
                to_tokens("v4_tok", tokens(B_))

                def queries_and_keys(p):
                    own = qk[p % 2]
                    for j, name in enumerate(("eq", "ek")):
                        linear((name, p), 1, lambda m: own[:, j, :])
                        act.wait_ge(dve_done.sem, dve_done.at(("e_low", p, j)))
                        nc.scalar.activation(own[:, 2 + j, :], own[:, 2 + j, :], ACT.Exp).then_inc(
                                act_done.sem, act_done.tick(("e_exp", p, j)))

                queries_and_keys(0)
                for p in range(KC):
                    act.wait_ge(bank_full.sem, bank_free.now(1))
                    nc.scalar.activation(ktok, filled()[:, :].rearrange("p (t f) -> p t f", t=NT), ACT.Identity).then_inc(
                            bank_free.sem, bank_free.tick(("e_ktok", p)))
                    if p + 1 < KC:
                        queries_and_keys(p + 1)
                    act.wait_ge(bank_full.sem, bank_free.now(1))
                    src = filled()
                    for s in range(2):
                        half = slice(64 * s, 64 * s + 64)
                        ins = nc.scalar.activation(kv_diag[half, :, half],
                                                   src[half, 0:2 * P].rearrange("p (j f) -> p j f", j=2)[:, :, half], ACT.Identity)
                        if s == 0:
                            ins.then_inc(act_done.sem, act_done.tick())
                    ins.then_inc(bank_free.sem, bank_free.tick(("e_kv", p)))
                    act.wait_ge(bank_full.sem, bank_free.now(1))
                    nc.scalar.activation(chunks(A_)[:, p, :], filled()[:, :], ACT.Identity).then_inc(
                            bank_free.sem, bank_free.tick(("e_out", p, 0)))
                    act.wait_ge(bank_full.sem, bank_free.now(1))
                    src = filled()
                    ev_free(p % 2, ("e_att", p))
                    nc.scalar.activation(EV[:, p % 2, :], src[:, :], ACT.Identity).then_inc(
                            bank_free.sem, bank_free.tick(("e_out", p, 1)))
                residual("proj2", bias_of("L2_mix_b_proj"))

            def rgcn_layer(tag, layer):
                put_tok = tokens(T_)
                for m in range(KC):
                    act.wait_ge(bank_full.sem, bank_free.now(1))
                    nc.scalar.activation(put_tok[:, :, m * P:(m + 1) * P], filled()[:, :].rearrange("p (t f) -> p t f", t=NT), ACT.Identity).then_inc(
                            bank_free.sem, bank_free.tick(((tag, "tok"), m)))
                for r in range(REL4):
                    linear((tag, "agg", r), KC, of(chunks((A_, B_, C_, D_)[r])))
                if layer is not None:
                    linear((tag, "out"), KC, of(chunks(T_)), ACT.Relu, lambda m: col("L2_gnn_b", layer * KC + m))

            linear("nodes0", KC, of(chunks(A_)), bias=bias_of("L0_gnn_bn"))
            linear("edge_part", KC, of(chunks(D_)))
            for done in spilled:
                act.wait_ge(done, 16)
            with loop(act, "gnn0", 3, (bank_free, act_done)) as layer:
                to_tokens("tok0", tokens(B_))
                linear("agg0", KC, of(chunks(C_)))
                linear("h0", KC, of(chunks(B_)), bias=lambda m: col("L0_gnn_b1", layer * KC + m))
                norm("lnh", chunks(B_))
                for m in range(KC):
                    act.wait_ge(dve_done.sem, dve_done.at(("lnh", m)))
                    nc.scalar.activation(chunks(B_)[:, m, :], chunks(B_)[:, m, :], ACT.Relu, bias=col("L0_gnn_ln_b", layer * KC + m), scale=col("L0_gnn_ln_g", layer * KC + m)).then_inc(
                            act_done.sem, act_done.tick(("relu0", m)))
                linear("w2", KC, of(chunks(C_)), bias=lambda m: col("L0_gnn_b2", layer * KC + m))
            softmax_attention()
            performer96()
            experts_of_one("moe0", "ln1", ACT.Gelu, "L0_ffn_b1")
            norm("ln2", XN)
            performer64()
            act.wait_ge(dve_done.sem, dve_done.at("y_read"))
            rgat(RGAT1)
            rgat(RGAT2)
            norm("ln3", XN)
            linear("f1_up", MF // P, of(chunks(A_)), ACT.Gelu, bias_of("L1_ffn_in_bias"))
            residual("f1")
            norm("ln4", XN)
            elu_attention()
            with loop(act, "rgcn", 2, (bank_free, act_done)) as layer:
                rgcn_layer("rgcn", layer)
            rgcn_layer("rgcnb", None)
            residual("routb", lambda m: col("L2_gnn_b", 2 * KC + m))
            experts_of_one("moe2", "ln5", ACT.Silu, "L2_ffn_b1")

            def graph_attention():
                tag, heads, relations = GAT
                linear("ft", KC, of(chunks(B_)))
                edge_logits(tag, heads, 0)

                def exps(h):
                    act.wait_ge(dve_done.sem, dve_done.at((tag, "neg_max", h)))
                    at = 128 * (h % 2) + 20
                    for t in range(NT):
                        w = scores[:, h % 3, t, :]
                        nc.scalar.activation(w, w, ACT.Exp, bias=stat[:, at + t:at + t + 1]).then_inc(
                            act_done.sem, act_done.tick((tag, "exp", h, 0, t)))

                def aggregated(h):
                    half = slice(64 * (h % 2), 64 * (h % 2) + 64)
                    act.wait_ge(bank_full.sem, bank_free.now(1))
                    nc.scalar.activation(chunks(D_)[half, h // 2, :], filled()[half, :], ACT.Identity).then_inc(
                        bank_free.sem, bank_free.tick((tag, "agg", h)))

                for h in range(2):
                    edge_scores(tag, heads, h, 0, h)
                to_tokens("ft_rows", tokens(A_))
                linear("res", KC, of(chunks(C_)))
                exps(0)
                for h in range(heads):
                    if h + 2 < heads:
                        edge_scores(tag, heads, h + 2, 0, (h + 2) % 3)
                    if h + 1 < heads:
                        exps(h + 1)
                    for c in range(NT):
                        act.wait_ge(bank_full.sem, bank_free.now(1))
                        nc.scalar.activation(weights_g[h % 2][:, c, :], filled()[:, :], ACT.Identity).then_inc(
                            bank_free.sem, bank_free.tick((tag, "weights_t", h, 0, c)))
                    if h:
                        aggregated(h - 1)
                aggregated(heads - 1)

            def feature_mix():
                for j, (name, dst) in enumerate((("xq", A_), ("xk", B_))):
                    for m in range(KC):
                        act.wait_ge(bank_full.sem, bank_free.now(1))
                        nc.scalar.activation(chunks(dst)[:, m, :], filled()[:, :], ACT.Identity, accum_out=stat[:, 6 * j + m:6 * j + m + 1]).then_inc(
                                bank_free.sem, bank_free.tick((name, m)))
                act.wait_ge(dve_done.sem, dve_done.at(("gat_x", KC - 1)))
                linear("xv", KC, of(chunks(C_)))
                act.wait_ge(dve_done.sem, dve_done.at("x_squares"))
                nc.scalar.activation(stat[:, 24:36], stat[:, 12:24], ACT.Sqrt).then_inc(act_done.sem, act_done.tick("x_norms"))
                residual("proj3", bias_of("L3_mix_b_proj"))

            def experts():
                act.wait_ge(dve_done.sem, dve_done.at(("xy", KC - 1)))
                for s in range(XRING):
                    act.dma_start(x_ring[:, s, :], io["experts"][s]).then_inc(x_tile_in[s], 16)
                act.wait_ge(bank_full.sem, bank_free.now(1))
                src = filled()
                nc.scalar.activation(choose[:, 1, :], src[0:NE, :], ACT.Sigmoid)
                nc.scalar.activation(choose[:, 0, :], src[0:NE, :], ACT.Identity).then_inc(
                        bank_free.sem, bank_free.tick("x_logit"))
                for m in range(SHARED // P):
                    act.wait_ge(bank_full.sem, bank_free.now(1))
                    nc.scalar.activation(shared_hidden[:, m, :], filled()[:, :], ACT.Silu).then_inc(
                            bank_free.sem, bank_free.tick(("shared_gate", m)))
                    act.wait_ge(bank_full.sem, bank_free.now(1))
                    src = filled()
                    ev_free(m % 2, ("shared_hidden", m))
                    nc.scalar.activation(EV[:, m % 2, :], src[:, :], ACT.Identity).then_inc(
                            bank_free.sem, bank_free.tick(("shared_up", m)))
                for label, dst in (("slots", slot_of), ("score", score_of)):
                    act.wait_ge(bank_full.sem, bank_free.now(1))
                    nc.scalar.activation(dst[:, :, :], filled()[:, 0:NT * NE].rearrange("p (t e) -> p t e", t=NT), ACT.Identity).then_inc(
                            bank_free.sem, bank_free.tick(("x_" + label, 0)))
                residual("shared")
                to_tokens("x_rows", x_rows)
                act.wait_ge(bank_full.sem, bank_free.now(1))
                nc.scalar.activation(slot_score[:, :], filled()[:, 0:NPAIR * NE], ACT.Identity).then_inc(
                        bank_free.sem, bank_free.tick("x_slot_score"))
                for p in range(NPAIR):
                    act.wait_ge(bank_full.sem, bank_free.now(1))
                    nc.scalar.activation(place_t[:, p, :], filled()[:, :], ACT.Identity).then_inc(
                            bank_free.sem, bank_free.tick(("x_place_t", p)))
                while bank_free.n % NB:
                    own = slice((bank_free.n % NB) * P, (bank_free.n % NB + 1) * P)
                    act.wait_ge(bank_full.sem, bank_free.now(1))
                    nc.scalar.activation(mean[:, own], filled()[:, 0:P], ACT.Identity).then_inc(bank_free.sem, bank_free.tick())
                for n in range(2):
                    ev_free(n, None)
                act.wait_ge(bank_free.sem, bank_free.at("x_slot_score"))
                with loop(act, "pairs", NPAIR, (bank_free, act_done)) as pair:
                    for j in range(2):
                        act.wait_ge(bank_full.sem, bank_free.now(1))
                        nc.scalar.activation(x_pair[:, 3 * j:3 * j + 3, :], filled()[:, 0:3 * P].rearrange("p (c s) -> p c s", c=3),
                                             ACT.Identity).then_inc(bank_free.sem, bank_free.tick(("x_gather", j)))

                    for b in range(FB):
                        act.wait_ge(bank_full.sem, bank_free.now(1))
                        nc.scalar.activation(x_hidden[:, b, :], filled()[:, :], ACT.Silu).then_inc(
                            bank_free.sem, bank_free.tick(("x_gate", b)))
                        act.wait_ge(bank_full.sem, bank_free.now(1))
                        src = filled()
                        if b >= 2:
                            act.wait_ge(dve_done.sem, dve_done.at(("x_h", b - 2)))
                        nc.scalar.activation(EV[:, b % 2, :], src[:, :], ACT.Identity).then_inc(
                            bank_free.sem, bank_free.tick(("x_up", b)))
                    for b in range(FB):
                        act.wait_ge(bank_full.sem, bank_free.now(1))
                        nc.scalar.activation(x_hidden_t[:, 4 * b:4 * b + 4, :], filled()[:, :].rearrange("p (c s) -> p c s", c=4),
                                             ACT.Identity).then_inc(bank_free.sem, bank_free.tick(("x_h_t", b)))
                    for half in range(2):
                        act.wait_ge(bank_full.sem, bank_free.now(1))
                        act.wait_ge(dve_done.sem, dve_done.at("pair_score"))
                        nc.scalar.activation(x_out[:, half * (D // 2):(half + 1) * (D // 2)], filled()[:, 0:D // 2], ACT.Identity,
                                             scale=pair_score[:, :]).then_inc(bank_free.sem, bank_free.tick(("x_down", half)))
                    for m in range(KC):
                        act.wait_ge(bank_full.sem, bank_free.now(1))
                        act.wait_ge(dve_done.sem, dve_done.at(("experts_x", m - 2) if m >= 2 else ("experts_x", m + KC - 2), m < 2))
                        nc.scalar.activation(x_back[m % 2], filled()[:, :], ACT.Identity).then_inc(
                                bank_free.sem, bank_free.tick(("experts", m)))

            norm("ln6", XN)
            graph_attention()
            feature_mix()
            norm("ln7", XN)
            experts()

        @block.vector
        def _(dve):
            v = nc.vector

            def add_up(label, x, m):
                if 1 <= m < KC - 1:
                    dve.wait_ge(dve_done.sem, dve_done.now())
                    v.tensor_tensor(mean[:, :], x[:, 0, :] if m == 1 else mean[:, :], x[:, m, :], ALU.add).then_inc(
                        dve_done.sem, dve_done.tick((label, "part")))

            def norm(label, src, dst):
                dve.wait_ge(agg_done.sem, agg_done.at((label, "sum")))
                for k in range(KC):
                    v.scalar_tensor_tensor(dst[:, k, :], bank[7][:, :], -1.0 / D, src[:, k, :], ALU.mult, ALU.add).then_inc(
                        dve_done.sem, dve_done.tick((label, "d", k)))
                dve.wait_ge(act_done.sem, act_done.at((label, "std")))
                v.reciprocal(rstd[:, :], rstd[:, :]).then_inc(dve_done.sem, dve_done.tick())
                dve.wait_ge(dve_done.sem, dve_done.now())
                for k in range(KC):
                    v.tensor_tensor(dst[:, k, :], dst[:, k, :], rstd[:, :], ALU.mult).then_inc(
                            dve_done.sem, dve_done.tick((label, k)))

            def residual(label, full=None, before=None):
                for m in range(KC):
                    dve.wait_ge(bank_free.sem, bank_free.at((full or label, m)))
                    v.tensor_tensor(XT[:, m, :], XT[:, m, :], EV[:, m % 2, :], ALU.add).then_inc(
                            dve_done.sem, dve_done.tick((label + "_x", m)))
                    if before:
                        add_up(before, XT, m)

            dve.wait_ge(pool_done.sem, pool_done.at("consts"))
            dve.wait_ge(edge_in, 64)
            v.tensor_copy(iota_f, iota_i).then_inc(dve_done.sem, dve_done.tick())
            v.tensor_copy(slot_iota[:, :], iota_i[:, 0:CAP]).then_inc(dve_done.sem, dve_done.tick())
            v.tensor_copy(edge_f[:, 0:2, :], edge_i[:, 0:2, :]).then_inc(dve_done.sem, dve_done.tick())
            for p, (first, second) in enumerate(PACKED):
                kinds = edge_i[:, 3 if p < 2 else 2, :]
                v.tensor_scalar(edge_f[:, 2 + p, :], kinds, float(second), float(PACK), ALU.is_equal, ALU.mult).then_inc(
                    dve_done.sem, dve_done.tick())
                v.tensor_scalar(edge_f[:, 5, :], kinds, float(first), None, ALU.is_equal).then_inc(dve_done.sem, dve_done.tick())
                dve.wait_ge(dve_done.sem, dve_done.now())
                v.tensor_tensor(edge_f[:, 2 + p, :], edge_f[:, 2 + p, :], edge_f[:, 5, :], ALU.add).then_inc(
                    dve_done.sem, dve_done.tick())
                dve.wait_ge(dve_done.sem, dve_done.now())

            def key(n, c):
                if isinstance(c, int):
                    return edge_f[:, n, c:c + 1]
                return edge_f[:, n, bass.ds(c, 1)]

            def feature_rows(c, b):
                return v.tensor_scalar(onehot32[:, b, :], iota_f, key(1, c), None, ALU.is_equal)

            for b in range(4):
                feature_rows(b, b).then_inc(onehot_ready, 1)
            dve.wait_ge(x_in, 16)
            for m in range(KC):
                add_up("ln0", XT, m)
            norm("ln0", XT, XN)
            with dve.Fori(1, EC // 4) as i:
                for b in range(4):
                    dve.wait_ge(onehot_used, i * 4 + (b - 3))
                    feature_rows(i * 4 + b, b).then_inc(onehot_ready, 1)

            for p in range(len(PACKED)):
                before = EC * (p + 1)
                a, b_ = (0, 1) if p < 2 else (1, 0)
                with dve.Fori(0, EC // 4) as i:
                    for b in range(4):
                        dve.wait_ge(onehot_used, i * 4 + (before + b - 3))
                        v.tensor_scalar(onehot_a[:, b, :], iota_f, key(a, i * 4 + b), None, ALU.is_equal)
                        v.tensor_scalar(onehot_b[:, b, :], iota_f, key(b_, i * 4 + b), key(2 + p, i * 4 + b),
                                        ALU.is_equal, ALU.mult).then_inc(onehot_ready, 1)
            for r in range(REL4):
                dve.wait_ge(bank_free.sem, bank_free.at(("degree", r)))
                if r == 0:
                    v.tensor_copy(EV[:, 1, :], degree[r]).then_inc(dve_done.sem, dve_done.tick())
                else:
                    v.tensor_tensor(EV[:, 1, :], EV[:, 1, :], degree[r], ALU.add).then_inc(dve_done.sem, dve_done.tick())
                dve.wait_ge(dve_done.sem, dve_done.now())
                v.tensor_scalar(degree[r], degree[r], 1.0, None, ALU.max).then_inc(dve_done.sem, dve_done.tick())
                dve.wait_ge(dve_done.sem, dve_done.now())
                v.reciprocal(degree[r], degree[r]).then_inc(dve_done.sem, dve_done.tick())
                dve.wait_ge(dve_done.sem, dve_done.now())
                v.tensor_tensor(fresh[r], fresh[r], degree[r].rearrange("p (a n) -> p a n", a=1).to_broadcast([P, NT, N]), ALU.mult).then_inc(
                    dve_done.sem, dve_done.tick(("norm", r)))
            dve.wait_ge(dve_done.sem, dve_done.now())
            dve.wait_ge(bank_free.sem, bank_free.at(("count_t", NT - 1)))
            for c in range(NT):
                own = slice(c * P, (c + 1) * P)
                v.tensor_tensor(EV[:, 0, own], ident[:, :], EV[:, 1, own], ALU.mult).then_inc(dve_done.sem, dve_done.tick())
            dve.wait_ge(dve_done.sem, dve_done.now())
            for c in range(NT):
                own = slice(c * P, (c + 1) * P)
                v.tensor_tensor(cnt[3][:, c, own], cnt[3][:, c, own], EV[:, 0, own], ALU.add).then_inc(
                        dve_done.sem, dve_done.tick("counts_looped"))
            dve.wait_ge(dve_done.sem, dve_done.now())
            dve.wait_ge(cols_in, 16)

            def softmax_attention():
                s = float(D8) ** -0.5
                for h in range(H8):
                    for t in range(NT):
                        dve.wait_ge(bank_full.sem, bank_full.at(("scores", h, t)))
                        j = bank_full.at(("scores", h, t)) - 1
                        v.reduce_max(stat[:, t:t + 1], bank[j % NB][:, :], axis=AX.X).then_inc(dve_done.sem, dve_done.tick())
                        dve.wait_ge(dve_done.sem, dve_done.now())
                        v.tensor_scalar(stat[:, 4 + t:5 + t], stat[:, t:t + 1], -s, None, ALU.mult).then_inc(
                                dve_done.sem, dve_done.tick(("neg_max", h, t)))
                    for t in range(NT):
                        dve.wait_ge(bank_free.sem, bank_free.at(("exp", h, t)))
                    v.reciprocal(stat[:, 12:16], stat[:, 8:12]).then_inc(dve_done.sem, dve_done.tick())
                    dve.wait_ge(dve_done.sem, dve_done.now())
                    for t in range(NT):
                        v.tensor_scalar(probs[:, t, :], probs[:, t, :], stat[:, 12 + t:13 + t], None, ALU.mult).then_inc(
                                dve_done.sem, dve_done.tick(("probs", h)))
                for m in range(KC):
                    dve.wait_ge(bank_free.sem, bank_free.at(("wo", m)))
                    v.tensor_tensor(EV[:, m % 2, :], EV[:, m % 2, :], chunks(A_)[:, m, :], ALU.add).then_inc(
                            dve_done.sem, dve_done.tick())
                    dve.wait_ge(dve_done.sem, dve_done.now())
                    v.tensor_tensor(XT[:, m, :], XT[:, m, :], EV[:, m % 2, :], ALU.add).then_inc(
                            dve_done.sem, dve_done.tick(("wo_x", m)))

            def divide(out, den, label):
                dve.wait_ge(dve_done.sem, dve_done.now())
                v.reciprocal(den, den).then_inc(dve_done.sem, dve_done.tick())
                dve.wait_ge(dve_done.sem, dve_done.now())
                v.tensor_tensor(out, out, den, ALU.mult).then_inc(dve_done.sem, dve_done.tick(label))

            def performer96():
                for h in range(H8):
                    dve.wait_ge(bank_free.sem, bank_free.at(("m_out", h, 1)))
                    v.tensor_scalar(EV[0:D8, h % 2, :], EV[0:D8, h % 2, :], 1e-6, None, ALU.max).then_inc(
                            dve_done.sem, dve_done.tick())
                    divide(att96[:, h, :], EV[0:D8, h % 2, :], ("m_att", h))
                residual("proj0", before="ln1")

            def experts_of_one(tag, ln, after):
                norm(ln, XT, XN)
                dve.wait_ge(bank_free.sem, bank_free.at((tag, "logit")))
                top, total = stat[:, 0:NT], stat[:, 8:8 + NT]
                wide = lambda x: x.rearrange("p (t a) -> p t a", a=1).to_broadcast([P, NT, ME])
                v.reduce_max(top, logit[:, :, :], axis=AX.X).then_inc(dve_done.sem, dve_done.tick())
                dve.wait_ge(dve_done.sem, dve_done.now())
                v.tensor_tensor(gate_exp[:, :, :], logit[:, :, :], wide(top), ALU.subtract).then_inc(
                        dve_done.sem, dve_done.tick())
                dve.wait_ge(dve_done.sem, dve_done.now())
                v.tensor_scalar(comb[:, :, :], gate_exp[:, :, :], 0.0, None, ALU.is_equal).then_inc(
                        dve_done.sem, dve_done.tick((tag, "shifted")))
                dve.wait_ge(dve_done.sem, dve_done.now())
                for t in range(NT):
                    v.tensor_tensor(comb[:, t, :], comb[:, t, :], down8[:, :], ALU.mult).then_inc(dve_done.sem, dve_done.tick())
                dve.wait_ge(dve_done.sem, dve_done.now())
                v.reduce_max(top, comb[:, :, :], axis=AX.X).then_inc(dve_done.sem, dve_done.tick())
                dve.wait_ge(dve_done.sem, dve_done.now())
                v.tensor_tensor(comb[:, :, :], comb[:, :, :], wide(top), ALU.is_equal).then_inc(dve_done.sem, dve_done.tick())
                dve.wait_ge(act_done.sem, act_done.at((tag, "exp")))
                v.reduce_sum(total, gate_exp[:, :, :], axis=AX.X).then_inc(dve_done.sem, dve_done.tick())
                dve.wait_ge(dve_done.sem, dve_done.now())
                v.reciprocal(total, total).then_inc(dve_done.sem, dve_done.tick())
                dve.wait_ge(dve_done.sem, dve_done.now())
                v.tensor_tensor(comb[:, :, :], comb[:, :, :], wide(total), ALU.mult).then_inc(
                        dve_done.sem, dve_done.tick((tag, "comb")))
                for e in range(ME):
                    dve.wait_ge(bank_free.sem, bank_free.at((tag, "scale", e)))
                for m in range(ME * MF // P):
                    part, start = ("up0", 0) if m < LEAD else ("up1", LEAD) if m < LEAD + KC else ("up2", LEAD + KC)
                    dve.wait_ge(bank_free.sem, bank_free.at(((tag, part), m - start)))
                    v.tensor_tensor(hidden[:, m, :], hidden[:, m, :], scale_row[:, m * P // MF, :], ALU.mult).then_inc(
                            dve_done.sem, dve_done.tick(((tag, "hidden"), m)))
                residual(tag, before=after)

            def performer64():
                for p in range(KC):
                    dve.wait_ge(bank_free.sem, bank_free.at(("n_out", p, 1)))
                    v.tensor_scalar(EV[:, p % 2, :], EV[:, p % 2, :], 1e-6, None, ALU.add).then_inc(dve_done.sem, dve_done.tick())
                    divide(chunks(A_)[:, p, :], EV[:, p % 2, :], ("n_att", p))
                Y = chunks(C_)
                for m in range(KC):
                    dve.wait_ge(bank_free.sem, bank_free.at(("proj1", m)))
                    v.tensor_tensor(Y[:, m, :], Y[:, m, :], XN[:, m, :], ALU.add).then_inc(dve_done.sem, dve_done.tick(("y", m)))
                    add_up("lny", Y, m)
                norm("lny", Y, Y)
                dve.wait_ge(dve_done.sem, dve_done.now())
                for m in range(KC):
                    v.scalar_tensor_tensor(XT[:, m, :], Y[:, m, :], col("L1_mix_gamma", m), XT[:, m, :], ALU.mult, ALU.add).then_inc(
                            dve_done.sem, dve_done.tick("y_read"))
                dve.wait_ge(dve_done.sem, dve_done.now())
                for m in range(KC):
                    v.tensor_scalar(XT[:, m, :], XT[:, m, :], col("L1_mix_beta", m), None, ALU.add).then_inc(
                            dve_done.sem, dve_done.tick())

            def edge_max(tag, h, relations, buf, at):
                top = stat[:, at:at + 3 * NT].rearrange("p (t r) -> p t r", t=NT)
                for r in range(relations):
                    dve.wait_ge(bank_free.sem, bank_free.at((tag, "row", h, r)))
                    wide = scores[:, buf + r, :, :]
                    v.scalar_tensor_tensor(wide, wide, 0.2, wide, ALU.mult, ALU.max).then_inc(dve_done.sem, dve_done.tick())
                    dve.wait_ge(dve_done.sem, dve_done.now())
                    for t in range(NT):
                        s = scores[:, buf + r, t, :]
                        v.tensor_tensor_reduce(out=s, in0=s, in1=mask[r][:, t, :], scale=1.0, scalar=-3e38,
                                                    op0=ALU.add, op1=ALU.max, accum_out=top[:, t, r:r + 1]).then_inc(
                                                            dve_done.sem, dve_done.tick())
                dve.wait_ge(dve_done.sem, dve_done.now())
                v.reduce_max(stat[:, at + 16:at + 16 + NT], top[:, :, 0:relations], axis=AX.X).then_inc(
                        dve_done.sem, dve_done.tick())
                dve.wait_ge(dve_done.sem, dve_done.now())
                v.tensor_scalar(stat[:, at + 20:at + 20 + NT], stat[:, at + 16:at + 16 + NT], -1.0, None, ALU.mult).then_inc(
                        dve_done.sem, dve_done.tick((tag, "neg_max", h)))

            def edge_weights(tag, h, relations, buf, counts, eps_add, at):
                z = stat[:, at + 24:at + 24 + 3 * NT].rearrange("p (t r) -> p t r", t=NT)
                total, inverse = stat[:, at + 36:at + 36 + NT], stat[:, at + 40:at + 40 + NT]
                for r in range(relations):
                    for t in range(NT):
                        dve.wait_ge(act_done.sem, act_done.at((tag, "exp", h, r, t)))
                        s = scores[:, buf + r, t, :]
                        v.tensor_tensor_reduce(out=s, in0=s, in1=counts[r][:, t, :], scale=1.0, scalar=0.0,
                                                    op0=ALU.mult, op1=ALU.add, accum_out=z[:, t, r:r + 1]).then_inc(
                                                            dve_done.sem, dve_done.tick())
                dve.wait_ge(dve_done.sem, dve_done.now())
                v.reduce_sum(total, z[:, :, 0:relations], axis=AX.X).then_inc(dve_done.sem, dve_done.tick())
                dve.wait_ge(dve_done.sem, dve_done.now())
                op, by = (ALU.add, 1e-16) if eps_add else (ALU.max, 1e-30)
                v.tensor_scalar(total, total, by, None, op).then_inc(dve_done.sem, dve_done.tick())
                dve.wait_ge(dve_done.sem, dve_done.now())
                v.reciprocal(inverse, total).then_inc(dve_done.sem, dve_done.tick())
                dve.wait_ge(dve_done.sem, dve_done.now())
                if h >= 2:
                    dve.wait_ge(bank_free.sem, bank_free.at((tag, "weights_t", h - 2, relations - 1, NT - 1)))
                for t in range(NT):
                    v.tensor_scalar(diag[h % 2][:, t, :], ident[:, :], inverse[:, t:t + 1], None, ALU.mult).then_inc(
                        dve_done.sem, dve_done.tick((tag, "diag", h)))

            def no_edge(r):
                v.tensor_scalar(mask[r], cnt[r], 0.0, -BIG, ALU.is_equal, ALU.mult).then_inc(dve_done.sem, dve_done.tick())

            def rgat(which):
                tag, heads, relations = which
                edge_max(tag, 0, relations, 0, 0)
                edge_weights(tag, 0, relations, 0, cnt, True, 0)
                for h in range(heads):
                    if h + 1 < heads:
                        edge_max(tag, h + 1, relations, 0, 0)
                        edge_weights(tag, h + 1, relations, 0, cnt, True, 0)
                    if tag == "rgat1":
                        dve.wait_ge(act_done.sem, act_done.at((tag, "out", h)))
                        dve.wait_ge(dve_done.sem, dve_done.now())
                        for j, (m, part) in enumerate(PIECES[h]):
                            v.tensor_scalar(EV[part, j, :], rgat1_out[part, m, :], 0.0, None, ALU.min).then_inc(
                                dve_done.sem, dve_done.tick((tag, "low", h, j)))
                        for j, (m, part) in enumerate(PIECES[h]):
                            x = rgat1_out[part, m, :]
                            dve.wait_ge(act_done.sem, act_done.at((tag, "elu_exp", h, j)))
                            v.tensor_scalar(EV[part, j, :], EV[part, j, :], -1.0, None, ALU.add).then_inc(
                                    dve_done.sem, dve_done.tick())
                            dve.wait_ge(dve_done.sem, dve_done.now())
                            v.scalar_tensor_tensor(x, x, 0.0, EV[part, j, :], ALU.max, ALU.add).then_inc(
                                dve_done.sem, dve_done.tick((tag, "elu", m)))

            def elu_attention():
                def queries_and_keys(p):
                    own = qk[p % 2]
                    for j, name in enumerate(("eq", "ek")):
                        dve.wait_ge(bank_free.sem, bank_free.at(((name, p), 0)))
                        v.tensor_scalar(own[:, 2 + j, :], own[:, j, :], 0.0, None, ALU.min).then_inc(
                                dve_done.sem, dve_done.tick(("e_low", p, j)))
                    for j in range(2):
                        dve.wait_ge(act_done.sem, act_done.at(("e_exp", p, j)))
                        v.scalar_tensor_tensor(own[:, j, :], own[:, j, :], 0.0, own[:, 2 + j, :], ALU.max, ALU.add).then_inc(
                                dve_done.sem, dve_done.tick(("e_q" if j == 0 else "e_k", p)))

                queries_and_keys(0)
                for p in range(KC):
                    if p + 1 < KC:
                        queries_and_keys(p + 1)
                    dve.wait_ge(bank_free.sem, bank_free.at(("e_out", p, 1)))
                    divide(chunks(A_)[:, p, :], EV[:, p % 2, :], ("e_att", p))
                residual("proj2")

            for j, name in enumerate(("L0_mix_bq", "L0_mix_bk")):
                at = cols_at[name]
                v.tensor_scalar(stat[0:D8, 32 + 8 * j:40 + 8 * j], cols[0:D8, at:at + H8], float(D8) ** -0.5, None, ALU.mult).then_inc(
                        dve_done.sem, dve_done.tick("scaled_bias"))
            for m in range(KC):
                dve.wait_ge(bank_free.sem, bank_free.at(("edge_part", m)))
                v.scalar_tensor_tensor(chunks(D_)[:, m, :], EV[:, 1, :], col("L0_gnn_be", m), chunks(D_)[:, m, :],
                                            ALU.mult, ALU.add).then_inc(dve_done.sem, dve_done.tick())
            dve.wait_ge(dve_done.sem, dve_done.now())
            with loop(dve, "gnn0", 3, (dve_done,)):
                for m in range(KC):
                    dve.wait_ge(bank_free.sem, bank_free.at(("agg0", m)))
                    v.tensor_tensor(chunks(C_)[:, m, :], chunks(C_)[:, m, :], chunks(D_)[:, m, :], ALU.add).then_inc(
                            dve_done.sem, dve_done.tick(("agg0_sum", m)))
                for m in range(KC - 1):
                    dve.wait_ge(bank_free.sem, bank_free.at(("h0", m)))
                    add_up("lnh", chunks(B_), m)
                norm("lnh", chunks(B_), chunks(B_))
                for m in range(KC):
                    dve.wait_ge(bank_free.sem, bank_free.at(("w2", m)))
                    v.tensor_tensor(chunks(A_)[:, m, :], chunks(A_)[:, m, :], chunks(C_)[:, m, :], ALU.add).then_inc(
                            dve_done.sem, dve_done.tick(("nodes", m)))
            softmax_attention()
            performer96()
            experts_of_one("moe0", "ln1", "ln2")
            norm("ln2", XT, XN)
            performer64()
            dve.wait_ge(pool_done.sem, pool_done.at("counts"))
            for r in range(REL3):
                no_edge(r)
            dve.wait_ge(dve_done.sem, dve_done.now())
            rgat(RGAT1)
            rgat(RGAT2)
            for m in range(KC):
                dve.wait_ge(bank_free.sem, bank_free.at(("rgat2", "out", m)))
                v.tensor_tensor(XT[:, m, :], XT[:, m, :], EV[:, m % 2, :], ALU.add).then_inc(
                        dve_done.sem, dve_done.tick(("rgat2_x", m)))
                add_up("ln3", XT, m)
            v.tensor_copy(stat[:, 0:1], stat[:, 1:2]).then_inc(dve_done.sem, dve_done.tick("rgat2_last"))
            norm("ln3", XT, XN)
            residual("f1", before="ln4")
            norm("ln4", XT, XN)
            elu_attention()
            with loop(dve, "rgcn", 2, (dve_done,)):
                dve.wait_ge(bank_free.sem, bank_free.at((("rgcn", "out"), KC - 1)))
                for m in range(KC):
                    v.tensor_copy(XN[:, m, :], chunks(T_)[:, m, :]).then_inc(dve_done.sem, dve_done.tick((("rgcn", "x"), m)))
            residual("routb", before="ln5")
            experts_of_one("moe2", "ln5", "ln6")
            def graph_attention():
                tag, heads, relations = GAT
                dve.wait_ge(reloaded[1], 16)
                no_edge(0)
                dve.wait_ge(dve_done.sem, dve_done.now())

                def joined(m):
                    x = chunks(D_)[:, m, :]
                    dve.wait_ge(bank_free.sem, bank_free.at((tag, "agg", 2 * m + 1)))
                    v.tensor_tensor(x, x, chunks(C_)[:, m, :], ALU.add).then_inc(dve_done.sem, dve_done.tick())
                    dve.wait_ge(dve_done.sem, dve_done.now())
                    v.scalar_tensor_tensor(XT[:, m, :], x, 0.0, XT[:, m, :], ALU.max, ALU.add).then_inc(
                        dve_done.sem, dve_done.tick(("gat_x", m)))

                edge_max(tag, 0, 1, 0, 0)
                for h in range(heads):
                    if h + 1 < heads:
                        edge_max(tag, h + 1, 1, (h + 1) % 3, 128 * ((h + 1) % 2))
                    edge_weights(tag, h, 1, h % 3, cnt, False, 128 * (h % 2))
                    if h % 2 and h > 2:
                        joined(h // 2 - 1)
                joined(KC - 1)

            def feature_mix():
                q, k, val, kk, y = chunks(A_), chunks(B_), chunks(C_), chunks(D_), chunks(T_)
                dve.wait_ge(dve_done.sem, dve_done.now())
                for j, (name, x, dst) in enumerate((("xq", q, y), ("xk", k, kk))):
                    for m in range(KC):
                        dve.wait_ge(bank_free.sem, bank_free.at((name, m)))
                        at = 12 + 6 * j + m
                        v.tensor_tensor_reduce(out=dst[:, m, :], in0=x[:, m, :], in1=x[:, m, :], scale=1.0, scalar=0.0,
                                                    op0=ALU.mult, op1=ALU.add, accum_out=stat[:, at:at + 1]).then_inc(
                                                            dve_done.sem, dve_done.tick("x_squares"))
                dve.wait_ge(dve_done.sem, dve_done.now())
                for m in range(KC):
                    v.tensor_tensor(q[:, m, :], q[:, m, :], kk[:, m, :], ALU.mult).then_inc(dve_done.sem, dve_done.tick())
                dve.wait_ge(act_done.sem, act_done.at("x_norms"))
                nq, nk, sums, both, coef = (stat[:, a:a + KC] for a in (24, 30, 36, 42, 48))
                v.tensor_tensor(sums, stat[:, 0:6], stat[:, 6:12], ALU.mult).then_inc(dve_done.sem, dve_done.tick())
                v.tensor_tensor(both, nq, nk, ALU.mult).then_inc(dve_done.sem, dve_done.tick())
                dve.wait_ge(dve_done.sem, dve_done.now())
                v.reciprocal(coef, both).then_inc(dve_done.sem, dve_done.tick())
                dve.wait_ge(dve_done.sem, dve_done.now())
                v.tensor_tensor(sums, sums, coef, ALU.mult).then_inc(dve_done.sem, dve_done.tick())
                dve.wait_ge(dve_done.sem, dve_done.now())
                v.tensor_scalar(sums, sums, float(N), None, ALU.add).then_inc(dve_done.sem, dve_done.tick())
                dve.wait_ge(dve_done.sem, dve_done.now())
                v.tensor_tensor(sums, sums, both, ALU.mult).then_inc(dve_done.sem, dve_done.tick())
                dve.wait_ge(dve_done.sem, dve_done.now())
                v.tensor_tensor(sums, sums, nk, ALU.mult).then_inc(dve_done.sem, dve_done.tick())
                dve.wait_ge(dve_done.sem, dve_done.now())
                v.reciprocal(coef, sums).then_inc(dve_done.sem, dve_done.tick())
                dve.wait_ge(dve_done.sem, dve_done.now())
                for m in range(KC):
                    dve.wait_ge(bank_free.sem, bank_free.at(("xv", m)))
                    v.scalar_tensor_tensor(y[:, m, :], val[:, m, :], coef[:, m:m + 1], q[:, m, :], ALU.mult, ALU.mult).then_inc(
                            dve_done.sem, dve_done.tick(("xy", m)))
                residual("proj3", before="ln7")

            def experts():
                logits, taken, ranks = choose[:, 0, :], choose[:, 2, :], choose[:, 3, :]
                dve.wait_ge(bank_free.sem, bank_free.at("x_logit"))
                v.tensor_scalar(logits, logits, 17.33, -103.97, ALU.min, ALU.max).then_inc(dve_done.sem, dve_done.tick())
                v.memset(ranks, 1.0).then_inc(dve_done.sem, dve_done.tick())
                dve.wait_ge(dve_done.sem, dve_done.now())
                for n in range(CAP // 8):
                    v.max(stat[0:NE, 0:8], logits).then_inc(dve_done.sem, dve_done.tick())
                    dve.wait_ge(dve_done.sem, dve_done.now())
                    v.match_replace(logits, stat[0:NE, 0:8], logits, -BIG).then_inc(dve_done.sem, dve_done.tick())
                    dve.wait_ge(dve_done.sem, dve_done.now())
                v.tensor_scalar(taken, logits, -BIG, None, ALU.is_equal).then_inc(dve_done.sem, dve_done.tick())
                dve.wait_ge(dve_done.sem, dve_done.now())
                v.tensor_tensor_scan(logits, ranks, taken, 0.0, ALU.mult, ALU.add).then_inc(dve_done.sem, dve_done.tick())
                dve.wait_ge(dve_done.sem, dve_done.now())
                v.tensor_tensor(taken, taken, logits, ALU.mult).then_inc(dve_done.sem, dve_done.tick())
                dve.wait_ge(dve_done.sem, dve_done.now())
                v.tensor_scalar(taken, taken, -1.0, None, ALU.add).then_inc(dve_done.sem, dve_done.tick("x_slots"))
                for m in range(SHARED // P):
                    dve.wait_ge(bank_free.sem, bank_free.at(("shared_up", m)))
                    v.tensor_tensor(shared_hidden[:, m, :], shared_hidden[:, m, :], EV[:, m % 2, :], ALU.mult).then_inc(
                            dve_done.sem, dve_done.tick(("shared_hidden", m)))
                dve.wait_ge(bank_free.sem, bank_free.at(("x_slots", 0)))
                for t in range(NT):
                    slots = place[:, t, :].rearrange("p (e s) -> p e s", e=NE)
                    v.tensor_tensor(slots, slot_iota[:, :].rearrange("p (a s) -> p a s", a=1).to_broadcast([P, NE, CAP]),
                                         slot_of[:, t, :].rearrange("p (e a) -> p e a", a=1).to_broadcast([P, NE, CAP]), ALU.is_equal).then_inc(
                                                 dve_done.sem, dve_done.tick("x_place"))
                residual("shared")
                dve.wait_ge(bank_free.sem, bank_free.at("x_slot_score"))
                with loop(dve, "pairs", NPAIR, (dve_done,)) as pair:
                    for e in range(2):
                        rows = slice(CAP * e, CAP * e + CAP)
                        v.tensor_copy(pair_score[rows, :], slot_score[rows, bass.ds(pair * (NE + 2) + e, 1)]).then_inc(
                            dve_done.sem, dve_done.tick("pair_score"))
                    for b in range(FB):
                        dve.wait_ge(bank_free.sem, bank_free.at(("x_up", b)))
                        v.tensor_tensor(x_hidden[:, b, :], x_hidden[:, b, :], EV[:, b % 2, :], ALU.mult).then_inc(
                            dve_done.sem, dve_done.tick(("x_h", b)))
                    dve.wait_ge(dve_done.sem, dve_done.now())
                    for m in range(KC):
                        dve.wait_ge(bank_free.sem, bank_free.at(("experts", m)))
                        v.tensor_tensor(XT[:, m, :], XT[:, m, :], x_back[m % 2], ALU.add).then_inc(
                            dve_done.sem, dve_done.tick(("experts_x", m)))

            norm("ln6", XT, XN)
            graph_attention()
            feature_mix()
            norm("ln7", XT, XN)
            experts()
            dve.wait_ge(dve_done.sem, dve_done.now())
            v.tensor_copy(stat[:, 0:1], stat[:, 0:1]).then_inc(dve_done.sem, dve_done.tick("result"))



def by_chunk(a, width=P):
    k, n = a.shape
    out = np.zeros((P, k // width, n), np.float32)
    out[:width] = a.reshape(k // width, width, n).transpose(1, 0, 2)
    return out


def weight_tiles(w, width_out=P, rows=P, rest=None):
    k, n = w.shape
    blocks = k // rows
    per = H8 if rows == D8 else min(KC, blocks)
    v = by_chunk(w, rows).reshape(P, blocks // per, per, n // width_out, width_out).transpose(3, 1, 0, 2, 4)
    out = np.zeros((n // width_out, blocks // per, P, SLOT), np.float32)
    out[..., :per * width_out] = v.reshape(n // width_out, blocks // per, P, per * width_out)
    if rest is not None:
        r = rest.reshape(rest.shape[0], n // width_out, width_out).transpose(1, 0, 2)
        out[:, -1, :rest.shape[0], KC * P:KC * P + width_out] = r
    return out.reshape(-1, P, SLOT)


def interleave(parts):
    per = [p.reshape(KC, -1, P, SLOT) for p in parts]
    return np.concatenate(per, axis=1).reshape(-1, P, SLOT)


def weight_stream(a):
    out = []
    out.append(weight_tiles(a["L0_gnn_Wn"].T))
    out.append(weight_tiles(a["L0_gnn_We"].T))
    for l in range(3):
        out.append(weight_tiles(a["L0_gnn_W1"][l].T))
        out.append(weight_tiles(a["L0_gnn_W2"][l].T))
    qkv = a["L0_gnn_Wqkv"].T
    out.append(weight_tiles(qkv[:, 2 * D:]))
    q, k = weight_tiles(qkv[:, :D], D8), weight_tiles(qkv[:, D:2 * D], D8)
    out.append(np.stack([q, k], 1).reshape(-1, P, SLOT))
    out.append(weight_tiles(a["L0_gnn_Wo"].T, P, D8))
    qkv = a["L0_mix_qkv_w"].T
    out.append(weight_tiles(qkv[:, 2 * D:]))
    q, k = weight_tiles(qkv[:, :D], D8), weight_tiles(qkv[:, D:2 * D], D8)
    out.append(np.stack([q, k], 1).reshape(-1, P, SLOT))
    out.append(weight_tiles(a["L0_mix_proj_w"].T, P, D8))
    out += moe_tiles(a, "L0_ffn")
    qkv = a["L1_mix_W_qkv"]
    out.append(weight_tiles(qkv[:, 2 * D:]))
    q, k = weight_tiles(qkv[:, :D]), weight_tiles(qkv[:, D:2 * D])
    out.append(np.stack([q, k], 1).reshape(-1, P, SLOT))
    out.append(weight_tiles(a["L1_mix_W_proj"]))
    out += [weight_tiles(w) for w in a["L1_gnn_W1"]]
    out += [weight_tiles(w) for w in a["L1_gnn_W2"]]
    out.append(weight_tiles(a["L1_ffn_in_weight"].T))
    out.append(weight_tiles(a["L1_ffn_out_weight"]))
    qkv = a["L2_mix_w_qkv"]
    out.append(weight_tiles(qkv[:, 2 * D:]))
    q, k = weight_tiles(qkv[:, :D]), weight_tiles(qkv[:, D:2 * D])
    out.append(np.stack([q, k], 1).reshape(-1, P, SLOT))
    out.append(weight_tiles(a["L2_mix_w_proj"]))
    for l in "123":
        out.append(interleave([weight_tiles(a["L2_gnn_root" + l])] + [weight_tiles(w) for w in a["L2_gnn_W" + l]]))
    out += moe_tiles(a, "L2_ffn")
    out += late_tiles(a)
    out = np.concatenate(out)
    pad = -len(out) % RING
    return np.concatenate([out, np.zeros((pad, P, SLOT), np.float32)]) if pad else out


def moe_tiles(a, name):
    up = a[name + "_W1"].transpose(1, 0, 2).reshape(D, ME * MF)
    return [weight_tiles(up), weight_tiles(a[name + "_W2"].reshape(ME * MF, D), rest=a[name + "_b2"])]


def late_tiles(a):
    out = []
    qkv = a["L3_mix_w_qkv"]
    out += [weight_tiles(qkv[:, n * D:(n + 1) * D]) for n in range(3)] + [weight_tiles(a["L3_mix_w_proj"])]
    gate, up = weight_tiles(a["L3_ffn_Ws_g"].T), weight_tiles(a["L3_ffn_Ws_u"].T)
    out += [np.stack([gate, up], 1).reshape(-1, P, SLOT), weight_tiles(a["L3_ffn_Ws_d"].T)]
    return out


def expert_tiles(a):
    flat = np.empty((NPAIR, 36, P, XSLOT), np.float32)
    up = flat[:, :24].reshape(NPAIR, FB, 2, 2, P, KC, 512)
    for n, name in enumerate(("L3_ffn_Wg", "L3_ffn_Wu")):
        w = a[name].reshape(NPAIR, 2, FB, 512, KC, P)
        up[:, :, n] = w.transpose(0, 2, 1, 5, 4, 3)
    w = a["L3_ffn_Wd"].reshape(NPAIR, 2, 2, D // 2, 3, 8, P)
    flat[:, 24:] = w.transpose(0, 2, 4, 1, 6, 5, 3).reshape(NPAIR, 12, P, XSLOT)
    return flat.reshape(-1, P, XSLOT)


def column_table(a):
    bq = a["L0_gnn_bqkv"].reshape(3, D)
    mq = a["L0_mix_qkv_b"].reshape(3, D)
    own = {"L0_gnn_bq": bq[0], "L0_gnn_bk": bq[1], "L0_gnn_bv": bq[2], "L0_mix_bq": mq[0], "L0_mix_bk": mq[1],
           "L0_mix_bv": mq[2], "L2_gnn_b": np.concatenate([a["L2_gnn_b" + l] for l in "123"])}
    starts, total = column_starts()
    out = np.zeros((P, total), np.float32)
    for name, n, width in COLS:
        x = (own[name] if name in own else a[name]).reshape(n // width, width)
        out[:width, starts[name]:starts[name] + n // width] = x.T
    return out


def two_heads(w):
    out = np.zeros((P, P), np.float32)
    out[:64, :64] = w
    out[64:, 64:] = w
    return out


def head_columns(v):
    out = np.zeros((D, 12), np.float32)
    for h in range(12):
        out[64 * h:64 * h + 64, h] = v[h]
    return by_chunk(out)


def kernel(**inputs):
    import concourse.bacc as bacc
    from concourse.bass_utils import run_bass_kernel_spmd

    a = {k: np.asarray(v) for k, v in inputs.items()}
    rf1 = np.zeros((P, 2, M_RF), np.float32)
    rf1[:64, 0] = a["L1_mix_random_features"].T
    rf1[64:, 1] = a["L1_mix_random_features"].T
    edges = np.stack([a[k].reshape(EC, P).T for k in ("src", "dst", "edge_type_3", "edge_type_4")])
    arrays = {
        "xT": by_chunk(a["x"].T), "cols": column_table(a), "weights": weight_stream(a), "edges": edges,
        "feats": a["edge_attr_256"].reshape(EC, P, 256).transpose(1, 0, 2),
        "L0_Ws": by_chunk(a["L0_ffn_Ws"]), "L0_bs": a["L0_ffn_bs"].reshape(1, ME), "L2_Ws": by_chunk(a["L2_ffn_Wg"]),
        "L3_gate": by_chunk(a["L3_ffn_gate_weight"].T), "rf0": a["L0_mix_rf"].T, "rf1": rf1,
        "q1": by_chunk(a["L1_gnn_q1"]), "k1": by_chunk(a["L1_gnn_k1"]), "q2": by_chunk(a["L1_gnn_q2"]),
        "k2": by_chunk(a["L1_gnn_k2"]), "fc": two_heads(a["L3_gnn_W_fc"].T), "res": two_heads(a["L3_gnn_W_res"].T),
        "attn_l": head_columns(a["L3_gnn_attn_l"]), "attn_r": head_columns(a["L3_gnn_attn_r"]),
        **late_arrays(a),
    }
    arrays = {k: np.ascontiguousarray(v) for k, v in arrays.items()}
    tables = {}
    for _ in range(2):
        nc = bacc.Bacc("TRN2", target_bir_lowering=False, num_devices=1)
        io = {k: nc.dram_tensor("in_" + k, v.shape, mybir.dt.from_np(v.dtype), kind="ExternalInput").ap()
              for k, v in arrays.items()}
        io["scratch"] = nc.dram_tensor("scratch", (REL4 + 1, P, NT, N), mybir.dt.float32, kind="Internal").ap()
        io["out"] = nc.dram_tensor("out", (P, KC, N), mybir.dt.float32, kind="ExternalOutput").ap()
        program(nc, io, tables)
    r = run_bass_kernel_spmd(nc, [{"in_" + k: v for k, v in arrays.items()}], core_ids=[0])
    return r.results[0]["out"].transpose(2, 1, 0).reshape(N, D)


def late_arrays(a):
    return {"experts": expert_tiles(a)}
```
